# Optimizing a Trainium2 kernel written in Bass

```python
import numpy as np
import jax
import jax.numpy as jnp

def _softmax(x, axis=-1):
    return jax.nn.softmax(x, axis=axis)

def _gelu(x):
    return jax.nn.gelu(x, approximate=True)

def _silu(x):
    return jax.nn.silu(x)

def _sigmoid(x):
    return jax.nn.sigmoid(x)

def _layernorm(x, axis=-1, eps=1e-05):
    m = jnp.mean(x, axis=axis, keepdims=True)
    v = jnp.var(x, axis=axis, keepdims=True)
    return (x - m) / jnp.sqrt(v + eps)

def _scatter_add(tgt, idx, src, axis=0):
    return tgt.at[idx].add(src)

def _segment_sum(src, seg, n):
    return jax.ops.segment_sum(src, seg, n)
kernel_name = 'mk_decoder_preln_d1_seqx_r4_597c94'

def setup_inputs(seed: int=0):
    np.random.seed(seed)
    _w = jnp.asarray

    def _rec_inputs():
        import jax
        import jax.numpy as jnp
        _rk = jax.random.key(seed)
        x = 7.22e-05 + 1 * jax.random.normal(jax.random.fold_in(_rk, 1), (16, 256, 256), jnp.float32)
        _lenS = 256 - jax.random.randint(jax.random.fold_in(_rk, 7), (16,), 0, max(1, 256 // 4) + 1, jnp.int32)
        _lenS2 = 256 - jax.random.randint(jax.random.fold_in(_rk, 8), (16,), 0, max(1, 256 // 4) + 1, jnp.int32)
        _ctx_1024P = jax.random.normal(jax.random.fold_in(_rk, 11), (16, 16, 256), jnp.float32)
        _ctx_1024c = jax.random.dirichlet(jax.random.fold_in(_rk, 511), 0.3 * jnp.ones((16,), jnp.float32), (16, 256))
        _ctx_1024t = jnp.einsum('bsk,bkd->bsd', _ctx_1024c, _ctx_1024P)
        _ctx_1024t = _ctx_1024t * jax.lax.rsqrt(jnp.mean(jnp.square(_ctx_1024t)) + 1e-12) * 0.953939
        ctx_1024 = 4.13588e-05 + 0.999923 * (_ctx_1024t + 0.3 * jax.random.normal(jax.random.fold_in(_rk, 611), (16, 256, 256), jnp.float32))
        _validS = jnp.arange(256)[None, :] < _lenS[:, None]
        _validS2 = jnp.arange(256)[None, :] < _lenS2[:, None]
        _causal = jnp.tril(jnp.ones((256, 256), dtype=bool))
        mask_BxS2_bf0 = jnp.logical_not(jnp.ones((16, 256), dtype=bool))
        return (x, ctx_1024, mask_BxS2_bf0)
    x, ctx_1024, mask_BxS2_bf0 = _rec_inputs()

    def _L0_attn_setup():
        import jax, jax.numpy as jnp
        import numpy as np
        B, S, D = (4, 512, 256)
        SCALE = 1.0 / np.sqrt(D)
        key = jax.random.key(seed)
        k1, k2, k3 = jax.random.split(key, 3)
        x = jax.random.normal(k1, (B, S, D), dtype=jnp.float32)
        bound = 1.0 / np.sqrt(D)
        W_qk = jax.random.uniform(k2, (D, D), minval=-bound, maxval=bound, dtype=jnp.float32)
        W_v = jax.random.uniform(k3, (D, D), minval=-bound, maxval=bound, dtype=jnp.float32)
        alibi_slope = jnp.full((1,), 0.5, dtype=jnp.float32)
        return {'x': x, 'W_qk': W_qk, 'W_v': W_v, 'alibi_slope': alibi_slope}
    _L0_attn_all = _L0_attn_setup()
    _L0_attn_in = {k: v for k, v in _L0_attn_all.items() if k in ('W_qk', 'W_v', 'alibi_slope')}
    del _L0_attn_all

    def _L0_xattn_setup():
        import jax, jax.numpy as jnp
        import numpy as np
        EMBED_DIM = 256
        NUM_HEADS = 16
        HEAD_DIM = EMBED_DIM // NUM_HEADS
        key = jax.random.key(seed)
        ks = jax.random.split(key, 7)
        B, S, E = (4, 512, EMBED_DIM)
        scale = 1.0 / np.sqrt(E)
        return {'Q': jax.random.normal(ks[0], (B, S, E), jnp.float32), 'K': jax.random.normal(ks[1], (B, S, E), jnp.float32), 'V': jax.random.normal(ks[2], (B, S, E), jnp.float32), 'mask': jnp.zeros((B, S), dtype=bool), 'wq': jax.random.normal(ks[3], (E, E), jnp.float32) * scale, 'wk': jax.random.normal(ks[4], (E, E), jnp.float32) * scale, 'wv': jax.random.normal(ks[5], (E, E), jnp.float32) * scale, 'wfc': jax.random.normal(ks[6], (E, E), jnp.float32) * scale}
    _L0_xattn_all = _L0_xattn_setup()
    _L0_xattn_in = {k: v for k, v in _L0_xattn_all.items() if k in ('wq', 'wk', 'wv', 'wfc')}
    del _L0_xattn_all

    def _L0_ffn_setup():
        import jax, jax.numpy as jnp
        import numpy as np
        B, S, D = (2, 512, 256)
        F = 1024
        E, K = (8, 2)
        EPS = 1e-09
        key = jax.random.key(seed)
        k1, k2, k3, k4 = jax.random.split(key, 4)
        x = jax.random.normal(k1, (B, S, D), dtype=jnp.float32)
        w_gate = jax.random.normal(k2, (D, E), dtype=jnp.float32) * 0.02
        w_gate_up = jax.random.normal(k3, (E, D, 2 * F), dtype=jnp.float32) * 0.02
        w_down = jax.random.normal(k4, (E, F, D), dtype=jnp.float32) * 0.02
        return {'x': x, 'w_gate': w_gate, 'w_gate_up': w_gate_up, 'w_down': w_down}
    _L0_ffn_all = _L0_ffn_setup()
    _L0_ffn_in = {k: v for k, v in _L0_ffn_all.items() if k in ('w_gate', 'w_gate_up', 'w_down')}
    del _L0_ffn_all
    return {'x': x, 'ctx_1024': ctx_1024, 'mask_BxS2_bf0': mask_BxS2_bf0, 'L0_attn_W_qk': _L0_attn_in['W_qk'], 'L0_attn_W_v': _L0_attn_in['W_v'], 'L0_attn_alibi_slope': _L0_attn_in['alibi_slope'], 'L0_xattn_wq': _L0_xattn_in['wq'], 'L0_xattn_wk': _L0_xattn_in['wk'], 'L0_xattn_wv': _L0_xattn_in['wv'], 'L0_xattn_wfc': _L0_xattn_in['wfc'], 'L0_ffn_w_gate': _L0_ffn_in['w_gate'], 'L0_ffn_w_gate_up': _L0_ffn_in['w_gate_up'], 'L0_ffn_w_down': _L0_ffn_in['w_down']}

def reference(x, ctx_1024, mask_BxS2_bf0, L0_attn_W_qk, L0_attn_W_v, L0_attn_alibi_slope, L0_xattn_wq, L0_xattn_wk, L0_xattn_wv, L0_xattn_wfc, L0_ffn_w_gate, L0_ffn_w_gate_up, L0_ffn_w_down):
    import jax
    import jax.numpy as jnp

    def _L0_attn_ref(x, W_qk, W_v, alibi_slope):
        import jax, jax.numpy as jnp
        import numpy as np
        B, S, D = (4, 512, 256)
        SCALE = 1.0 / np.sqrt(D)
        seq_len = x.shape[1]
        scores = jnp.einsum('bqe,bke->bqk', x @ W_qk, x) * SCALE
        kpos = jnp.arange(seq_len, dtype=x.dtype)[None, :]
        qpos = jnp.arange(seq_len, dtype=x.dtype)[:, None]
        scores = scores + (kpos - qpos) * alibi_slope[0]
        causal = qpos >= kpos
        scores = jnp.where(causal, scores, -jnp.inf)
        attn = jax.nn.softmax(scores, axis=-1)
        v = x @ W_v.T
        return jnp.einsum('bqk,bkd->bqd', attn, v)

    def _L0_xattn_ref(Q, K, V, mask, wq, wk, wv, wfc):
        import jax, jax.numpy as jnp
        import numpy as np
        EMBED_DIM = 256
        NUM_HEADS = 16
        HEAD_DIM = EMBED_DIM // NUM_HEADS
        B, S, E = Q.shape
        H, D = (NUM_HEADS, HEAD_DIM)
        q = (Q @ wq.T).reshape(B, S, H, D).transpose(0, 2, 1, 3)
        k = (K @ wk.T).reshape(B, S, H, D).transpose(0, 2, 1, 3)
        v = (V @ wv.T).reshape(B, S, H, D).transpose(0, 2, 1, 3)
        scores = jnp.einsum('bhqd,bhkd->bhqk', q, k) / jnp.sqrt(jnp.float32(D))
        scores = jnp.where(mask[:, None, None, :], -jnp.inf, scores)
        attn = jax.nn.softmax(scores, axis=-1)
        out = jnp.einsum('bhqk,bhkd->bhqd', attn, v)
        out = out.transpose(0, 2, 1, 3).reshape(B, S, E)
        return out @ wfc.T

    def _L0_ffn_ref(x, w_gate, w_gate_up, w_down):
        import jax, jax.numpy as jnp
        import numpy as np
        B, S, D = (2, 512, 256)
        F = 1024
        E, K = (8, 2)
        EPS = 1e-09
        gate_logits = x @ w_gate
        gate_probs = jax.nn.softmax(gate_logits, axis=-1)
        topk_vals, topk_idx = jax.lax.top_k(gate_probs, K)
        masked = jnp.sum(jax.nn.one_hot(topk_idx, E, dtype=gate_probs.dtype) * topk_vals[..., None], axis=-2)
        denom = jnp.maximum(jnp.sum(masked, axis=-1, keepdims=True), EPS)
        gate_probs = masked / denom
        gu = jnp.einsum('bsd,edh->ebsh', x, w_gate_up)
        g, u = jnp.split(gu, 2, axis=-1)
        act = jax.nn.silu(g) * u
        expert_out = jnp.einsum('ebsf,efd->ebsd', act, w_down)
        return jnp.einsum('bse,ebsd->bsd', gate_probs, expert_out)
    x = x + _L0_attn_ref(_layernorm(x, axis=-1), L0_attn_W_qk, L0_attn_W_v, L0_attn_alibi_slope)
    x = x + _L0_xattn_ref(_layernorm(x, axis=-1), ctx_1024, ctx_1024, mask_BxS2_bf0, L0_xattn_wq, L0_xattn_wk, L0_xattn_wv, L0_xattn_wfc)
    x = x + _L0_ffn_ref(_layernorm(x, axis=-1), L0_ffn_w_gate, L0_ffn_w_gate_up, L0_ffn_w_down)
    return x

_drawn_inputs = setup_inputs


def setup_inputs(seed=0):
    import zlib

    import numpy as np

    out = dict(_drawn_inputs(seed))
    spreads = {}
    factors = {'L0_ffn_w_gate': 3.207, 'L0_ffn_w_gate_up': 2.773, 'L0_ffn_w_down': 2.771}
    for name, (base, spread) in spreads.items():
        noise = np.random.default_rng([zlib.crc32(name.encode()), seed]).standard_normal(out[name].shape)
        drawn = base * np.exp(spread * noise) if base else spread * noise
        out[name] = jnp.asarray(drawn.astype(out[name].dtype))
    for name, factor in factors.items():
        out[name] = (out[name] * factor).astype(out[name].dtype)
    return out
```

```python
from contextlib import ExitStack

import numpy as np
import concourse.bass as bass
from concourse import mybir

F32 = mybir.dt.float32
F16 = mybir.dt.float16
U32 = mybir.dt.uint32
I32 = mybir.dt.int32
U8 = mybir.dt.uint8
ALU = mybir.AluOpType
ACT = mybir.ActivationFunctionType
AX = mybir.AxisListType

B, S, D = 16, 256, 256
P = 128
NT = S // P
NC = D // P
H, HD = 16, 16
HJ = H // 2
E, F, TOPK = 8, 1024, 2
EPS_LN, EPS_GATE = 1e-5, 1e-9
SCALE = float(D) ** -0.5
HSCALE = float(HD) ** -0.5
NEG = -1.0e30
MASK_BIAS = -3.0e38
MASK_Q, MASK_K = 32768.0, -32768.0
MAX_Q, MAX_K = 1.0 / 64, 64.0

SLOT = 256
NSLOT = B * S * TOPK // SLOT + E - 1
REGION = B * S + SLOT
DUMMY = E * REGION
ROWS = DUMMY + SLOT
FC = F // P
NBANKS = 4


def decoder_layer(nc, x, ctx, mask, w_qk, w_v, slope, wq, wk, wv, wfc, w_gate, w_gu, w_down, out):
    with ExitStack() as stack:
        def sb(name, shape, dt=F32):
            return stack.enter_context(nc.sbuf_tensor(name, shape, dt))

        def bank(name):
            return stack.enter_context(nc.psum_tensor(name, [P, 512], F32))

        def sem(name):
            return stack.enter_context(nc.semaphore(name))

        def sems(name, n=2):
            return [sem(f"{name}{i}") for i in range(n)]

        routed = nc.dram_tensor("routed_rows", [ROWS, D], F32, kind="Internal").ap()
        expert_out = nc.dram_tensor("expert_rows", [NSLOT * SLOT, D], F32, kind="Internal").ap()
        stream = nc.dram_tensor("stream", [B, S, D], F32, kind="Internal").ap()
        mask_rows = nc.dram_tensor("mask_rows", [B, HJ, S], F16, kind="Internal").ap()

        ident = sb("ident", [P, P])
        tri = sb("tri", [P, P], F16)
        ones = sb("ones", [P, P], F16)
        half_neg = sb("half_neg", [P, NT])
        iota_e = sb("iota_e", [P, E])
        pad_iota = sb("pad_iota", [P, E, NT])
        alibi = sb("alibi", [P, P + S])
        slope_sb = sb("slope_sb", [P, 1])
        zero_rows = sb("zero_rows", [P, D])
        row_const = sb("row_const", [HJ, 3, S], F16)
        mask_u8 = sb("mask_u8", [B, S], U8)
        mask_f = sb("mask_f", [B, S])
        mask_h = sb("mask_h", [B, S], F16)
        mask_bias = sb("mask_bias", [P, NT, B])
        w_t = sb("w_t", [P, 5, NC, D])
        wqk_sb = sb("wqk_sb", [P, NC, D])
        wg_sb = sb("wg_sb", [P, NC, E])
        WV1, WQ, WK, WV2, WFC = range(5)

        x_in = sb("x_in", [P, 2, NT, D])
        ctx_in = sb("ctx_in", [P, 2, NT, D])
        stats = sb("stats", [P, NT, 6])
        moments = sb("moments", [P, NT, 2])
        var_eps = sb("var_eps", [P, NT])
        rstd = sb("rstd", [P, NT])
        xn = sb("xn", [P, NT, D])
        xn_t = sb("xn_t", [P, NC, S])
        q1_t = sb("q1_t", [P, NC, S])
        v1 = sb("v1", [P, NT, D])
        s1 = sb("s1", [P, P + S])
        nmax1 = sb("nmax1", [P, NT])
        p1 = sb("p1", [P, P + S])
        sum1 = sb("sum1", [P, NT])
        rsum1 = sb("rsum1", [P, NT])
        p1_t = sb("p1_t", [P, 3, P])
        x1 = sb("x1", [P, 2, NT, D])
        xn2 = sb("xn2", [P, NT, D])
        xn2_t = sb("xn2_t", [P, NC, S])
        ctx_t = sb("ctx_t", [P, NC, S])
        q_hi = sb("q_hi", [P, NC, S], F16)
        q_lo = sb("q_lo", [P, NC, S], F16)
        k_hi = sb("k_hi", [P, NC, S], F16)
        k_lo = sb("k_lo", [P, NC, S], F16)
        q_stack = sb("q_stack", [P, 2, HJ, S], F16)
        k_stack = sb("k_stack", [P, 2, 2, HJ, S], F16)
        v_aug = sb("v_aug", [P, 2, NT, H, 32])

        nmax = sb("nmax", [P, NT, 2, HJ])
        nmax_t = sb("nmax_t", [H, S], F16)
        probs_t = sb("probs_t", [P, 2, 2, 2, S])
        o_t = sb("o_t", [P, HJ // 2, S])

        rden = sb("rden", [P, HJ // 2, 4])
        o_n = sb("o_n", [P, NT, D])
        o_nt = sb("o_nt", [P, NC, S])
        x2 = sb("x2", [P, 2, NT, D])
        stats3 = sb("stats3", [P, NT, 6])
        moments3 = sb("moments3", [P, NT, 2])
        var_eps3 = sb("var_eps3", [P, NT])
        rstd3 = sb("rstd3", [P, NT])
        xn3 = sb("xn3", [P, 2, NT, D])
        xn3_t = sb("xn3_t", [P, NC, S])
        lmax = sb("lmax", [P, NT])
        logits = sb("logits", [P, NT, E])
        gexp = sb("gexp", [P, NT, E])
        gsum = sb("gsum", [P, NT])
        grec = sb("grec", [P, NT])
        gprob = sb("gprob", [P, NT, E])
        top_v = sb("top_v", [P, NT, 8])
        top_i = sb("top_i", [P, NT, 8], U32)
        top_f = sb("top_f", [P, NT, TOPK])
        gden = sb("gden", [P, NT])
        gden1 = sb("gden1", [P, NT])
        gdenr = sb("gdenr", [P, NT])
        onehot = sb("onehot", [P, NT, TOPK, E])
        chosen = sb("chosen", [P, NT, E], F16)
        rank = sb("rank", [P, NT, E])
        onehot_pos = sb("onehot_pos", [P, NT, TOPK, E])
        pos_f = sb("pos_f", [P, NT * TOPK])
        pos_i = sb("pos_i", [P, 2, NT * TOPK], U32)
        next_row = sb("next_row", [P, E])
        pos_all = sb("pos_all", [P, B * NT * TOPK])
        onehot_all = sb("onehot_all", [P, B * NT * TOPK, E])
        gate_all = sb("gate_all", [P, B * NT, TOPK])

        region0 = sb("region0", [P, E])
        pad_f = sb("pad_f", [P, E, NT])
        pad_i = sb("pad_i", [P, E * NT], U32)
        count = sb("count", [P, E])
        count_i = sb("count_i", [P, E], I32)
        slots_i = sb("slots_i", [P, E], I32)
        slots_f = sb("slots_f", [P, E])
        one_e = sb("one_e", [P, E])
        slot_end = sb("slot_end", [P, E])
        moved = sb("moved", [P, E])
        onehot_moved = sb("onehot_moved", [P, B * NT * TOPK, E])
        pos_moved = sb("pos_moved", [P, B * NT * TOPK])
        gather_all = sb("gather_all", [P, B * NT * TOPK], U32)
        jump = sb("jump", [1, E])
        slot_id = sb("slot_id", [1, NSLOT])
        past = sb("past", [1, NSLOT, E])
        past_jump = sb("past_jump", [1, NSLOT, E])
        slot_e = sb("slot_e", [1, NSLOT])
        slot_r = sb("slot_r", [1, NSLOT])
        slot_r1 = sb("slot_r1", [1, NSLOT])
        slot_tab = sb("slot_tab", [1, 2, NSLOT], I32)
        rows = sb("rows", [P, 2, NT, D])
        rows_t = sb("rows_t", [P, 2, NC, SLOT])
        wgu_sb = sb("wgu_sb", [P, 2, NC, 2 * F])
        wd_sb = sb("wd_sb", [P, 2, FC, D])
        w_raw = wgu_sb[:, 0].rearrange("p c h -> p (c h)")[:, 0:5 * NC * D].rearrange(
            "p (i c n) -> p i c n", i=5, c=NC)
        silu_g = sb("silu_g", [P, 2, SLOT])
        act_t = sb("act_t", [P, 4, SLOT])
        y_sb = sb("y_sb", [P, 2, NT, D])

        gather_i = sb("gather_i", [P, 2, NT * TOPK], U32)
        gathered = wd_sb[:, :, 0:NT * TOPK].rearrange("p b (t k) d -> p b t k d", t=NT)
        stream_in = wd_sb[:, :, NT * TOPK:NT * TOPK + NT]
        acc = sb("acc", [P, NT, D])
        out_sb = sb("out_sb", [P, 2, NT, D])

        ring = [bank(f"ring{i}") for i in range(NBANKS)]
        pv = [bank(f"pv{i}") for i in range(2)]
        front = bank("front")
        tail = bank("tail")

        consts_loaded = sem("consts_loaded")
        pool_const = sem("pool_const")
        vec_const = sem("vec_const")
        w_tps = sem("w_tps")
        w_tsb = sem("w_tsb")
        mask_tps = sem("mask_tps")
        rows_set = sem("rows_set")
        x_loaded, ctx_loaded = sems("x_loaded"), sems("ctx_loaded")
        ln_step, ln_var, ln_rstd, ln1_done, ln2_done = map(sem, "ln_step ln_var ln_rstd ln1_done ln2_done".split())
        xnt_ps, xnt_sb, q1_ps, q1_sb, v1_ps, v1_sb = map(sem, "xnt_ps xnt_sb q1_ps q1_sb v1_ps v1_sb".split())
        sc_ps, s1_step, nmax1_sb, p1_sb, rsum1_sb = map(sem, "sc_ps s1_step nmax1_sb p1_sb rsum1_sb".split())
        p1t_ps, p1t_sb, at_ps, x1_sb = map(sem, "p1t_ps p1t_sb at_ps x1_sb".split())
        xn2t_ps, xn2t_sb, ctxt_ps, ctxt_sb = map(sem, "xn2t_ps xn2t_sb ctxt_ps ctxt_sb".split())
        q_ps, qhi_sb, qlo_sb, k_ps, khi_sb, klo_sb = map(sem, "q_ps qhi_sb qlo_sb k_ps khi_sb klo_sb".split())
        v2_ps, v2_sb = sem("v2_ps"), sem("v2_sb")
        stacked = sems("stacked")
        STACK_DMAS = 16
        s_ps, smax, nmt_ps, nmt_sb = map(sem, "s_ps smax nmt_ps nmt_sb".split())
        max_stacked = sems("max_stacked")
        st_ps, exp_sb, pv_ps, o_sb = map(sem, "st_ps exp_sb pv_ps o_sb".split())
        oq_ps, on_step, on_sb, ont_ps, ont_sb = map(sem, "oq_ps on_step on_sb ont_ps ont_sb".split())
        fc_ps, x2_sb, ln3_step, ln3_var, ln3_rstd, ln3_done = map(
            sem, "fc_ps x2_sb ln3_step ln3_var ln3_rstd ln3_done".split())
        xn3t_ps, xn3t_sb, gate_ps, gate_step, logits_sb, gexp_sb = map(
            sem, "xn3t_ps xn3t_sb gate_ps gate_step logits_sb gexp_sb".split())
        chosen_sb, rank_ps, rank_sb, pos_sb = map(sem, "chosen_sb rank_ps rank_sb pos_sb".split())
        scattered, streamed, xn3_free = sems("scattered"), sems("streamed"), sem("xn3_free")
        slot_step, pad_sb, table_sb, padded = map(sem, "slot_step pad_sb table_sb padded".split())
        dummied = sem("dummied")
        rows_in, w_in, y_out = sems("rows_in"), sems("w_in"), sems("y_out")
        rt_ps, rt_sb, gu_ps, silu_sb, act_sb = map(sem, "rt_ps rt_sb gu_ps silu_sb act_sb".split())
        down_ps, y0_sb, y1_sb, act_used = map(sem, "down_ps y0_sb y1_sb act_used".split())
        idx_sb, acc_step, out_ready = sem("idx_sb"), sem("acc_step"), sem("out_ready")
        rows_got, stream_got, out_done = sems("rows_got"), sems("stream_got"), sems("out_done")

        act_passed, vec_passed, pool_passed = map(sem, "act_passed vec_passed pool_passed".split())

        block = stack.enter_context(nc.Block())

        CONST_LOADS = 4 + 5 + 1
        ROW_SETS = 2 * 2 * 2 + HJ
        LN_STEPS = 3
        GATE_STEPS = 17

        @block.sync
        def _(sp):
            sp.dma_start(wqk_sb[:], w_qk.rearrange("(c p) n -> p c n", p=P)).then_inc(consts_loaded, 16)
            sp.dma_start(wg_sb[:], w_gate.rearrange("(c p) n -> p c n", p=P)).then_inc(consts_loaded, 16)
            sp.dma_start(slope_sb[:], slope.rearrange("(a n) -> a n", a=1).to_broadcast([P, 1])
                         ).then_inc(consts_loaded, 16)
            sp.dma_start(mask_u8[:], mask).then_inc(consts_loaded, 16)
            for i, w in enumerate((w_v, wq, wk, wv, wfc)):
                sp.dma_start(w_raw[:, i], w.rearrange("(c p) n -> p c n", p=P)).then_inc(consts_loaded, 16)

            for p in range(2):
                sp.sem_inc(streamed[p], 16)

            def load(b, p):
                sp.dma_start(x_in[:, p], x[b].rearrange("(t p) d -> p t d", p=P)).then_inc(x_loaded[p], 16)
                sp.dma_start(ctx_in[:, p], ctx[b].rearrange("(t p) d -> p t d", p=P)).then_inc(ctx_loaded[p], 16)

            load(0, 0)
            load(1, 1)
            sp.wait_ge(vec_const, 1)
            for p in range(2):
                for r in range(2):
                    sp.dma_start(q_stack[64 * r + 48:64 * r + 49, p], row_const[:, 0]).then_inc(rows_set, 16)
                    sp.dma_start(k_stack[64 * r + 49:64 * r + 50, p, r], row_const[:, 1]).then_inc(rows_set, 16)
            sp.wait_ge(vec_const, 2)
            for j in range(HJ):
                sp.dma_start(mask_rows[:, j], mask_h[:]).then_inc(rows_set, 16)
            for t in range(NT):
                sp.dma_start(routed[DUMMY + t * P:DUMMY + (t + 1) * P], zero_rows[:]).then_inc(dummied, 16)
            sp.wait_ge(rows_set, 16 * ROW_SETS)

            def stack_heads(n, p):
                for r in range(2):
                    o = 64 * r
                    sp.dma_start(q_stack[o + 49:o + 50, p], row_const[:, 2]).then_inc(stacked[p], 16)
                    sp.dma_start(k_stack[o + 48:o + 49, p, r], mask_rows[n]).then_inc(stacked[p], 16)
                sp.wait_ge(qhi_sb, n + 1)
                for r in range(2):
                    o = 64 * r
                    sp.dma_start(q_stack[o:o + 16, p], q_hi[:, r]).then_inc(stacked[p], 16)
                    sp.dma_start(q_stack[o + 32:o + 48, p], q_hi[:, r]).then_inc(stacked[p], 16)
                sp.wait_ge(qlo_sb, n + 1)
                for r in range(2):
                    o = 64 * r
                    sp.dma_start(q_stack[o + 16:o + 32, p], q_lo[:, r]).then_inc(stacked[p], 16)
                sp.wait_ge(khi_sb, n + 1)
                for r in range(2):
                    o = 64 * r
                    sp.dma_start(k_stack[o:o + 16, p, r], k_hi[:, r]).then_inc(stacked[p], 16)
                    sp.dma_start(k_stack[o + 16:o + 32, p, r], k_hi[:, r]).then_inc(stacked[p], 16)
                sp.wait_ge(klo_sb, n + 1)
                for r in range(2):
                    o = 64 * r
                    sp.dma_start(k_stack[o + 32:o + 48, p, r], k_lo[:, r]).then_inc(stacked[p], 16)

            def stack_max(b, p):
                sp.wait_ge(nmt_sb, b + 1)
                for r in range(2):
                    sp.dma_start(q_stack[64 * r + 49:64 * r + 50, p], nmax_t[HJ * r:HJ * (r + 1)]).then_inc(max_stacked[p], 16)

            def store_stream(c, p):
                sp.wait_ge(x2_sb, c + 1)
                sp.dma_start(stream[c].rearrange("(t p) d -> p t d", p=P), x2[:, p]).then_inc(streamed[p], 16)

            def iteration(b, p, tail_of, front_of, fetch):
                if fetch:
                    sp.wait_ge(x1_sb, b + 1)
                    sp.wait_ge(ctxt_sb, b + 1)
                    load(b + 2, p)
                if tail_of:
                    store_stream(b - 1, 1 - p)
                stack_max(b, p)
                if front_of:
                    if tail_of:
                        sp.wait_ge(pv_ps, 8 * b)
                    stack_heads(b + 1, 1 - p)

            stack_heads(0, 0)
            iteration(0, 0, False, True, True)
            with sp.Fori(0, 6) as i:
                iteration(2 * i + 1, 1, True, True, True)
                iteration(2 * i + 2, 0, True, True, True)
            iteration(13, 1, True, True, True)
            iteration(14, 0, True, True, False)
            iteration(15, 1, True, False, False)
            store_stream(15, 1)

            sp.wait_ge(table_sb, 1)
            sp.wait_ge(padded, 16 * E * NT)
            sp.wait_ge(dummied, 16 * NT)
            for p in range(2):
                sp.wait_ge(scattered[p], 64 * (B // 2))
                sp.wait_ge(streamed[p], 16 * (B // 2 + 1))

            def load_slot(s, p):
                row = sp.value_load(slot_tab[0:1, 0, bass.ds(s, 1)], min_val=0, max_val=DUMMY)
                e = sp.value_load(slot_tab[0:1, 1, bass.ds(s, 1)], min_val=0, max_val=E - 1)
                sp.dma_start(rows[:, p], routed[bass.ds(row, SLOT)].rearrange("(t p) d -> p t d", p=P)
                             ).then_inc(rows_in[p], 16)
                sp.dma_start(wgu_sb[:, p], w_gu[bass.ds(e, 1)].rearrange("e (c p) h -> p (e c) h", p=P)
                             ).then_inc(w_in[p], 16)
                sp.dma_start(wd_sb[:, p], w_down[bass.ds(e, 1)].rearrange("e (c p) h -> p (e c) h", p=P)
                             ).then_inc(w_in[p], 16)

            def store_slot(s, p):
                sp.wait_ge(y0_sb, s + 1)
                sp.wait_ge(y1_sb, s + 1)
                sp.dma_start(expert_out[bass.ds(s * SLOT, SLOT)].rearrange("(t p) d -> p t d", p=P), y_sb[:, p]
                             ).then_inc(y_out[p], 16)

            load_slot(0, 0)
            load_slot(1, 1)

            def slot(s, p, h, fetch):
                store_slot(s, p)
                sp.wait_ge(y_out[p], 16 * h + 16)
                if fetch:
                    load_slot(s + 2, p)

            with sp.Fori(0, (NSLOT - 3) // 2) as i:
                slot(2 * i, 0, i, True)
                slot(2 * i + 1, 1, i, True)
            slot(NSLOT - 3, 0, (NSLOT - 3) // 2, True)
            slot(NSLOT - 2, 1, (NSLOT - 3) // 2, False)
            slot(NSLOT - 1, 0, (NSLOT - 1) // 2, False)

            def load_stream(b, p):
                sp.dma_start(stream_in[:, p], stream[b].rearrange("(t p) d -> p t d", p=P)
                             ).then_inc(stream_got[p], 16)

            def store_out(b, p):
                sp.wait_ge(out_ready, b + 1)
                sp.dma_start(out[b].rearrange("(t p) d -> p t d", p=P), out_sb[:, p]).then_inc(out_done[p], 16)

            load_stream(0, 0)
            load_stream(1, 1)
            with sp.Fori(0, B // 2 - 1) as i:
                for p in range(2):
                    store_out(2 * i + p, p)
                    load_stream(2 * i + p + 2, p)
            for p in range(2):
                store_out(B - 2 + p, p)
            for p in range(2):
                sp.wait_ge(out_done[p], 16 * (B // 2))

        @block.gpsimd
        def _(pool):
            pool.sem_inc(xn3_free, 2)
            nc.gpsimd.memset(ident[:], 0.0).then_inc(pool_const, 1)
            nc.gpsimd.memset(tri[:], 1.0).then_inc(pool_const, 1)
            nc.gpsimd.memset(half_neg[:], -0.5).then_inc(pool_const, 1)
            nc.gpsimd.iota(iota_e[:], pattern=[[1, E]], base=0, channel_multiplier=0,
                           allow_small_or_imprecise_dtypes=True).then_inc(pool_const, 1)
            nc.gpsimd.iota(region0[:], pattern=[[REGION, E]], base=0, channel_multiplier=0,
                           allow_small_or_imprecise_dtypes=True).then_inc(pool_const, 1)
            nc.gpsimd.iota(pad_iota[:], pattern=[[0, E], [P, NT]], base=0, channel_multiplier=1,
                           allow_small_or_imprecise_dtypes=True).then_inc(pool_const, 1)
            nc.gpsimd.iota(slot_id[:], pattern=[[1, NSLOT]], base=0, channel_multiplier=0,
                           allow_small_or_imprecise_dtypes=True).then_inc(pool_const, 1)
            nc.gpsimd.iota(alibi[:, 0:P], pattern=[[1, P]], base=0, channel_multiplier=-1,
                           allow_small_or_imprecise_dtypes=True).then_inc(pool_const, 1)
            nc.gpsimd.iota(alibi[:, P:P + S], pattern=[[1, S]], base=-P, channel_multiplier=-1,
                           allow_small_or_imprecise_dtypes=True).then_inc(pool_const, 1)
            pool.wait_ge(pool_const, 9)
            nc.gpsimd.affine_select(out=ident[:], in_=ident[:], compare_op=ALU.not_equal, fill=1.0, base=0,
                                    pattern=[[-1, P]], channel_multiplier=1).then_inc(pool_const, 1)
            nc.gpsimd.affine_select(out=tri[:], in_=tri[:], compare_op=ALU.is_gt, fill=0.0, base=0,
                                    pattern=[[1, P]], channel_multiplier=-1).then_inc(pool_const, 1)
            pool.wait_ge(vec_const, 3)
            nc.gpsimd.affine_select(out=alibi[:, 0:P], in_=alibi[:, 0:P], compare_op=ALU.is_ge, fill=NEG, base=0,
                                    pattern=[[-1, P]], channel_multiplier=1).then_inc(pool_const, 1)
            nc.gpsimd.affine_select(out=alibi[:, P:P + S], in_=alibi[:, P:P + S], compare_op=ALU.is_ge, fill=NEG,
                                    base=P, pattern=[[-1, S]], channel_multiplier=1).then_inc(pool_const, 1)

            def rsqrt_front(m):
                pool.wait_ge(ln_var, m)
                nc.gpsimd.tensor_tensor(rstd[:], var_eps[:], half_neg[:], ALU.pow).then_inc(ln_rstd, 1)

            def rsqrt_tail(c):
                pool.wait_ge(ln3_var, c + 1)
                nc.gpsimd.tensor_tensor(rstd3[:], var_eps3[:], half_neg[:], ALU.pow).then_inc(ln3_rstd, 1)

            def scatter(c, p):
                pool.wait_ge(pos_sb, c + 1)
                pool.sem_inc(pool_passed, 1)
                for t in range(NT):
                    for k in range(TOPK):
                        nc.gpsimd.indirect_dma_start(
                            out=routed, out_offset=bass.IndirectOffsetOnAxis(
                                ap=pos_i[:, p, t * TOPK + k:t * TOPK + k + 1], axis=0),
                            in_=xn3[:, p, t], in_offset=None).then_inc(scattered[p], 16)

            def iteration(b, p, h, tail_of, front_of):
                if front_of:
                    rsqrt_front(2 * b + 3)
                if h is not None:
                    pool.wait_ge(scattered[p], 64 * h)
                    pool.sem_inc(xn3_free, 1)
                if tail_of:
                    rsqrt_tail(b - 1)
                if front_of:
                    rsqrt_front(2 * b + 4)
                if tail_of:
                    scatter(b - 1, 1 - p)

            rsqrt_front(1)
            rsqrt_front(2)
            iteration(0, 0, None, False, True)
            iteration(1, 1, None, True, True)
            with pool.Fori(0, 6) as i:
                iteration(2 * i + 2, 0, i + 1, True, True)
                iteration(2 * i + 3, 1, i + 1, True, True)
            iteration(14, 0, 7, True, True)
            iteration(15, 1, 7, True, False)
            rsqrt_tail(15)
            scatter(15, 1)
            pool.wait_ge(pad_sb, 1)
            for k in range(E * NT):
                nc.gpsimd.indirect_dma_start(
                    out=routed, out_offset=bass.IndirectOffsetOnAxis(ap=pad_i[:, k:k + 1], axis=0),
                    in_=zero_rows[:], in_offset=None).then_inc(padded, 16)

            pool.wait_ge(y_out[0], 16 * ((NSLOT + 1) // 2))
            pool.wait_ge(y_out[1], 16 * (NSLOT // 2))

            def gather(b, p):
                pool.wait_ge(idx_sb, b + 1)
                pool.sem_inc(pool_passed, 1)
                for t in range(NT):
                    for k in range(TOPK):
                        nc.gpsimd.indirect_dma_start(
                            out=gathered[:, p, t, k], out_offset=None, in_=expert_out,
                            in_offset=bass.IndirectOffsetOnAxis(
                                ap=gather_i[:, p, t * TOPK + k:t * TOPK + k + 1], axis=0),
                        ).then_inc(rows_got[p], 16)

            with pool.Fori(0, B // 2) as i:
                for p in range(2):
                    gather(2 * i + p, p)

        @block.scalar
        def _(act):
            def copy(to, frm):
                return nc.scalar.activation(to, frm, ACT.Copy)

            for i in range(5):
                act.wait_ge(w_tps, i + 1)
                if i in (WQ, WK):
                    for c in range(NC):
                        for r in range(2):
                            o = copy(w_t[:, i, c, r * P:(r + 1) * P].rearrange("p (d j) -> p j d", j=HJ),
                                     front[:, c * D + r * P:c * D + (r + 1) * P].rearrange("p (j d) -> p j d", d=HD))
                    o.then_inc(w_tsb, 1)
                else:
                    copy(w_t[:, i], front[:].rearrange("p (c n) -> p c n", c=NC)).then_inc(w_tsb, 1)
            act.wait_ge(mask_tps, 1)
            nc.scalar.activation(mask_bias[:], tail[:, 0:NT * B].rearrange("p (t b) -> p t b", t=NT), ACT.Copy,
                                 scale=MASK_BIAS).then_inc(w_tsb, 1)

            def as_chunks(bank_):
                return bank_[:].rearrange("p (c n) -> p c n", c=NC)

            def f_xnt(n):
                act.wait_ge(xnt_ps, n + 1)
                copy(xn_t[:], as_chunks(front)).then_inc(xnt_sb, 1)

            def f_q1(n):
                act.wait_ge(q1_ps, n + 1)
                copy(q1_t[:], as_chunks(front)).then_inc(q1_sb, 1)

            def f_v1(n):
                act.wait_ge(v1_ps, n + 1)
                copy(v1[:], as_chunks(front)).then_inc(v1_sb, 1)

            def f_probs(n):
                act.wait_ge(nmax1_sb, n + 1)
                nc.scalar.activation(p1[:, 0:P], s1[:, 0:P], ACT.Exp, bias=nmax1[:, 0:1], accum_out=sum1[:, 0:1])
                nc.scalar.activation(p1[:, P:P + S], s1[:, P:P + S], ACT.Exp, bias=nmax1[:, 1:2],
                                     accum_out=sum1[:, 1:2]).then_inc(p1_sb, 1)

            def f_probs_t(n):
                act.wait_ge(p1t_ps, n + 1)
                copy(p1_t[:], front[:, 0:3 * P].rearrange("p (b q) -> p b q", b=3)).then_inc(p1t_sb, 1)

            def f_xn2t(n):
                act.wait_ge(xn2t_ps, n + 1)
                copy(xn2_t[:], as_chunks(front)).then_inc(xn2t_sb, 1)

            def f_ctxt(n):
                act.wait_ge(ctxt_ps, n + 1)
                copy(ctx_t[:], as_chunks(front)).then_inc(ctxt_sb, 1)

            def f_q(n):
                act.wait_ge(q_ps, n + 1)
                nc.scalar.activation(q_hi[:], as_chunks(front), ACT.Copy, scale=HSCALE).then_inc(qhi_sb, 1)

            def f_k(n):
                act.wait_ge(k_ps, n + 1)
                copy(k_hi[:], as_chunks(front)).then_inc(khi_sb, 1)

            def f_v2(n, p):
                act.wait_ge(v2_ps, n + 1)
                copy(v_aug[:, p, :, :, 0:HD],
                     front[:].rearrange("p (t h d) -> p t h d", t=NT, h=H)).then_inc(v2_sb, 1)

            def h_max(b):
                act.wait_ge(nmt_ps, b + 1)
                nc.scalar.activation(nmax_t[:], tail[0:H, 0:S], ACT.Copy, scale=MAX_Q).then_inc(nmt_sb, 1)

            def h_exp(b, g):
                kt = g % 2
                act.wait_ge(st_ps, 8 * b + g + 1)
                if not isinstance(b, int) or b > 0 or g >= 2:
                    act.wait_ge(pv_ps, 8 * b + g - 1)
                act.sem_inc(act_passed, 1)
                for r in range(2):
                    o = nc.scalar.activation(
                        probs_t[:, g % 2, r], ring[2 * (g % 2) + r][:].rearrange("p (j q) -> p j q", j=2),
                        ACT.Exp, bias=mask_bias[:, kt, bass.ds(b, 1)])
                o.then_inc(exp_sb, 1)

            def t_ont(c):
                act.wait_ge(ont_ps, c + 1)
                copy(o_nt[:], as_chunks(tail)).then_inc(ont_sb, 1)

            def t_xn3t(c):
                act.wait_ge(xn3t_ps, c + 1)
                copy(xn3_t[:], as_chunks(tail)).then_inc(xn3t_sb, 1)

            def t_gate(c):
                act.wait_ge(logits_sb, c + 1)
                nc.scalar.activation(gexp[:], logits[:], ACT.Exp).then_inc(gexp_sb, 1)

            def iteration(b, p, tail_of, front_of):
                c, n = b - 1, b + 1
                if front_of:
                    f_xnt(n)
                    f_q1(n)
                if tail_of:
                    t_ont(c)
                if front_of:
                    f_v1(n)
                    f_probs(n)
                if tail_of:
                    t_xn3t(c)
                if front_of:
                    f_probs_t(n)
                if tail_of:
                    t_gate(c)
                h_max(b)
                if front_of:
                    f_xn2t(n)
                    f_ctxt(n)
                for g in range(8):
                    h_exp(b, g)
                    if front_of and g == 1:
                        f_q(n)
                    if front_of and g == 3:
                        f_k(n)
                    if front_of and g == 5:
                        f_v2(n, 1 - p)

            f_xnt(0)
            f_q1(0)
            f_v1(0)
            f_probs(0)
            f_probs_t(0)
            f_xn2t(0)
            f_ctxt(0)
            f_q(0)
            f_k(0)
            f_v2(0, 0)
            iteration(0, 0, False, True)
            with act.Fori(0, 7) as i:
                iteration(2 * i + 1, 1, True, True)
                iteration(2 * i + 2, 0, True, True)
            iteration(15, 1, True, False)
            t_ont(15)
            t_xn3t(15)
            t_gate(15)

            def rows_copy(s, p):
                act.wait_ge(rt_ps, s + 1)
                copy(rows_t[:, p], as_chunks(tail)).then_inc(rt_sb, 1)

            def slot(s, p, ahead):
                for f in range(FC):
                    act.wait_ge(gu_ps, FC * s + f + 1)
                    if not isinstance(s, int) or s > 0 or f >= 2:
                        act.wait_ge(act_sb, FC * s + f - 1)
                    nc.scalar.activation(silu_g[:, f % 2], ring[f % NBANKS][:, 0:SLOT], ACT.Silu
                                         ).then_inc(silu_sb, 1)
                    if ahead and f == 5:
                        rows_copy(s + 1, 1 - p)
                act.wait_ge(down_ps, s + 1)
                copy(y_sb[:, p, 0], pv[0][:, 0:D]).then_inc(y0_sb, 1)

            rows_copy(0, 0)
            slot(0, 0, True)
            with act.Fori(0, (NSLOT - 3) // 2) as i:
                slot(2 * i + 1, 1, True)
                slot(2 * i + 2, 0, True)
            slot(NSLOT - 2, 1, True)
            slot(NSLOT - 1, 0, False)

        @block.vector
        def _(vec):
            nc.vector.memset(row_const[:, 0], MASK_Q)
            nc.vector.memset(row_const[:, 1], MAX_K)
            nc.vector.memset(row_const[:, 2], 0.0)
            nc.vector.memset(zero_rows[:], 0.0)
            nc.vector.memset(ones[:], 1.0)
            nc.vector.memset(one_e[:], 1.0)
            nc.vector.memset(q_stack[:], 0.0)
            nc.vector.memset(k_stack[:], 0.0)
            nc.vector.memset(v_aug[:], 0.0).then_inc(slot_step, 1)
            vec.wait_ge(slot_step, 1)
            nc.vector.memset(v_aug[:, :, :, :, HD:HD + 1], 1.0).then_inc(vec_const, 1)
            vec.wait_ge(consts_loaded, 16 * (CONST_LOADS - 1))
            nc.vector.tensor_copy(mask_f[:], mask_u8[:])
            nc.vector.tensor_scalar(mask_h[:], mask_u8[:], MASK_K, None, ALU.mult).then_inc(vec_const, 1)
            vec.wait_ge(pool_const, 11)
            nc.vector.tensor_copy(next_row[:], region0[:])
            nc.vector.tensor_scalar(alibi[:], alibi[:], slope_sb[:, 0:1], None, ALU.mult).then_inc(vec_const, 1)

            def normalise(src, dst, k, st, mo, ve, rs, step, var, rst, done):
                for t in range(NT):
                    o = nc.vector.bn_stats(st[:, t], src[:, t])
                o.then_inc(step, 1)
                vec.wait_ge(step, LN_STEPS * k + 1)
                vec.sem_inc(vec_passed, 1)
                for t in range(NT):
                    o = nc.vector.bn_aggr(mo[:, t], st[:, t])
                o.then_inc(step, 1)
                vec.wait_ge(step, LN_STEPS * k + 2)
                nc.vector.tensor_scalar(ve[:], mo[:, :, 1], EPS_LN, None, ALU.add).then_inc(var, 1)
                vec.wait_ge(rst, k + 1)
                for t in range(NT):
                    o = nc.vector.tensor_scalar(dst[:, t], src[:, t], mo[:, t, 0:1], rs[:, t:t + 1],
                                                ALU.subtract, ALU.mult)
                    if t == 0:
                        o.then_inc(step, 1)
                o.then_inc(done, 1)

            def f_ln1(n, p, h):
                vec.wait_ge(x_loaded[p], 16 * h + 16)
                normalise(x_in[:, p], xn, 2 * n, stats, moments, var_eps, rstd, ln_step, ln_var, ln_rstd, ln1_done)

            def f_scores(n):
                vec.wait_ge(sc_ps, n + 1)
                nc.vector.scalar_tensor_tensor(s1[:], front[:, 0:P + S], SCALE, alibi[:], ALU.mult, ALU.add
                                               ).then_inc(s1_step, 1)
                vec.wait_ge(s1_step, n + 1)
                nc.vector.tensor_reduce(nmax1[:, 0:1], s1[:, 0:P], AX.X, ALU.max, negate=True)
                nc.vector.tensor_reduce(nmax1[:, 1:2], s1[:, P:P + S], AX.X, ALU.max, negate=True
                                        ).then_inc(nmax1_sb, 1)

            def f_sums(n):
                vec.wait_ge(p1_sb, n + 1)
                nc.vector.reciprocal(rsum1[:], sum1[:]).then_inc(rsum1_sb, 1)

            def f_attn(n, p):
                vec.wait_ge(at_ps, n + 1)
                vec.wait_ge(rsum1_sb, n + 1)
                for t in range(NT):
                    o = nc.vector.scalar_tensor_tensor(x1[:, p, t], front[:, t * D:(t + 1) * D], rsum1[:, t:t + 1],
                                                       x_in[:, p, t], ALU.mult, ALU.add)
                o.then_inc(x1_sb, 1)
                vec.wait_ge(x1_sb, n + 1)
                normalise(x1[:, p], xn2, 2 * n + 1, stats, moments, var_eps, rstd, ln_step, ln_var, ln_rstd, ln2_done)

            def f_q(n):
                vec.wait_ge(qhi_sb, n + 1)
                nc.vector.scalar_tensor_tensor(q_lo[:], front[:].rearrange("p (c n) -> p c n", c=NC), HSCALE,
                                               q_hi[:], ALU.mult, ALU.subtract).then_inc(qlo_sb, 1)

            def f_k(n):
                vec.wait_ge(khi_sb, n + 1)
                nc.vector.tensor_tensor(k_lo[:], front[:].rearrange("p (c n) -> p c n", c=NC), k_hi[:], ALU.subtract
                                        ).then_inc(klo_sb, 1)

            def h_max(b, n0, n1):
                for n in range(n0, n1):
                    vec.wait_ge(s_ps, 16 * b + n + 1)
                    nc.vector.tensor_reduce(nmax[:, n // HJ, :, n % HJ],
                                            ring[n % NBANKS][:].rearrange("p (r k) -> p r k", r=2),
                                            AX.X, ALU.max, negate=True).then_inc(smax, 1)

            def h_out(b, jp):
                vec.wait_ge(pv_ps, 8 * b + 2 * jp + 2)
                nc.vector.tensor_copy(o_t[:, jp], pv[jp % 2][:, 0:S]).then_inc(o_sb, 1)

            def t_norm(c, qt):
                vec.wait_ge(oq_ps, 2 * c + qt + 1)
                o = tail[:].rearrange("p (j c w) -> p j c w", j=HJ // 2, w=32)
                nc.vector.reciprocal(rden[:], o[:, :, :, HD]).then_inc(on_step, 1)
                vec.wait_ge(on_step, 2 * c + qt + 1)
                for r in range(2):
                    m = nc.vector.tensor_tensor(
                        o_n[:, qt, r * P:(r + 1) * P].rearrange("p (j c d) -> p j c d", c=2, d=HD),
                        o[:, :, 2 * r:2 * r + 2, 0:HD],
                        rden[:, :, 2 * r:2 * r + 2].unsqueeze(3).to_broadcast([P, HJ // 2, 2, HD]), ALU.mult)
                m.then_inc(on_sb, 1)

            def t_stream(c, p, h):
                vec.wait_ge(fc_ps, c + 1)
                vec.wait_ge(streamed[p], 16 * h + 16)
                vec.wait_ge(xn3_free, c + 1)
                nc.vector.tensor_tensor(x2[:, p], tail[:].rearrange("p (t d) -> p t d", t=NT), x1[:, p], ALU.add
                                        ).then_inc(x2_sb, 1)
                vec.wait_ge(x2_sb, c + 1)
                normalise(x2[:, p], xn3[:, p], c, stats3, moments3, var_eps3, rstd3, ln3_step, ln3_var, ln3_rstd,
                          ln3_done)

            def t_logits(c):
                at = GATE_STEPS * c
                vec.wait_ge(gate_ps, c + 1)
                lg = tail[:, 0:NT * E].rearrange("p (t e) -> p t e", t=NT)
                nc.vector.tensor_reduce(lmax[:], lg, AX.X, ALU.max).then_inc(gate_step, 1)
                vec.wait_ge(gate_step, at + 1)
                nc.vector.tensor_tensor(logits[:], lg, lmax[:].unsqueeze(2).to_broadcast([P, NT, E]), ALU.subtract
                                        ).then_inc(logits_sb, 1)

            def t_choose(c):
                at = GATE_STEPS * c
                vec.wait_ge(gexp_sb, c + 1)
                nc.vector.tensor_reduce(gsum[:], gexp[:], AX.X, ALU.add).then_inc(gate_step, 1)
                vec.wait_ge(gate_step, at + 2)
                nc.vector.reciprocal(grec[:], gsum[:]).then_inc(gate_step, 1)
                vec.wait_ge(gate_step, at + 3)
                nc.vector.tensor_tensor(gprob[:], gexp[:], grec[:].unsqueeze(2).to_broadcast([P, NT, E]), ALU.mult
                                        ).then_inc(gate_step, 1)
                vec.wait_ge(gate_step, at + 4)
                vec.sem_inc(vec_passed, 1)
                for t in range(NT):
                    nc.vector.max(top_v[:, t], gprob[:, t]).then_inc(gate_step, 1)
                vec.wait_ge(gate_step, at + 6)
                vec.sem_inc(vec_passed, 1)
                for t in range(NT):
                    nc.vector.max_index(top_i[:, t], top_v[:, t], gprob[:, t]).then_inc(gate_step, 1)
                nc.vector.tensor_tensor(gden[:], top_v[:, :, 0], top_v[:, :, 1], ALU.add).then_inc(gate_step, 1)
                vec.wait_ge(gate_step, at + 9)
                nc.vector.tensor_copy(top_f[:], top_i[:, :, 0:TOPK]).then_inc(gate_step, 1)
                nc.vector.tensor_scalar(gden1[:], gden[:], EPS_GATE, None, ALU.max).then_inc(gate_step, 1)
                vec.wait_ge(gate_step, at + 11)
                nc.vector.tensor_tensor(
                    onehot[:].rearrange("p t k e -> p (t k) e"),
                    iota_e[:].unsqueeze(1).to_broadcast([P, NT * TOPK, E]),
                    top_f[:].rearrange("p t k -> p (t k)").unsqueeze(2).to_broadcast([P, NT * TOPK, E]),
                    ALU.is_equal).then_inc(gate_step, 1)
                nc.vector.reciprocal(gdenr[:], gden1[:]).then_inc(gate_step, 1)
                vec.wait_ge(gate_step, at + 13)
                nc.vector.tensor_tensor(chosen[:], onehot[:, :, 0], onehot[:, :, 1], ALU.add).then_inc(chosen_sb, 1)
                nc.vector.tensor_tensor(gate_all[:, bass.ds(c * NT, NT)], top_v[:, :, 0:TOPK],
                                        gdenr[:].unsqueeze(2).to_broadcast([P, NT, TOPK]), ALU.mult)
                nc.vector.tensor_copy(onehot_all[:, bass.ds(c * NT * TOPK, NT * TOPK)],
                                      onehot[:].rearrange("p t k e -> p (t k) e")).then_inc(gate_step, 1)

            def t_place(c, p):
                at = GATE_STEPS * c
                vec.wait_ge(rank_ps, c + 1)
                nc.vector.tensor_tensor(rank[:], tail[:, 0:NT * E].rearrange("p (t e) -> p t e", t=NT),
                                        next_row[:].unsqueeze(1).to_broadcast([P, NT, E]), ALU.add
                                        ).then_inc(gate_step, 1)
                vec.wait_ge(gate_step, at + 15)
                for t in range(NT):
                    o = nc.vector.tensor_tensor(onehot_pos[:, t], onehot[:, t],
                                                rank[:, t].unsqueeze(1).to_broadcast([P, TOPK, E]), ALU.mult)
                o.then_inc(gate_step, 1)
                nc.vector.tensor_tensor(next_row[:], next_row[:], tail[:, NT * E:(NT + 1) * E], ALU.add
                                        ).then_inc(rank_sb, 1)
                vec.wait_ge(gate_step, at + 16)
                nc.vector.tensor_reduce(pos_f[:], onehot_pos[:].rearrange("p t k e -> p (t k) e"), AX.X, ALU.add
                                        ).then_inc(gate_step, 1)
                vec.wait_ge(gate_step, at + 17)
                nc.vector.tensor_copy(pos_all[:, bass.ds(c * NT * TOPK, NT * TOPK)], pos_f[:])
                nc.vector.tensor_copy(pos_i[:, p], pos_f[:]).then_inc(pos_sb, 1)

            def iteration(b, p, h, tail_of, front_of):
                c, n = b - 1, b + 1
                if front_of:
                    f_ln1(n, 1 - p, h + p)
                h_max(b, 0, 4)
                if tail_of:
                    t_norm(c, 0)
                h_max(b, 4, 6)
                if tail_of:
                    t_norm(c, 1)
                h_max(b, 6, 10)
                if front_of:
                    f_scores(n)
                if tail_of:
                    t_stream(c, 1 - p, h - 1 + p)
                h_max(b, 10, 12)
                if front_of:
                    f_sums(n)
                h_max(b, 12, 14)
                if tail_of:
                    t_logits(c)
                if front_of:
                    f_attn(n, 1 - p)
                if tail_of:
                    t_choose(c)
                h_max(b, 14, 16)
                if tail_of:
                    t_place(c, 1 - p)
                if front_of:
                    f_q(n)
                h_out(b, 0)
                if front_of:
                    f_k(n)
                for jp in range(1, HJ // 2):
                    h_out(b, jp)

            vec.wait_ge(pool_const, 13)
            f_ln1(0, 0, 0)
            f_scores(0)
            f_sums(0)
            f_attn(0, 0)
            f_q(0)
            f_k(0)
            iteration(0, 0, 0, False, True)
            with vec.Fori(0, 7) as i:
                iteration(2 * i + 1, 1, i, True, True)
                iteration(2 * i + 2, 0, i + 1, True, True)
            iteration(15, 1, 7, True, False)
            t_norm(15, 0)
            t_norm(15, 1)
            t_stream(15, 1, 7)
            t_logits(15)
            t_choose(15)
            t_place(15, 1)

            step = [1]

            def then(ins):
                step[0] += 1
                ins.then_inc(slot_step, 1)
                vec.wait_ge(slot_step, step[0])

            vec.wait_ge(rank_sb, B)
            then(nc.vector.tensor_tensor(pad_f[:], pad_iota[:], next_row[:].unsqueeze(2).to_broadcast([P, E, NT]),
                                         ALU.add))
            nc.vector.tensor_copy(pad_i[:], pad_f[:].rearrange("p e t -> p (e t)")).then_inc(pad_sb, 1)
            then(nc.vector.tensor_tensor(count[:], next_row[:], region0[:], ALU.subtract))
            then(nc.vector.tensor_scalar(count[:], count[:], float(SLOT - 1), None, ALU.add))
            then(nc.vector.tensor_copy(count_i[:], count[:]))
            then(nc.vector.tensor_scalar(slots_i[:], count_i[:], SLOT.bit_length() - 1, None,
                                         ALU.arith_shift_right))
            then(nc.vector.tensor_copy(slots_f[:], slots_i[:]))
            then(nc.vector.tensor_tensor_scan(slot_end[:], one_e[:], slots_f[:], 0.0, ALU.mult, ALU.add))
            then(nc.vector.tensor_scalar(jump[:], slots_f[0:1], -float(SLOT), float(REGION), ALU.mult, ALU.add))
            then(nc.vector.tensor_tensor(past[:], slot_end[0:1].unsqueeze(1).to_broadcast([1, NSLOT, E]),
                                         slot_id[:].unsqueeze(2).to_broadcast([1, NSLOT, E]), ALU.is_le))
            then(nc.vector.tensor_tensor(past_jump[:], past[:], jump[:].unsqueeze(1).to_broadcast([1, NSLOT, E]),
                                         ALU.mult))
            then(nc.vector.tensor_reduce(slot_e[:], past[:], AX.X, ALU.add))
            then(nc.vector.tensor_reduce(slot_r[:], past_jump[:], AX.X, ALU.add))
            then(nc.vector.scalar_tensor_tensor(slot_r1[:], slot_id[:], float(SLOT), slot_r[:], ALU.mult, ALU.add))
            then(nc.vector.tensor_scalar(slot_tab[:, 0], slot_r1[:], float(DUMMY), None, ALU.min))
            nc.vector.tensor_scalar(slot_tab[:, 1], slot_e[:], float(E - 1), None, ALU.min).then_inc(table_sb, 1)
            then(nc.vector.tensor_tensor(moved[:], slot_end[:], slots_f[:], ALU.subtract))
            then(nc.vector.scalar_tensor_tensor(moved[:], moved[:], float(SLOT), region0[:], ALU.mult, ALU.subtract))
            then(nc.vector.tensor_tensor(onehot_moved[:], onehot_all[:],
                                         moved[:].unsqueeze(1).to_broadcast([P, B * NT * TOPK, E]), ALU.mult))
            then(nc.vector.tensor_reduce(pos_moved[:], onehot_moved[:], AX.X, ALU.add))
            then(nc.vector.tensor_tensor(gather_all[:], pos_moved[:], pos_all[:], ALU.add))

            def slot(s, p):
                for f in range(FC):
                    vec.wait_ge(silu_sb, FC * s + f + 1)
                    if not isinstance(s, int) or s > 0 or f >= 4:
                        vec.wait_ge(act_used, FC * s + f - 3)
                    nc.vector.tensor_tensor(act_t[:, f % 4], silu_g[:, f % 2], ring[f % NBANKS][:, SLOT:2 * SLOT],
                                            ALU.mult).then_inc(act_sb, 1)
                vec.wait_ge(down_ps, s + 1)
                nc.vector.tensor_copy(y_sb[:, p, 1], pv[1][:, 0:D]).then_inc(y1_sb, 1)

            slot(0, 0)
            with vec.Fori(0, (NSLOT - 3) // 2) as i:
                slot(2 * i + 1, 1)
                slot(2 * i + 2, 0)
            slot(NSLOT - 2, 1)
            slot(NSLOT - 1, 0)

            def places(b, p):
                nc.vector.tensor_copy(gather_i[:, p], gather_all[:, bass.ds(b * NT * TOPK, NT * TOPK)]
                                      ).then_inc(idx_sb, 1)

            def combine(b, p, h):
                vec.wait_ge(rows_got[p], 64 * h + 64)
                vec.wait_ge(stream_got[p], 16 * h + 16)
                if not isinstance(b, int) or b >= 2:
                    vec.wait_ge(out_done[p], 16 * h)
                for t in range(NT):
                    o = nc.vector.scalar_tensor_tensor(acc[:, t], gathered[:, p, t, 0],
                                                       gate_all[:, bass.ds(b * NT + t, 1), 0],
                                                       stream_in[:, p, t], ALU.mult, ALU.add)
                o.then_inc(acc_step, 1)
                vec.wait_ge(acc_step, b + 1)
                for t in range(NT):
                    o = nc.vector.scalar_tensor_tensor(out_sb[:, p, t], gathered[:, p, t, 1],
                                                       gate_all[:, bass.ds(b * NT + t, 1), 1],
                                                       acc[:, t], ALU.mult, ALU.add)
                o.then_inc(out_ready, 1)
                vec.wait_ge(out_ready, b + 1)

            places(0, 0)
            places(1, 1)
            for p in range(2):
                combine(p, p, 0)
                places(p + 2, p)
            with vec.Fori(1, B // 2 - 1) as i:
                for p in range(2):
                    combine(2 * i + p, p, i)
                    places(2 * i + p + 2, p)
            for p in range(2):
                combine(B - 2 + p, p, B // 2 - 1)

        @block.tensor
        def _(pe):
            def transpose(to, frm):
                return nc.tensor.transpose(to, frm, ident[0:frm.shape[0], 0:frm.shape[0]])

            def transpose_tiles(bank_, src):
                for t in range(NT):
                    for c in range(NC):
                        o = transpose(bank_[:, c * S + t * P:c * S + (t + 1) * P], src[:, t, c * P:(c + 1) * P])
                return o

            def project_t(bank_, w, src_t):
                for ob in range(NC):
                    for c in range(NC):
                        o = nc.tensor.matmul(bank_[:, ob * S:(ob + 1) * S], w[:, c, ob * P:(ob + 1) * P],
                                             src_t[:, c], start=(c == 0), stop=(c == NC - 1))
                return o

            def project(bank_, src_t, w):
                for t in range(NT):
                    for c in range(NC):
                        o = nc.tensor.matmul(bank_[:, t * D:(t + 1) * D], src_t[:, c, t * P:(t + 1) * P],
                                             w[:, c], start=(c == 0), stop=(c == NC - 1))
                return o

            pe.wait_ge(pool_const, 11)
            pe.wait_ge(consts_loaded, 16 * (CONST_LOADS - 1))
            for i in range(5):
                if i:
                    pe.wait_ge(w_tsb, i)
                transpose_tiles(front, w_raw[:, i]).then_inc(w_tps, 1)
            pe.wait_ge(vec_const, 2)
            for t in range(NT):
                o = transpose(tail[:, t * B:(t + 1) * B], mask_f[:, t * P:(t + 1) * P])
            o.then_inc(mask_tps, 1)
            pe.wait_ge(w_tsb, 6)

            def f_xnt(n):
                pe.wait_ge(ln1_done, n + 1)
                if not isinstance(n, int) or n > 0:
                    pe.wait_ge(v2_sb, n)
                transpose_tiles(front, xn).then_inc(xnt_ps, 1)

            def f_q1(n):
                pe.wait_ge(xnt_sb, n + 1)
                project_t(front, wqk_sb, xn_t).then_inc(q1_ps, 1)

            def f_v1(n):
                pe.wait_ge(q1_sb, n + 1)
                project(front, xn_t, w_t[:, WV1]).then_inc(v1_ps, 1)

            def f_scores(n):
                pe.wait_ge(v1_sb, n + 1)
                for q0, k1, to in ((0, P, 0), (P, S, P)):
                    for c in range(NC):
                        o = nc.tensor.matmul(front[:, to:to + k1], q1_t[:, c, q0:q0 + P], xn_t[:, c, 0:k1],
                                             start=(c == 0), stop=(c == NC - 1))
                o.then_inc(sc_ps, 1)

            def f_probs_t(n):
                pe.wait_ge(p1_sb, n + 1)
                for blk in range(3):
                    o = transpose(front[:, blk * P:(blk + 1) * P], p1[:, blk * P:(blk + 1) * P])
                o.then_inc(p1t_ps, 1)

            def f_attn(n):
                pe.wait_ge(p1t_sb, n + 1)
                nc.tensor.matmul(front[:, 0:D], p1_t[:, 0], v1[:, 0], start=True, stop=True)
                nc.tensor.matmul(front[:, D:2 * D], p1_t[:, 1], v1[:, 0], start=True, stop=False)
                nc.tensor.matmul(front[:, D:2 * D], p1_t[:, 2], v1[:, 1], start=False, stop=True).then_inc(at_ps, 1)

            def f_xn2t(n):
                pe.wait_ge(ln2_done, n + 1)
                transpose_tiles(front, xn2).then_inc(xn2t_ps, 1)

            def f_ctxt(n, p, h):
                pe.wait_ge(xn2t_sb, n + 1)
                pe.wait_ge(ctx_loaded[p], 16 * h + 16)
                transpose_tiles(front, ctx_in[:, p]).then_inc(ctxt_ps, 1)

            def f_q(n):
                pe.wait_ge(ctxt_sb, n + 1)
                project_t(front, w_t[:, WQ], xn2_t).then_inc(q_ps, 1)

            def f_k(n):
                pe.wait_ge(qlo_sb, n + 1)
                project_t(front, w_t[:, WK], ctx_t).then_inc(k_ps, 1)

            def f_v2(n):
                pe.wait_ge(klo_sb, n + 1)
                project(front, ctx_t, w_t[:, WV2]).then_inc(v2_ps, 1)

            def h_scores(b, p, n0, n1):
                for n in range(n0, n1):
                    qt, j = n // HJ, n % HJ
                    if n >= NBANKS:
                        pe.wait_ge(smax, 16 * b + n - NBANKS + 1)
                    for r in range(2):
                        o = nc.tensor.matmul(ring[n % NBANKS][:, r * S:(r + 1) * S],
                                             q_stack[:, p, j, qt * P:(qt + 1) * P], k_stack[:, p, r, j],
                                             start=True, stop=True)
                    o.then_inc(s_ps, 1)

            def h_max(b):
                pe.wait_ge(smax, 16 * b + 16)
                for qt in range(NT):
                    o = transpose(tail[0:H, qt * P:(qt + 1) * P], nmax[:, qt].rearrange("p r j -> p (r j)"))
                o.then_inc(nmt_ps, 1)

            def h_scores_t(b, p, g):
                jp, kt = g // 2, g % 2
                if g >= 2:
                    pe.wait_ge(exp_sb, 8 * b + g - 1)
                for r in range(2):
                    for jj in range(2):
                        o = nc.tensor.matmul(ring[2 * (g % 2) + r][:, jj * S:(jj + 1) * S],
                                             k_stack[:, p, r, 2 * jp + jj, kt * P:(kt + 1) * P],
                                             q_stack[:, p, 2 * jp + jj], start=True, stop=True)
                o.then_inc(st_ps, 1)

            def h_values(b, p, g):
                jp, kt = g // 2, g % 2
                pe.wait_ge(exp_sb, 8 * b + g + 1)
                if kt == 0 and (not isinstance(b, int) or b > 0 or jp >= 2):
                    pe.wait_ge(o_sb, 4 * b + jp - 1)
                for r in range(2):
                    for jj in range(2):
                        q = 32 * (2 * r + jj)
                        o = nc.tensor.matmul(pv[jp % 2][q:q + 32, 0:S], v_aug[:, p, kt, HJ * r + 2 * jp + jj],
                                             probs_t[:, g % 2, r, jj], start=(kt == 0), stop=(kt == 1))
                o.then_inc(pv_ps, 1)

            def t_queries(c, qt):
                if qt == 0:
                    pe.wait_ge(o_sb, 4 * c + 4)
                else:
                    pe.wait_ge(on_sb, 2 * c + 1)
                for jp in range(HJ // 2):
                    o = transpose(tail[:, jp * P:(jp + 1) * P], o_t[:, jp, qt * P:(qt + 1) * P])
                o.then_inc(oq_ps, 1)

            def t_ont(c):
                pe.wait_ge(on_sb, 2 * c + 2)
                transpose_tiles(tail, o_n).then_inc(ont_ps, 1)

            def t_fc(c):
                pe.wait_ge(ont_sb, c + 1)
                project(tail, o_nt, w_t[:, WFC]).then_inc(fc_ps, 1)

            def t_xn3t(c, p):
                pe.wait_ge(ln3_done, c + 1)
                transpose_tiles(tail, xn3[:, p]).then_inc(xn3t_ps, 1)

            def t_gate(c):
                pe.wait_ge(xn3t_sb, c + 1)
                for t in range(NT):
                    for k in range(NC):
                        o = nc.tensor.matmul(tail[:, t * E:(t + 1) * E], xn3_t[:, k, t * P:(t + 1) * P], wg_sb[:, k],
                                             start=(k == 0), stop=(k == NC - 1))
                o.then_inc(gate_ps, 1)

            def t_rank(c):
                pe.wait_ge(chosen_sb, c + 1)
                nc.tensor.matmul(tail[:, 0:NT * E], tri[:], chosen[:].rearrange("p t e -> p (t e)"),
                                 start=True, stop=False)
                nc.tensor.matmul(tail[:, E:2 * E], ones[:], chosen[:, 0], start=False, stop=True)
                nc.tensor.matmul(tail[:, NT * E:(NT + 1) * E], ones[:], chosen[:, 0], start=True, stop=False)
                nc.tensor.matmul(tail[:, NT * E:(NT + 1) * E], ones[:], chosen[:, 1], start=False, stop=True
                                 ).then_inc(rank_ps, 1)

            def iteration(b, p, h, tail_of, front_of):
                c, n, q = b - 1, b + 1, 1 - p
                pe.wait_ge(stacked[p], 16 * STACK_DMAS * (h + 1))
                h_scores(b, p, 0, 4)
                if tail_of:
                    t_queries(c, 0)
                if front_of:
                    f_xnt(n)
                h_scores(b, p, 4, 6)
                if tail_of:
                    t_queries(c, 1)
                if front_of:
                    f_q1(n)
                h_scores(b, p, 6, 8)
                if tail_of:
                    t_ont(c)
                if front_of:
                    f_v1(n)
                h_scores(b, p, 8, 10)
                if tail_of:
                    t_fc(c)
                if front_of:
                    f_scores(n)
                h_scores(b, p, 10, 12)
                if tail_of:
                    t_xn3t(c, q)
                if front_of:
                    f_probs_t(n)
                h_scores(b, p, 12, 14)
                if tail_of:
                    t_gate(c)
                if front_of:
                    f_attn(n)
                h_scores(b, p, 14, 16)
                if tail_of:
                    t_rank(c)
                    pe.wait_ge(rank_sb, c + 1)
                h_max(b)
                if front_of:
                    f_xn2t(n)
                    f_ctxt(n, q, h + p)
                pe.wait_ge(max_stacked[p], 32 * (h + 1))
                pe.wait_ge(v2_sb, b + 1)
                h_scores_t(b, p, 0)
                for g in range(8):
                    if g < 7:
                        h_scores_t(b, p, g + 1)
                    if front_of and g == 1:
                        f_q(n)
                    if front_of and g == 3:
                        f_k(n)
                    if front_of and g == 5:
                        f_v2(n)
                    h_values(b, p, g)

            f_xnt(0)
            f_q1(0)
            f_v1(0)
            f_scores(0)
            f_probs_t(0)
            f_attn(0)
            f_xn2t(0)
            f_ctxt(0, 0, 0)
            f_q(0)
            f_k(0)
            f_v2(0)
            iteration(0, 0, 0, False, True)
            with pe.Fori(0, 7) as i:
                iteration(2 * i + 1, 1, i, True, True)
                iteration(2 * i + 2, 0, i + 1, True, True)
            iteration(15, 1, 7, True, False)
            t_queries(15, 0)
            t_queries(15, 1)
            t_ont(15)
            t_fc(15)
            t_xn3t(15, 1)
            t_gate(15)
            t_rank(15)

            def rows_transposed(s, p, h):
                pe.wait_ge(rows_in[p], 16 * h + 16)
                transpose_tiles(tail, rows[:, p]).then_inc(rt_ps, 1)

            def gate_up(s, p, f):
                if not isinstance(s, int) or s > 0 or f >= NBANKS:
                    pe.wait_ge(act_sb, FC * s + f - NBANKS + 1)
                for half in range(2):
                    for c in range(NC):
                        o = nc.tensor.matmul(ring[f % NBANKS][:, half * SLOT:(half + 1) * SLOT],
                                             wgu_sb[:, p, c, half * F + f * P:half * F + (f + 1) * P],
                                             rows_t[:, p, c], start=(c == 0), stop=(c == NC - 1))
                o.then_inc(gu_ps, 1)

            def down(s, p, f):
                pe.wait_ge(act_sb, FC * s + f + 1)
                if f == 0 and (not isinstance(s, int) or s > 0):
                    pe.wait_ge(y0_sb, s)
                    pe.wait_ge(y1_sb, s)
                for t in range(NT):
                    o = nc.tensor.matmul(pv[t][:, 0:D], act_t[:, f % 4, t * P:(t + 1) * P], wd_sb[:, p, f],
                                         start=(f == 0), stop=(f == FC - 1))
                    if t == 0 and f == FC - 1:
                        o.then_inc(act_used, 1)
                o.then_inc(down_ps if f == FC - 1 else act_used, 1)

            def slot(s, p, h, ahead):
                pe.wait_ge(rt_sb, s + 1)
                pe.wait_ge(w_in[p], 32 * h + 32)
                for f in range(FC):
                    gate_up(s, p, f)
                    if ahead and f == 4:
                        rows_transposed(s + 1, 1 - p, h + p)
                    if f >= 2:
                        down(s, p, f - 2)
                down(s, p, FC - 2)
                down(s, p, FC - 1)

            pe.wait_ge(rank_sb, B)
            rows_transposed(0, 0, 0)
            slot(0, 0, 0, True)
            with pe.Fori(0, (NSLOT - 3) // 2) as i:
                slot(2 * i + 1, 1, i, True)
                slot(2 * i + 2, 0, i + 1, True)
            slot(NSLOT - 2, 1, (NSLOT - 3) // 2, True)
            slot(NSLOT - 1, 0, (NSLOT - 1) // 2, False)


def kernel(x, ctx_1024, mask_BxS2_bf0, L0_attn_W_qk, L0_attn_W_v, L0_attn_alibi_slope, L0_xattn_wq, L0_xattn_wk,
           L0_xattn_wv, L0_xattn_wfc, L0_ffn_w_gate, L0_ffn_w_gate_up, L0_ffn_w_down):
    import concourse.bacc as bacc
    from concourse.bass_utils import run_bass_kernel_spmd

    given = {"x": x, "ctx": ctx_1024, "mask": mask_BxS2_bf0,
             "w_qk": L0_attn_W_qk, "w_v": L0_attn_W_v, "slope": L0_attn_alibi_slope, "wq": L0_xattn_wq,
             "wk": L0_xattn_wk, "wv": L0_xattn_wv, "wfc": L0_xattn_wfc, "w_gate": L0_ffn_w_gate,
             "w_gu": L0_ffn_w_gate_up, "w_down": L0_ffn_w_down}
    given = {k: np.ascontiguousarray(v) for k, v in given.items()}
    nc = bacc.Bacc("TRN2", target_bir_lowering=False, num_devices=1)
    aps = {k: nc.dram_tensor(f"in_{k}", v.shape, mybir.dt.from_np(v.dtype), kind="ExternalInput").ap()
           for k, v in given.items()}
    out = nc.dram_tensor("out", (B, S, D), F32, kind="ExternalOutput").ap()
    decoder_layer(nc, **aps, out=out)
    r = run_bass_kernel_spmd(nc, [{f"in_{k}": v for k, v in given.items()}], core_ids=[0])
    return r.results[0]["out"]
```

```python
from contextlib import ExitStack

import numpy as np
import concourse.bass as bass
from concourse import mybir

F32 = mybir.dt.float32
F16 = mybir.dt.float16
U32 = mybir.dt.uint32
I32 = mybir.dt.int32
U8 = mybir.dt.uint8
ALU = mybir.AluOpType
ACT = mybir.ActivationFunctionType
AX = mybir.AxisListType

B, S, D = 16, 256, 256
P = 128
NT = S // P
NC = D // P
H, HD = 16, 16
HJ = H // 2
E, F, TOPK = 8, 1024, 2
EPS_LN, EPS_GATE = 1e-5, 1e-9
SCALE = float(D) ** -0.5
HSCALE = float(HD) ** -0.5
NEG = -1.0e30
MASK_BIAS = -3.0e38
MASK_Q, MASK_K = 32768.0, -32768.0
MAX_Q, MAX_K = 1.0 / 64, 64.0

SLOT = 256
NSLOT = B * S * TOPK // SLOT + E - 1
REGION = B * S + SLOT
DUMMY = E * REGION
ROWS = DUMMY + SLOT
FC = F // P
WSCALE, RSCALE, ASCALE = 128.0, 32.0, 32.0
CHUNK = 1024
CHUNKS = 3
GU_CHUNKS = 2 * F * NC // CHUNK


def decoder_layer(nc, x, ctx, mask, w_qk, w_v, slope, wq, wk, wv, wfc, w_gate, w_gu, w_down, out):
    with ExitStack() as stack:
        def sb(name, shape, dt=F32):
            return stack.enter_context(nc.sbuf_tensor(name, shape, dt))

        attention = ExitStack()

        def ab(name, shape, dt=F32):
            return attention.enter_context(nc.sbuf_tensor(name, shape, dt))

        def bank(name):
            return stack.enter_context(nc.psum_tensor(name, [P, 512], F32))

        def sem(name):
            return stack.enter_context(nc.semaphore(name))

        def sems(name, n=2):
            return [sem(f"{name}{i}") for i in range(n)]

        routed = nc.dram_tensor("routed_rows", [ROWS, D], F32, kind="Internal").ap()
        expert_out = nc.dram_tensor("expert_rows", [NSLOT * SLOT, D], F32, kind="Internal").ap()
        gu_split = nc.dram_tensor("gu_split", [E, P, 2, NC * 2 * F], F16, kind="Internal").ap()
        down_split = nc.dram_tensor("down_split", [E, P, 2, FC * D], F16, kind="Internal").ap()
        mask_rows = nc.dram_tensor("mask_rows", [B, HJ, S], F16, kind="Internal").ap()

        ident = sb("ident", [P, P])
        tri = sb("tri", [P, P], F16)
        ones = sb("ones", [P, P], F16)
        half_neg = sb("half_neg", [P, NT])
        iota_e = sb("iota_e", [P, E])
        pad_iota = sb("pad_iota", [P, E, NT])
        alibi = sb("alibi", [P, P + S])
        slope_sb = sb("slope_sb", [P, 1])
        zero_rows = sb("zero_rows", [P, D])
        row_const = sb("row_const", [HJ, 3, S], F16)
        mask_u8 = sb("mask_u8", [B, S], U8)
        mask_f = sb("mask_f", [B, S])
        mask_h = sb("mask_h", [B, S], F16)
        mask_bias = sb("mask_bias", [P, NT, B])
        w_t = sb("w_t", [P, 5, NC, D])
        wqk_sb = sb("wqk_sb", [P, NC, D])
        wg_sb = sb("wg_sb", [P, NC, E])
        WV1, WQ, WK, WV2, WFC = range(5)

        x_res = sb("x_res", [P, B * NT, D])
        x_in = sb("x_in", [P, 2, NT, D])
        ctx_in = sb("ctx_in", [P, 2, NT, D])
        stats = sb("stats", [P, NT, 6])
        moments = sb("moments", [P, NT, 2])
        var_eps = sb("var_eps", [P, NT])
        rstd = sb("rstd", [P, NT])
        xn = sb("xn", [P, NT, D])
        xn_t = sb("xn_t", [P, NC, S])
        q1_t = sb("q1_t", [P, NC, S])
        v1 = sb("v1", [P, NT, D])
        s1 = sb("s1", [P, P + S])
        nmax1 = sb("nmax1", [P, NT])
        p1 = sb("p1", [P, P + S])
        sum1 = sb("sum1", [P, NT])
        rsum1 = sb("rsum1", [P, NT])
        p1_t = sb("p1_t", [P, 3, P])
        xn2 = sb("xn2", [P, NT, D])
        xn2_t = sb("xn2_t", [P, NC, S])
        ctx_t = sb("ctx_t", [P, NC, S])
        q_hi = sb("q_hi", [P, NC, S], F16)
        q_lo = sb("q_lo", [P, NC, S], F16)
        k_hi = sb("k_hi", [P, NC, S], F16)
        k_lo = sb("k_lo", [P, NC, S], F16)

        nmax = sb("nmax", [P, NT, 2, HJ])
        nmax_t = sb("nmax_t", [H, S], F16)
        o_t = sb("o_t", [P, 2, HJ // 2, S])

        rden = sb("rden", [P, NT, HJ // 2, 4])
        o_n = sb("o_n", [P, NT, D])
        o_nt = sb("o_nt", [P, NC, S])
        stats3 = sb("stats3", [P, NT, 6])
        moments3 = sb("moments3", [P, NT, 2])
        var_eps3 = sb("var_eps3", [P, NT])
        rstd3 = sb("rstd3", [P, NT])
        xn3 = sb("xn3", [P, 2, NT, D])
        xn3_t = sb("xn3_t", [P, NC, S])
        lmax = sb("lmax", [P, NT])
        logits = sb("logits", [P, NT, E])
        gexp = sb("gexp", [P, NT, E])
        gsum = sb("gsum", [P, NT])
        grec = sb("grec", [P, NT])
        gprob = sb("gprob", [P, NT, E])
        top_v = sb("top_v", [P, NT, 8])
        top_i = sb("top_i", [P, NT, 8], U32)
        top_f = sb("top_f", [P, NT, TOPK])
        gden = sb("gden", [P, NT])
        gden1 = sb("gden1", [P, NT])
        gdenr = sb("gdenr", [P, NT])
        onehot = sb("onehot", [P, NT, TOPK, E])
        chosen = sb("chosen", [P, NT, E], F16)
        rank = sb("rank", [P, NT, E])
        onehot_pos = sb("onehot_pos", [P, NT, TOPK, E])
        pos_f = sb("pos_f", [P, NT * TOPK])
        pos_i = sb("pos_i", [P, 2, NT * TOPK], U32)
        next_row = sb("next_row", [P, E])
        pos_all = sb("pos_all", [P, B * NT * TOPK])
        onehot_all = sb("onehot_all", [P, B * NT * TOPK, E])
        gate_all = sb("gate_all", [P, B * NT, TOPK])

        region0 = sb("region0", [P, E])
        pad_f = sb("pad_f", [P, E, NT])
        pad_i = sb("pad_i", [P, E * NT], U32)
        count = sb("count", [P, E])
        count_i = sb("count_i", [P, E], I32)
        slots_i = sb("slots_i", [P, E], I32)
        slots_f = sb("slots_f", [P, E])
        one_e = sb("one_e", [P, E])
        slot_end = sb("slot_end", [P, E])
        moved = sb("moved", [P, E])
        onehot_moved = sb("onehot_moved", [P, B * NT * TOPK, E])
        pos_moved = sb("pos_moved", [P, B * NT * TOPK])
        gather_all = sb("gather_all", [P, B * NT * TOPK], U32)
        jump = sb("jump", [1, E])
        slot_id = sb("slot_id", [1, NSLOT])
        past = sb("past", [1, NSLOT, E])
        past_jump = sb("past_jump", [1, NSLOT, E])
        slot_e = sb("slot_e", [1, NSLOT])
        slot_r = sb("slot_r", [1, NSLOT])
        slot_r1 = sb("slot_r1", [1, NSLOT])
        slot_tab = sb("slot_tab", [1, 2, NSLOT], I32)
        rows = sb("rows", [P, 2, NT, D])
        rows_hi = sb("rows_hi", [P, 2, NC, SLOT], F16)
        rows_lo = sb("rows_lo", [P, 2, NC, SLOT], F16)

        q_stack = ab("q_stack", [P, 2, HJ, S], F16)
        k_stack = ab("k_stack", [P, 2, 2, HJ, S], F16)
        v_aug = ab("v_aug", [P, 2, NT, H, 32])
        probs_t = ab("probs_t", [P, 2, 2, 2, S])
        w_piece = ab("w_piece", [P, CHUNKS, CHUNK])
        w_scaled = ab("w_scaled", [P, CHUNKS, CHUNK])
        w_halves = ab("w_halves", [P, CHUNKS, 2, CHUNK], F16)
        w_raw = ab("w_raw", [P, 5, NC, D])
        attention.close()
        wgu_sb = sb("wgu_sb", [P, 2, 2, NC * 2 * F], F16)
        wd_sb = sb("wd_sb", [P, 2, 2, FC * D], F16)
        silu_g = sb("silu_g", [P, 2, SLOT])
        act_t = sb("act_t", [P, 2, SLOT])
        act_hi = sb("act_hi", [P, 4, SLOT], F16)
        act_lo = sb("act_lo", [P, 4, SLOT], F16)
        y_sb = sb("y_sb", [P, 2, NT, D])

        gather_i = sb("gather_i", [P, 2, NT * TOPK], U32)
        gathered = sb("gathered", [P, 2, NT, TOPK, D])
        acc = sb("acc", [P, NT, D])
        out_sb = sb("out_sb", [P, 2, NT, D])

        s_ring = [bank(f"s_ring{i}") for i in range(2)]
        t_ring = [bank(f"t_ring{i}") for i in range(2)]
        pv = bank("pv")
        front = [bank(f"front{i}") for i in range(2)]
        tail = bank("tail")
        gu_ring = s_ring + t_ring
        consts_loaded = sem("consts_loaded")
        pool_const = sem("pool_const")
        vec_const = sem("vec_const")
        w_tps = sem("w_tps")
        w_tsb = sem("w_tsb")
        mask_tps = sem("mask_tps")
        rows_set = sem("rows_set")
        x_loaded, ctx_loaded = sems("x_loaded"), sems("ctx_loaded")
        ln_step, ln_var, ln_rstd, ln1_done, ln2_done = map(sem, "ln_step ln_var ln_rstd ln1_done ln2_done".split())
        xnt_ps, xnt_sb, q1_ps, q1_sb, v1_ps, v1_sb = map(sem, "xnt_ps xnt_sb q1_ps q1_sb v1_ps v1_sb".split())
        sc_ps, s1_step, nmax1_sb, p1_sb, rsum1_sb = map(sem, "sc_ps s1_step nmax1_sb p1_sb rsum1_sb".split())
        p1t_ps, p1t_sb, at_ps, x1_sb = map(sem, "p1t_ps p1t_sb at_ps x1_sb".split())
        xn2t_ps, xn2t_sb, ctxt_ps, ctxt_sb = map(sem, "xn2t_ps xn2t_sb ctxt_ps ctxt_sb".split())
        q_ps, qhi_sb, qlo_sb, k_ps, khi_sb, klo_sb = map(sem, "q_ps qhi_sb qlo_sb k_ps khi_sb klo_sb".split())
        v2_ps, v2_sb = sem("v2_ps"), sem("v2_sb")
        stacked = sems("stacked")
        STACK_DMAS = 16
        s_ps, smax, nmt_ps, nmt_sb = map(sem, "s_ps smax nmt_ps nmt_sb".split())
        max_stacked = sems("max_stacked")
        st_ps, exp_sb, pv_ps, o_sb = map(sem, "st_ps exp_sb pv_ps o_sb".split())
        oq_ps, on_step, on_sb, ont_ps, ont_sb = map(sem, "oq_ps on_step on_sb ont_ps ont_sb".split())
        fc_ps, x2_sb, ln3_step, ln3_var, ln3_rstd, ln3_done = map(
            sem, "fc_ps x2_sb ln3_step ln3_var ln3_rstd ln3_done".split())
        xn3t_ps, xn3t_sb, gate_ps, gate_step, logits_sb, gexp_sb = map(
            sem, "xn3t_ps xn3t_sb gate_ps gate_step logits_sb gexp_sb".split())
        chosen_sb, rank_ps, rank_sb, pos_sb = map(sem, "chosen_sb rank_ps rank_sb pos_sb".split())
        scattered, xn3_free = sems("scattered"), sem("xn3_free")
        piece_in, piece_hi, piece_split, piece_out = map(sem, "piece_in piece_hi piece_split piece_out".split())
        slot_step, pad_sb, table_sb, padded = map(sem, "slot_step pad_sb table_sb padded".split())
        dummied = sem("dummied")
        rows_in, w_in, y_out = sems("rows_in"), sems("w_in"), sems("y_out")
        rt_ps, rhi_sb, rlo_sb, gu_ps, silu_sb, act_sb = map(
            sem, "rt_ps rhi_sb rlo_sb gu_ps silu_sb act_sb".split())
        ahi_sb, alo_sb, down_ps, y0_sb, y1_sb, act_used = map(sem, "ahi_sb alo_sb down_ps y0_sb y1_sb act_used".split())
        idx_sb, acc_step, out_ready = sem("idx_sb"), sem("acc_step"), sem("out_ready")
        rows_got, out_done = sems("rows_got"), sems("out_done")

        act_passed, vec_passed, pool_passed = map(sem, "act_passed vec_passed pool_passed".split())

        block = stack.enter_context(nc.Block())

        CONST_LOADS = 4 + 5
        ROW_SETS = 2 * 2 * 2 + HJ
        LN_STEPS = 2
        GATE_STEPS = 17

        def attention_loop(eng, iteration):
            iteration(-2, 0, -1, False, False, False, True, True)
            iteration(-1, 1, -1, False, False, True, True, True)
            iteration(0, 0, 0, False, True, True, True, True)
            with eng.Fori(0, 6) as i:
                iteration(2 * i + 1, 1, i, True, True, True, True, True)
                iteration(2 * i + 2, 0, i + 1, True, True, True, True, True)
            iteration(13, 1, 6, True, True, True, True, False)
            iteration(14, 0, 7, True, True, True, False, False)
            iteration(15, 1, 7, True, True, False, False, False)
            iteration(16, 0, 8, True, False, False, False, False)

        @block.sync
        def _(sp):
            sp.dma_start(wqk_sb[:], w_qk.rearrange("(c p) n -> p c n", p=P)).then_inc(consts_loaded, 16)
            sp.dma_start(wg_sb[:], w_gate.rearrange("(c p) n -> p c n", p=P)).then_inc(consts_loaded, 16)
            sp.dma_start(slope_sb[:], slope.rearrange("(a n) -> a n", a=1).to_broadcast([P, 1])
                         ).then_inc(consts_loaded, 16)
            sp.dma_start(mask_u8[:], mask).then_inc(consts_loaded, 16)
            for i, w in enumerate((w_v, wq, wk, wv, wfc)):
                sp.dma_start(w_raw[:, i], w.rearrange("(c p) n -> p c n", p=P)).then_inc(consts_loaded, 16)

            def load(b, p):
                sp.dma_start(x_in[:, p], x[b].rearrange("(t p) d -> p t d", p=P)).then_inc(x_loaded[p], 16)
                sp.dma_start(ctx_in[:, p], ctx[b].rearrange("(t p) d -> p t d", p=P)).then_inc(ctx_loaded[p], 16)

            load(0, 0)
            load(1, 1)

            def load_pieces(k, p):
                for i in range(CHUNKS):
                    q = p * CHUNKS + i
                    if q < GU_CHUNKS:
                        src = w_gu[bass.ds(k, 1), q // 2 * P:(q // 2 + 1) * P, q % 2 * CHUNK:(q % 2 + 1) * CHUNK
                                   ].rearrange("e p n -> p (e n)")
                        sp.dma_start(w_piece[:, i], src).then_inc(piece_in, 16)
                    else:
                        r = (q - GU_CHUNKS) * 4
                        src = w_down[bass.ds(k, 1), r * P:(r + 4) * P].rearrange("e (c p) n -> p (e c) n", p=P)
                        sp.dma_start(w_piece[:, i].rearrange("p (c n) -> p c n", c=4), src).then_inc(piece_in, 16)

            def store_pieces(b, k, p):
                if isinstance(b, int) and b == 0:
                    return
                sp.wait_ge(piece_split, CHUNKS * b)
                for i in range(CHUNKS):
                    q = p * CHUNKS + i
                    if q < GU_CHUNKS:
                        to = gu_split[bass.ds(k, 1), :, :, q * CHUNK:(q + 1) * CHUNK]
                    else:
                        to = down_split[bass.ds(k, 1), :, :, (q - GU_CHUNKS) * CHUNK:(q - GU_CHUNKS + 1) * CHUNK]
                    sp.dma_start(to.rearrange("e p a n -> p (e a) n"), w_halves[:, i]).then_inc(piece_out, 16)

            sp.wait_ge(vec_const, 1)
            for p in range(2):
                for r in range(2):
                    sp.dma_start(q_stack[64 * r + 48:64 * r + 49, p], row_const[:, 0]).then_inc(rows_set, 16)
                    sp.dma_start(k_stack[64 * r + 49:64 * r + 50, p, r], row_const[:, 1]).then_inc(rows_set, 16)
            sp.wait_ge(vec_const, 2)
            for j in range(HJ):
                sp.dma_start(mask_rows[:, j], mask_h[:]).then_inc(rows_set, 16)
            for t in range(NT):
                sp.dma_start(routed[DUMMY + t * P:DUMMY + (t + 1) * P], zero_rows[:]).then_inc(dummied, 16)
            sp.wait_ge(rows_set, 16 * ROW_SETS)

            def stack_rows(n, p):
                if not isinstance(n, int) or n >= 2:
                    sp.wait_ge(st_ps, 16 * n - 16)
                for r in range(2):
                    o = 64 * r
                    sp.dma_start(q_stack[o + 49:o + 50, p], row_const[:, 2]).then_inc(stacked[p], 16)
                    sp.dma_start(k_stack[o + 48:o + 49, p, r], mask_rows[n]).then_inc(stacked[p], 16)

            def stack_k(n, p):
                sp.wait_ge(khi_sb, n + 1)
                for r in range(2):
                    o = 64 * r
                    sp.dma_start(k_stack[o:o + 16, p, r], k_hi[:, r]).then_inc(stacked[p], 16)
                    sp.dma_start(k_stack[o + 16:o + 32, p, r], k_hi[:, r]).then_inc(stacked[p], 16)
                sp.wait_ge(klo_sb, n + 1)
                for r in range(2):
                    o = 64 * r
                    sp.dma_start(k_stack[o + 32:o + 48, p, r], k_lo[:, r]).then_inc(stacked[p], 16)

            def stack_q_hi(n, p):
                sp.wait_ge(qhi_sb, n + 1)
                for r in range(2):
                    o = 64 * r
                    sp.dma_start(q_stack[o:o + 16, p], q_hi[:, r]).then_inc(stacked[p], 16)
                    sp.dma_start(q_stack[o + 32:o + 48, p], q_hi[:, r]).then_inc(stacked[p], 16)

            def stack_q_lo(n, p):
                sp.wait_ge(qlo_sb, n + 1)
                for r in range(2):
                    o = 64 * r
                    sp.dma_start(q_stack[o + 16:o + 32, p], q_lo[:, r]).then_inc(stacked[p], 16)

            def load_next(n, p):
                if not isinstance(n, int) or n >= 2:
                    sp.wait_ge(x1_sb, n - 1)
                    sp.wait_ge(ctxt_sb, n - 1)
                    load(n, p)

            def iteration(b, p, h, c, t, s, f, n):
                if n:
                    load_next(b + 3, 1 - p)
                if t:
                    store_pieces(b, h - 1 + p, 1 - p)
                    load_pieces(h, p)
                if f:
                    stack_rows(b + 2, p)
                    stack_k(b + 2, p)
                    stack_q_hi(b + 2, p)
                    stack_q_lo(b + 2, p)

            attention_loop(sp, iteration)
            store_pieces(B, E - 1, 1)

            sp.wait_ge(table_sb, 1)
            sp.wait_ge(padded, 16 * E * NT)
            sp.wait_ge(dummied, 16 * NT)
            sp.wait_ge(piece_out, 16 * CHUNKS * B)
            for p in range(2):
                sp.wait_ge(scattered[p], 64 * (B // 2))

            def load_slot(s, p):
                row = sp.value_load(slot_tab[0:1, 0, bass.ds(s, 1)], min_val=0, max_val=DUMMY)
                e = sp.value_load(slot_tab[0:1, 1, bass.ds(s, 1)], min_val=0, max_val=E - 1)
                sp.dma_start(rows[:, p], routed[bass.ds(row, SLOT)].rearrange("(t p) d -> p t d", p=P)
                             ).then_inc(rows_in[p], 16)
                sp.dma_start(wgu_sb[:, p], gu_split[bass.ds(e, 1)].rearrange("e p a n -> p (e a) n")
                             ).then_inc(w_in[p], 16)
                sp.dma_start(wd_sb[:, p], down_split[bass.ds(e, 1)].rearrange("e p a n -> p (e a) n")
                             ).then_inc(w_in[p], 16)

            def store_slot(s, p):
                sp.wait_ge(y0_sb, s + 1)
                sp.wait_ge(y1_sb, s + 1)
                sp.dma_start(expert_out[bass.ds(s * SLOT, SLOT)].rearrange("(t p) d -> p t d", p=P), y_sb[:, p]
                             ).then_inc(y_out[p], 16)

            load_slot(0, 0)
            load_slot(1, 1)

            def slot(s, p, h, fetch):
                store_slot(s, p)
                sp.wait_ge(y_out[p], 16 * h + 16)
                if fetch:
                    load_slot(s + 2, p)

            with sp.Fori(0, (NSLOT - 3) // 2) as i:
                slot(2 * i, 0, i, True)
                slot(2 * i + 1, 1, i, True)
            slot(NSLOT - 3, 0, (NSLOT - 3) // 2, True)
            slot(NSLOT - 2, 1, (NSLOT - 3) // 2, False)
            slot(NSLOT - 1, 0, (NSLOT - 1) // 2, False)

            def store_out(b, p):
                sp.wait_ge(out_ready, b + 1)
                sp.dma_start(out[b].rearrange("(t p) d -> p t d", p=P), out_sb[:, p]).then_inc(out_done[p], 16)

            with sp.Fori(0, B // 2) as i:
                for p in range(2):
                    store_out(2 * i + p, p)
            for p in range(2):
                sp.wait_ge(out_done[p], 16 * (B // 2))

        @block.gpsimd
        def _(pool):
            pool.sem_inc(xn3_free, 2)
            nc.gpsimd.memset(ident[:], 0.0).then_inc(pool_const, 1)
            nc.gpsimd.memset(tri[:], 1.0).then_inc(pool_const, 1)
            nc.gpsimd.memset(half_neg[:], -0.5).then_inc(pool_const, 1)
            nc.gpsimd.iota(iota_e[:], pattern=[[1, E]], base=0, channel_multiplier=0,
                           allow_small_or_imprecise_dtypes=True).then_inc(pool_const, 1)
            nc.gpsimd.iota(region0[:], pattern=[[REGION, E]], base=0, channel_multiplier=0,
                           allow_small_or_imprecise_dtypes=True).then_inc(pool_const, 1)
            nc.gpsimd.iota(pad_iota[:], pattern=[[0, E], [P, NT]], base=0, channel_multiplier=1,
                           allow_small_or_imprecise_dtypes=True).then_inc(pool_const, 1)
            nc.gpsimd.iota(slot_id[:], pattern=[[1, NSLOT]], base=0, channel_multiplier=0,
                           allow_small_or_imprecise_dtypes=True).then_inc(pool_const, 1)
            nc.gpsimd.iota(alibi[:, 0:P], pattern=[[1, P]], base=0, channel_multiplier=-1,
                           allow_small_or_imprecise_dtypes=True).then_inc(pool_const, 1)
            nc.gpsimd.iota(alibi[:, P:P + S], pattern=[[1, S]], base=-P, channel_multiplier=-1,
                           allow_small_or_imprecise_dtypes=True).then_inc(pool_const, 1)
            pool.wait_ge(pool_const, 9)
            nc.gpsimd.affine_select(out=ident[:], in_=ident[:], compare_op=ALU.not_equal, fill=1.0, base=0,
                                    pattern=[[-1, P]], channel_multiplier=1).then_inc(pool_const, 1)
            nc.gpsimd.affine_select(out=tri[:], in_=tri[:], compare_op=ALU.is_gt, fill=0.0, base=0,
                                    pattern=[[1, P]], channel_multiplier=-1).then_inc(pool_const, 1)
            pool.wait_ge(vec_const, 3)
            nc.gpsimd.affine_select(out=alibi[:, 0:P], in_=alibi[:, 0:P], compare_op=ALU.is_ge, fill=NEG, base=0,
                                    pattern=[[-1, P]], channel_multiplier=1).then_inc(pool_const, 1)
            nc.gpsimd.affine_select(out=alibi[:, P:P + S], in_=alibi[:, P:P + S], compare_op=ALU.is_ge, fill=NEG,
                                    base=P, pattern=[[-1, S]], channel_multiplier=1).then_inc(pool_const, 1)

            def rsqrt_front(m):
                pool.wait_ge(ln_var, m)
                nc.gpsimd.tensor_tensor(rstd[:], var_eps[:], half_neg[:], ALU.pow).then_inc(ln_rstd, 1)

            def rsqrt_tail(c):
                pool.wait_ge(ln3_var, c + 1)
                nc.gpsimd.tensor_tensor(rstd3[:], var_eps3[:], half_neg[:], ALU.pow).then_inc(ln3_rstd, 1)

            def scatter(c, p, u):
                pool.wait_ge(pos_sb, c + 1)
                pool.sem_inc(pool_passed, 1)
                for t in range(NT):
                    for k in range(TOPK):
                        nc.gpsimd.indirect_dma_start(
                            out=routed, out_offset=bass.IndirectOffsetOnAxis(
                                ap=pos_i[:, p, t * TOPK + k:t * TOPK + k + 1], axis=0),
                            in_=xn3[:, p, t], in_offset=None).then_inc(scattered[p], 16)
                pool.wait_ge(scattered[p], 64 * u)
                pool.sem_inc(xn3_free, 1)

            def split_lo(k, i):
                pool.wait_ge(piece_hi, CHUNKS * k + i + 1)
                nc.gpsimd.tensor_tensor(w_halves[:, i, 1], w_scaled[:, i], w_halves[:, i, 0], ALU.subtract
                                        ).then_inc(piece_split, 1)

            def iteration(b, p, h, c, t, s, f, n):
                if c:
                    rsqrt_tail(b - 1)
                if f:
                    rsqrt_front(2 * b + 6)
                if t:
                    split_lo(b, 0)
                if n:
                    rsqrt_front(2 * b + 7)
                if t:
                    split_lo(b, 1)
                    split_lo(b, 2)
                if c:
                    scatter(b - 1, 1 - p, h + p)

            rsqrt_front(1)
            attention_loop(pool, iteration)
            pool.wait_ge(pad_sb, 1)
            for k in range(E * NT):
                nc.gpsimd.indirect_dma_start(
                    out=routed, out_offset=bass.IndirectOffsetOnAxis(ap=pad_i[:, k:k + 1], axis=0),
                    in_=zero_rows[:], in_offset=None).then_inc(padded, 16)

            pool.wait_ge(y_out[0], 16 * ((NSLOT + 1) // 2))
            pool.wait_ge(y_out[1], 16 * (NSLOT // 2))

            def gather(b, p):
                pool.wait_ge(idx_sb, b + 1)
                pool.sem_inc(pool_passed, 1)
                for t in range(NT):
                    for k in range(TOPK):
                        nc.gpsimd.indirect_dma_start(
                            out=gathered[:, p, t, k], out_offset=None, in_=expert_out,
                            in_offset=bass.IndirectOffsetOnAxis(
                                ap=gather_i[:, p, t * TOPK + k:t * TOPK + k + 1], axis=0),
                        ).then_inc(rows_got[p], 16)

            with pool.Fori(0, B // 2) as i:
                for p in range(2):
                    gather(2 * i + p, p)

        @block.scalar
        def _(act):
            def copy(to, frm):
                return nc.scalar.activation(to, frm, ACT.Copy)

            def as_chunks(bank_):
                return bank_[:].rearrange("p (c n) -> p c n", c=NC)

            for i in range(5):
                act.wait_ge(w_tps, i + 1)
                if i in (WQ, WK):
                    for c in range(NC):
                        for r in range(2):
                            o = copy(w_t[:, i, c, r * P:(r + 1) * P].rearrange("p (d j) -> p j d", j=HJ),
                                     front[i % 2][:, c * D + r * P:c * D + (r + 1) * P].rearrange(
                                         "p (j d) -> p j d", d=HD))
                    o.then_inc(w_tsb, 1)
                else:
                    copy(w_t[:, i], as_chunks(front[i % 2])).then_inc(w_tsb, 1)
            act.wait_ge(mask_tps, 1)
            nc.scalar.activation(mask_bias[:], tail[:, 0:NT * B].rearrange("p (t b) -> p t b", t=NT), ACT.Copy,
                                 scale=MASK_BIAS).then_inc(w_tsb, 1)

            def f_xnt(n):
                act.wait_ge(xnt_ps, n + 1)
                copy(xn_t[:], as_chunks(front[0])).then_inc(xnt_sb, 1)

            def f_q1(n):
                act.wait_ge(q1_ps, n + 1)
                copy(q1_t[:], as_chunks(front[0])).then_inc(q1_sb, 1)

            def f_v1(n):
                act.wait_ge(v1_ps, n + 1)
                copy(v1[:], as_chunks(front[1])).then_inc(v1_sb, 1)

            def f_probs(n):
                act.wait_ge(nmax1_sb, n + 1)
                nc.scalar.activation(p1[:, 0:P], s1[:, 0:P], ACT.Exp, bias=nmax1[:, 0:1], accum_out=sum1[:, 0:1])
                nc.scalar.activation(p1[:, P:P + S], s1[:, P:P + S], ACT.Exp, bias=nmax1[:, 1:2],
                                     accum_out=sum1[:, 1:2]).then_inc(p1_sb, 1)

            def f_probs_t(n):
                act.wait_ge(p1t_ps, n + 1)
                copy(p1_t[:], front[0][:, 0:3 * P].rearrange("p (b q) -> p b q", b=3)).then_inc(p1t_sb, 1)

            def f_xn2t(n):
                act.wait_ge(xn2t_ps, n + 1)
                copy(xn2_t[:], as_chunks(front[0])).then_inc(xn2t_sb, 1)

            def f_ctxt(n):
                act.wait_ge(ctxt_ps, n + 1)
                copy(ctx_t[:], as_chunks(front[1])).then_inc(ctxt_sb, 1)

            def f_q(n):
                act.wait_ge(q_ps, n + 1)
                nc.scalar.activation(q_hi[:], as_chunks(front[1]), ACT.Copy, scale=HSCALE).then_inc(qhi_sb, 1)

            def f_k(n, q, u):
                act.wait_ge(k_ps, n + 1)
                if not isinstance(n, int) or n > 0:
                    act.wait_ge(stacked[q], 16 * STACK_DMAS * u)
                copy(k_hi[:], as_chunks(front[1])).then_inc(khi_sb, 1)

            def f_v2(n, p):
                act.wait_ge(v2_ps, n + 1)
                if not isinstance(n, int) or n >= 2:
                    act.wait_ge(pv_ps, 8 * n - 8)
                copy(v_aug[:, p, :, :, 0:HD],
                     front[0][:].rearrange("p (t h d) -> p t h d", t=NT, h=H)).then_inc(v2_sb, 1)

            def h_max(s, p):
                act.wait_ge(nmt_ps, s + 1)
                nc.scalar.activation(nmax_t[:], s_ring[0][0:H, 0:S], ACT.Copy, scale=MAX_Q).then_inc(nmt_sb, 1)
                act.wait_ge(nmt_sb, s + 1)
                for r in range(2):
                    nc.scalar.dma_start(q_stack[64 * r + 49:64 * r + 50, p], nmax_t[HJ * r:HJ * (r + 1)]
                                        ).then_inc(max_stacked[p], 16)

            def h_exp(b, g, r):
                act.wait_ge(st_ps, 16 * b + 2 * g + r + 1)
                if r == 0 and (not isinstance(b, int) or b > 0 or g >= 2):
                    act.wait_ge(pv_ps, 8 * b + g - 1)
                act.sem_inc(act_passed, 1)
                nc.scalar.activation(probs_t[:, g % 2, r], t_ring[r][:].rearrange("p (j q) -> p j q", j=2),
                                     ACT.Exp, bias=mask_bias[:, g % 2, bass.ds(b, 1)]).then_inc(exp_sb, 1)

            def t_ont(c):
                act.wait_ge(ont_ps, c + 1)
                copy(o_nt[:], as_chunks(tail)).then_inc(ont_sb, 1)

            def t_xn3t(c):
                act.wait_ge(xn3t_ps, c + 1)
                copy(xn3_t[:], as_chunks(tail)).then_inc(xn3t_sb, 1)

            def t_gate(c):
                act.wait_ge(logits_sb, c + 1)
                nc.scalar.activation(gexp[:], logits[:], ACT.Exp).then_inc(gexp_sb, 1)

            def split_hi(k, i):
                act.wait_ge(piece_in, 16 * CHUNKS * k + 16 * CHUNKS)
                if i == 0 and not (isinstance(k, int) and k == 0):
                    act.wait_ge(piece_split, CHUNKS * k)
                    act.wait_ge(piece_out, 16 * CHUNKS * k)
                nc.scalar.activation(w_halves[:, i, 0], w_piece[:, i], ACT.Copy, scale=WSCALE)
                nc.scalar.activation(w_scaled[:, i], w_piece[:, i], ACT.Copy, scale=WSCALE).then_inc(piece_hi, 1)

            def iteration(b, p, h, c, t, s, f, n):
                if f:
                    f_xnt(b + 2)
                    f_ctxt(b + 2)
                    f_q1(b + 2)
                    f_probs(b + 2)
                    f_k(b + 2, 1 - p, h + p + 1)
                if t:
                    h_exp(b, 0, 0)
                    h_exp(b, 0, 1)
                if c:
                    t_ont(b - 1)
                if t:
                    h_exp(b, 1, 0)
                if f:
                    f_probs_t(b + 2)
                if t:
                    h_exp(b, 1, 1)
                    split_hi(b, 0)
                    h_exp(b, 2, 0)
                    split_hi(b, 1)
                if f:
                    f_v1(b + 2)
                if t:
                    h_exp(b, 2, 1)
                    h_exp(b, 3, 0)
                    h_exp(b, 3, 1)
                    h_exp(b, 4, 0)
                    h_exp(b, 4, 1)
                    h_exp(b, 5, 0)
                    h_exp(b, 5, 1)
                    h_exp(b, 6, 0)
                    h_exp(b, 6, 1)
                if c:
                    t_xn3t(b - 1)
                if f:
                    f_xn2t(b + 2)
                if t:
                    h_exp(b, 7, 0)
                    h_exp(b, 7, 1)
                if c:
                    t_gate(b - 1)
                if f:
                    f_q(b + 2)
                if t:
                    split_hi(b, 2)
                if f:
                    f_v2(b + 2, p)
                if s:
                    h_max(b + 1, 1 - p)

            attention_loop(act, iteration)

            def rows_round(s, p):
                act.wait_ge(rt_ps, s + 1)
                nc.scalar.activation(rows_hi[:, p], as_chunks(tail), ACT.Copy, scale=RSCALE).then_inc(rhi_sb, 1)

            def act_round(s, f):
                act.wait_ge(act_sb, FC * s + f + 1)
                if not isinstance(s, int) or s > 0 or f >= 4:
                    act.wait_ge(act_used, FC * s + f - 3)
                copy(act_hi[:, f % 4], act_t[:, f % 2]).then_inc(ahi_sb, 1)

            def slot(s, p, ahead):
                for f in range(FC):
                    act.wait_ge(gu_ps, FC * s + f + 1)
                    if not isinstance(s, int) or s > 0 or f >= 2:
                        act.wait_ge(act_sb, FC * s + f - 1)
                    nc.scalar.activation(silu_g[:, f % 2], gu_ring[f % 4][:, 0:SLOT], ACT.Silu,
                                         scale=1 / (WSCALE * RSCALE)).then_inc(silu_sb, 1)
                    if ahead and f == 5:
                        rows_round(s + 1, 1 - p)
                    if f >= 1:
                        act_round(s, f - 1)
                act_round(s, FC - 1)
                act.wait_ge(down_ps, s + 1)
                nc.scalar.activation(y_sb[:, p, 0], front[0][:, 0:D], ACT.Copy, scale=1 / (WSCALE * ASCALE)
                                     ).then_inc(y0_sb, 1)

            rows_round(0, 0)
            slot(0, 0, True)
            with act.Fori(0, (NSLOT - 3) // 2) as i:
                slot(2 * i + 1, 1, True)
                slot(2 * i + 2, 0, True)
            slot(NSLOT - 2, 1, True)
            slot(NSLOT - 1, 0, False)

        @block.vector
        def _(vec):
            nc.vector.memset(row_const[:, 0], MASK_Q)
            nc.vector.memset(row_const[:, 1], MAX_K)
            nc.vector.memset(row_const[:, 2], 0.0)
            nc.vector.memset(zero_rows[:], 0.0)
            nc.vector.memset(ones[:], 1.0)
            nc.vector.memset(one_e[:], 1.0)
            nc.vector.memset(q_stack[:], 0.0)
            nc.vector.memset(k_stack[:], 0.0)
            nc.vector.memset(v_aug[:], 0.0).then_inc(slot_step, 1)
            vec.wait_ge(slot_step, 1)
            nc.vector.memset(v_aug[:, :, :, :, HD:HD + 1], 1.0).then_inc(vec_const, 1)
            vec.wait_ge(consts_loaded, 16 * CONST_LOADS)
            nc.vector.tensor_copy(mask_f[:], mask_u8[:])
            nc.vector.tensor_scalar(mask_h[:], mask_u8[:], MASK_K, None, ALU.mult).then_inc(vec_const, 1)
            vec.wait_ge(pool_const, 11)
            nc.vector.tensor_copy(next_row[:], region0[:])
            nc.vector.tensor_scalar(alibi[:], alibi[:], slope_sb[:, 0:1], None, ALU.mult).then_inc(vec_const, 1)

            def moments_of(src, k, st, mo, ve, step, var):
                vec.sem_inc(vec_passed, 1)
                for t in range(NT):
                    o = nc.vector.bn_stats(st[:, t], src[:, t])
                o.then_inc(step, 1)
                vec.wait_ge(step, LN_STEPS * k + 1)
                vec.sem_inc(vec_passed, 1)
                for t in range(NT):
                    o = nc.vector.bn_aggr(mo[:, t], st[:, t])
                o.then_inc(step, 1)
                vec.wait_ge(step, LN_STEPS * k + 2)
                nc.vector.tensor_scalar(ve[:], mo[:, :, 1], EPS_LN, None, ALU.add).then_inc(var, 1)

            def normalise(src, dst, k, mo, rs, rst, done):
                vec.wait_ge(rst, k + 1)
                for t in range(NT):
                    o = nc.vector.tensor_scalar(dst[:, t], src[:, t], mo[:, t, 0:1], rs[:, t:t + 1],
                                                ALU.subtract, ALU.mult)
                o.then_inc(done, 1)

            def residual(m):
                return x_res[:, bass.ds(m * NT, NT)]

            def f_moments1(n, p, u):
                vec.wait_ge(x_loaded[p], 16 * u + 16)
                moments_of(x_in[:, p], 2 * n, stats, moments, var_eps, ln_step, ln_var)

            def f_norm1(n, p):
                normalise(x_in[:, p], xn, 2 * n, moments, rstd, ln_rstd, ln1_done)

            def f_scores(n):
                vec.wait_ge(sc_ps, n + 1)
                nc.vector.scalar_tensor_tensor(s1[:], front[0][:, 0:P + S], SCALE, alibi[:], ALU.mult, ALU.add
                                               ).then_inc(s1_step, 1)
                vec.wait_ge(s1_step, n + 1)
                nc.vector.tensor_reduce(nmax1[:, 0:1], s1[:, 0:P], AX.X, ALU.max, negate=True)
                nc.vector.tensor_reduce(nmax1[:, 1:2], s1[:, P:P + S], AX.X, ALU.max, negate=True
                                        ).then_inc(nmax1_sb, 1)

            def f_sums(n):
                vec.wait_ge(p1_sb, n + 1)
                nc.vector.reciprocal(rsum1[:], sum1[:]).then_inc(rsum1_sb, 1)

            def f_attn(n, p):
                vec.wait_ge(at_ps, n + 1)
                vec.wait_ge(rsum1_sb, n + 1)
                for t in range(NT):
                    o = nc.vector.scalar_tensor_tensor(
                        x_res[:, bass.ds(n * NT + t, 1)].rearrange("p a d -> p (a d)"),
                        front[1][:, t * D:(t + 1) * D], rsum1[:, t:t + 1], x_in[:, p, t], ALU.mult, ALU.add)
                o.then_inc(x1_sb, 1)
                vec.wait_ge(x1_sb, n + 1)
                moments_of(residual(n), 2 * n + 1, stats, moments, var_eps, ln_step, ln_var)

            def f_norm2(n):
                normalise(residual(n), xn2, 2 * n + 1, moments, rstd, ln_rstd, ln2_done)

            def f_q(n):
                vec.wait_ge(qhi_sb, n + 1)
                nc.vector.scalar_tensor_tensor(q_lo[:], front[1][:].rearrange("p (c n) -> p c n", c=NC), HSCALE,
                                               q_hi[:], ALU.mult, ALU.subtract).then_inc(qlo_sb, 1)

            def f_k(n):
                vec.wait_ge(khi_sb, n + 1)
                nc.vector.tensor_tensor(k_lo[:], front[1][:].rearrange("p (c n) -> p c n", c=NC), k_hi[:],
                                        ALU.subtract).then_inc(klo_sb, 1)

            def h_max(s, n0, n1):
                for n in range(n0, n1):
                    vec.wait_ge(s_ps, 16 * s + n + 1)
                    nc.vector.tensor_reduce(nmax[:, n // HJ, :, n % HJ],
                                            s_ring[n % 2][:].rearrange("p (r k) -> p r k", r=2),
                                            AX.X, ALU.max, negate=True).then_inc(smax, 1)

            def h_out(b, p, jp):
                vec.wait_ge(pv_ps, 8 * b + 2 * jp + 2)
                nc.vector.tensor_copy(o_t[:, p, jp], pv[:, 0:S]).then_inc(o_sb, 1)

            def t_norm(c):
                outs = [bank_[:].rearrange("p (j c w) -> p j c w", j=HJ // 2, w=32) for bank_ in (tail, s_ring[1])]
                for qt in range(NT):
                    vec.wait_ge(oq_ps, 2 * c + qt + 1)
                    nc.vector.reciprocal(rden[:, qt], outs[qt][:, :, :, HD]).then_inc(on_step, 1)
                for qt in range(NT):
                    vec.wait_ge(on_step, 2 * c + qt + 1)
                    for r in range(2):
                        m = nc.vector.tensor_tensor(
                            o_n[:, qt, r * P:(r + 1) * P].rearrange("p (j c d) -> p j c d", c=2, d=HD),
                            outs[qt][:, :, 2 * r:2 * r + 2, 0:HD],
                            rden[:, qt, :, 2 * r:2 * r + 2].unsqueeze(3).to_broadcast([P, HJ // 2, 2, HD]), ALU.mult)
                    m.then_inc(on_sb, 1)

            def t_stream(c):
                vec.wait_ge(fc_ps, c + 1)
                nc.vector.tensor_tensor(residual(c), tail[:].rearrange("p (t d) -> p t d", t=NT), residual(c), ALU.add
                                        ).then_inc(x2_sb, 1)
                vec.wait_ge(x2_sb, c + 1)
                moments_of(residual(c), c, stats3, moments3, var_eps3, ln3_step, ln3_var)

            def t_norm3(c, p):
                vec.wait_ge(xn3_free, c + 1)
                normalise(residual(c), xn3[:, p], c, moments3, rstd3, ln3_rstd, ln3_done)

            def t_logits(c):
                at = GATE_STEPS * c
                vec.wait_ge(gate_ps, c + 1)
                lg = tail[:, 0:NT * E].rearrange("p (t e) -> p t e", t=NT)
                nc.vector.tensor_reduce(lmax[:], lg, AX.X, ALU.max).then_inc(gate_step, 1)
                vec.wait_ge(gate_step, at + 1)
                nc.vector.tensor_tensor(logits[:], lg, lmax[:].unsqueeze(2).to_broadcast([P, NT, E]), ALU.subtract
                                        ).then_inc(logits_sb, 1)

            def t_choose(c):
                at = GATE_STEPS * c
                vec.wait_ge(gexp_sb, c + 1)
                nc.vector.tensor_reduce(gsum[:], gexp[:], AX.X, ALU.add).then_inc(gate_step, 1)
                vec.wait_ge(gate_step, at + 2)
                nc.vector.reciprocal(grec[:], gsum[:]).then_inc(gate_step, 1)
                vec.wait_ge(gate_step, at + 3)
                nc.vector.tensor_tensor(gprob[:], gexp[:], grec[:].unsqueeze(2).to_broadcast([P, NT, E]), ALU.mult
                                        ).then_inc(gate_step, 1)
                vec.wait_ge(gate_step, at + 4)
                vec.sem_inc(vec_passed, 1)
                for t in range(NT):
                    nc.vector.max(top_v[:, t], gprob[:, t]).then_inc(gate_step, 1)
                vec.wait_ge(gate_step, at + 6)
                vec.sem_inc(vec_passed, 1)
                for t in range(NT):
                    nc.vector.max_index(top_i[:, t], top_v[:, t], gprob[:, t]).then_inc(gate_step, 1)
                nc.vector.tensor_tensor(gden[:], top_v[:, :, 0], top_v[:, :, 1], ALU.add).then_inc(gate_step, 1)
                vec.wait_ge(gate_step, at + 9)
                nc.vector.tensor_copy(top_f[:], top_i[:, :, 0:TOPK]).then_inc(gate_step, 1)
                nc.vector.tensor_scalar(gden1[:], gden[:], EPS_GATE, None, ALU.max).then_inc(gate_step, 1)
                vec.wait_ge(gate_step, at + 11)
                nc.vector.tensor_tensor(
                    onehot[:].rearrange("p t k e -> p (t k) e"),
                    iota_e[:].unsqueeze(1).to_broadcast([P, NT * TOPK, E]),
                    top_f[:].rearrange("p t k -> p (t k)").unsqueeze(2).to_broadcast([P, NT * TOPK, E]),
                    ALU.is_equal).then_inc(gate_step, 1)
                nc.vector.reciprocal(gdenr[:], gden1[:]).then_inc(gate_step, 1)
                vec.wait_ge(gate_step, at + 13)
                nc.vector.tensor_tensor(chosen[:], onehot[:, :, 0], onehot[:, :, 1], ALU.add).then_inc(chosen_sb, 1)
                nc.vector.tensor_tensor(gate_all[:, bass.ds(c * NT, NT)], top_v[:, :, 0:TOPK],
                                        gdenr[:].unsqueeze(2).to_broadcast([P, NT, TOPK]), ALU.mult)
                nc.vector.tensor_copy(onehot_all[:, bass.ds(c * NT * TOPK, NT * TOPK)],
                                      onehot[:].rearrange("p t k e -> p (t k) e")).then_inc(gate_step, 1)

            def t_place(c, p):
                at = GATE_STEPS * c
                vec.wait_ge(rank_ps, c + 1)
                nc.vector.tensor_tensor(rank[:], tail[:, 0:NT * E].rearrange("p (t e) -> p t e", t=NT),
                                        next_row[:].unsqueeze(1).to_broadcast([P, NT, E]), ALU.add
                                        ).then_inc(gate_step, 1)
                vec.wait_ge(gate_step, at + 15)
                for t in range(NT):
                    o = nc.vector.tensor_tensor(onehot_pos[:, t], onehot[:, t],
                                                rank[:, t].unsqueeze(1).to_broadcast([P, TOPK, E]), ALU.mult)
                o.then_inc(gate_step, 1)
                nc.vector.tensor_tensor(next_row[:], next_row[:], tail[:, NT * E:(NT + 1) * E], ALU.add
                                        ).then_inc(rank_sb, 1)
                vec.wait_ge(gate_step, at + 16)
                nc.vector.tensor_reduce(pos_f[:], onehot_pos[:].rearrange("p t k e -> p (t k) e"), AX.X, ALU.add
                                        ).then_inc(gate_step, 1)
                vec.wait_ge(gate_step, at + 17)
                nc.vector.tensor_copy(pos_all[:, bass.ds(c * NT * TOPK, NT * TOPK)], pos_f[:])
                nc.vector.tensor_copy(pos_i[:, p], pos_f[:]).then_inc(pos_sb, 1)

            def iteration(b, p, h, c, t, s, f, n):
                if c:
                    t_norm(b - 1)
                if f:
                    f_scores(b + 2)
                if s:
                    h_max(b + 1, 0, 6)
                if f:
                    f_k(b + 2)
                if s:
                    h_max(b + 1, 6, 7)
                if f:
                    f_sums(b + 2)
                if c:
                    t_stream(b - 1)
                if s:
                    h_max(b + 1, 7, 9)
                if t:
                    h_out(b, p, 0)
                if c:
                    t_norm3(b - 1, 1 - p)
                if s:
                    h_max(b + 1, 9, 10)
                if f:
                    f_attn(b + 2, p)
                if t:
                    h_out(b, p, 1)
                if s:
                    h_max(b + 1, 10, 11)
                if f:
                    f_norm2(b + 2)
                if s:
                    h_max(b + 1, 11, 13)
                if t:
                    h_out(b, p, 2)
                if s:
                    h_max(b + 1, 13, 14)
                if n:
                    f_moments1(b + 3, 1 - p, h + 1 + p)
                if c:
                    t_logits(b - 1)
                if s:
                    h_max(b + 1, 14, 15)
                if c:
                    t_choose(b - 1)
                if s:
                    h_max(b + 1, 15, 16)
                if n:
                    f_norm1(b + 3, 1 - p)
                if f:
                    f_q(b + 2)
                if t:
                    h_out(b, p, 3)
                if c:
                    t_place(b - 1, 1 - p)

            vec.wait_ge(pool_const, 13)
            f_moments1(0, 0, 0)
            f_norm1(0, 0)
            attention_loop(vec, iteration)

            step = [1]

            def then(ins):
                step[0] += 1
                ins.then_inc(slot_step, 1)
                vec.wait_ge(slot_step, step[0])

            vec.wait_ge(rank_sb, B)
            then(nc.vector.tensor_tensor(pad_f[:], pad_iota[:], next_row[:].unsqueeze(2).to_broadcast([P, E, NT]),
                                         ALU.add))
            nc.vector.tensor_copy(pad_i[:], pad_f[:].rearrange("p e t -> p (e t)")).then_inc(pad_sb, 1)
            then(nc.vector.tensor_tensor(count[:], next_row[:], region0[:], ALU.subtract))
            then(nc.vector.tensor_scalar(count[:], count[:], float(SLOT - 1), None, ALU.add))
            then(nc.vector.tensor_copy(count_i[:], count[:]))
            then(nc.vector.tensor_scalar(slots_i[:], count_i[:], SLOT.bit_length() - 1, None,
                                         ALU.arith_shift_right))
            then(nc.vector.tensor_copy(slots_f[:], slots_i[:]))
            then(nc.vector.tensor_tensor_scan(slot_end[:], one_e[:], slots_f[:], 0.0, ALU.mult, ALU.add))
            then(nc.vector.tensor_scalar(jump[:], slots_f[0:1], -float(SLOT), float(REGION), ALU.mult, ALU.add))
            then(nc.vector.tensor_tensor(past[:], slot_end[0:1].unsqueeze(1).to_broadcast([1, NSLOT, E]),
                                         slot_id[:].unsqueeze(2).to_broadcast([1, NSLOT, E]), ALU.is_le))
            then(nc.vector.tensor_tensor(past_jump[:], past[:], jump[:].unsqueeze(1).to_broadcast([1, NSLOT, E]),
                                         ALU.mult))
            then(nc.vector.tensor_reduce(slot_e[:], past[:], AX.X, ALU.add))
            then(nc.vector.tensor_reduce(slot_r[:], past_jump[:], AX.X, ALU.add))
            then(nc.vector.scalar_tensor_tensor(slot_r1[:], slot_id[:], float(SLOT), slot_r[:], ALU.mult, ALU.add))
            then(nc.vector.tensor_scalar(slot_tab[:, 0], slot_r1[:], float(DUMMY), None, ALU.min))
            nc.vector.tensor_scalar(slot_tab[:, 1], slot_e[:], float(E - 1), None, ALU.min).then_inc(table_sb, 1)
            then(nc.vector.tensor_tensor(moved[:], slot_end[:], slots_f[:], ALU.subtract))
            then(nc.vector.scalar_tensor_tensor(moved[:], moved[:], float(SLOT), region0[:], ALU.mult, ALU.subtract))
            then(nc.vector.tensor_tensor(onehot_moved[:], onehot_all[:],
                                         moved[:].unsqueeze(1).to_broadcast([P, B * NT * TOPK, E]), ALU.mult))
            then(nc.vector.tensor_reduce(pos_moved[:], onehot_moved[:], AX.X, ALU.add))
            then(nc.vector.tensor_tensor(gather_all[:], pos_moved[:], pos_all[:], ALU.add))

            def rows_rest(s, p):
                vec.wait_ge(rhi_sb, s + 1)
                nc.vector.scalar_tensor_tensor(rows_lo[:, p], tail[:].rearrange("p (c n) -> p c n", c=NC), RSCALE,
                                               rows_hi[:, p], ALU.mult, ALU.subtract).then_inc(rlo_sb, 1)

            def act_rest(s, f):
                vec.wait_ge(ahi_sb, FC * s + f + 1)
                nc.vector.tensor_tensor(act_lo[:, f % 4], act_t[:, f % 2], act_hi[:, f % 4], ALU.subtract
                                        ).then_inc(alo_sb, 1)

            def slot(s, p, ahead):
                for f in range(FC):
                    vec.wait_ge(silu_sb, FC * s + f + 1)
                    if not isinstance(s, int) or s > 0 or f >= 2:
                        vec.wait_ge(alo_sb, FC * s + f - 1)
                    nc.vector.scalar_tensor_tensor(act_t[:, f % 2], gu_ring[f % 4][:, SLOT:2 * SLOT],
                                                   ASCALE / (WSCALE * RSCALE), silu_g[:, f % 2], ALU.mult, ALU.mult
                                                   ).then_inc(act_sb, 1)
                    if ahead and f == 5:
                        rows_rest(s + 1, 1 - p)
                    if f >= 1:
                        act_rest(s, f - 1)
                act_rest(s, FC - 1)
                vec.wait_ge(down_ps, s + 1)
                nc.vector.tensor_scalar(y_sb[:, p, 1], front[1][:, 0:D], 1 / (WSCALE * ASCALE), None, ALU.mult
                                        ).then_inc(y1_sb, 1)

            rows_rest(0, 0)
            slot(0, 0, True)
            with vec.Fori(0, (NSLOT - 3) // 2) as i:
                slot(2 * i + 1, 1, True)
                slot(2 * i + 2, 0, True)
            slot(NSLOT - 2, 1, True)
            slot(NSLOT - 1, 0, False)

            def places(b, p):
                nc.vector.tensor_copy(gather_i[:, p], gather_all[:, bass.ds(b * NT * TOPK, NT * TOPK)]
                                      ).then_inc(idx_sb, 1)

            def combine(b, p, h):
                vec.wait_ge(rows_got[p], 64 * h + 64)
                if not isinstance(b, int) or b >= 2:
                    vec.wait_ge(out_done[p], 16 * h)
                for t in range(NT):
                    o = nc.vector.scalar_tensor_tensor(acc[:, t], gathered[:, p, t, 0],
                                                       gate_all[:, bass.ds(b * NT + t, 1), 0],
                                                       x_res[:, bass.ds(b * NT + t, 1)].rearrange("p a d -> p (a d)"),
                                                       ALU.mult, ALU.add)
                o.then_inc(acc_step, 1)
                vec.wait_ge(acc_step, b + 1)
                for t in range(NT):
                    o = nc.vector.scalar_tensor_tensor(out_sb[:, p, t], gathered[:, p, t, 1],
                                                       gate_all[:, bass.ds(b * NT + t, 1), 1],
                                                       acc[:, t], ALU.mult, ALU.add)
                o.then_inc(out_ready, 1)
                vec.wait_ge(out_ready, b + 1)

            places(0, 0)
            places(1, 1)
            for p in range(2):
                combine(p, p, 0)
                places(p + 2, p)
            with vec.Fori(1, B // 2 - 1) as i:
                for p in range(2):
                    combine(2 * i + p, p, i)
                    places(2 * i + p + 2, p)
            for p in range(2):
                combine(B - 2 + p, p, B // 2 - 1)

        @block.tensor
        def _(pe):
            def transpose(to, frm):
                return nc.tensor.transpose(to, frm, ident[0:frm.shape[0], 0:frm.shape[0]])

            def transpose_tiles(bank_, src):
                for t in range(NT):
                    for c in range(NC):
                        o = transpose(bank_[:, c * S + t * P:c * S + (t + 1) * P], src[:, t, c * P:(c + 1) * P])
                return o

            def project_t(bank_, w, src_t):
                for ob in range(NC):
                    for c in range(NC):
                        o = nc.tensor.matmul(bank_[:, ob * S:(ob + 1) * S], w[:, c, ob * P:(ob + 1) * P],
                                             src_t[:, c], start=(c == 0), stop=(c == NC - 1))
                return o

            def project(bank_, src_t, w):
                for t in range(NT):
                    for c in range(NC):
                        o = nc.tensor.matmul(bank_[:, t * D:(t + 1) * D], src_t[:, c, t * P:(t + 1) * P],
                                             w[:, c], start=(c == 0), stop=(c == NC - 1))
                return o

            pe.wait_ge(pool_const, 11)
            pe.wait_ge(consts_loaded, 16 * CONST_LOADS)
            for i in range(5):
                if i >= 2:
                    pe.wait_ge(w_tsb, i - 1)
                transpose_tiles(front[i % 2], w_raw[:, i]).then_inc(w_tps, 1)
            pe.wait_ge(vec_const, 2)
            for t in range(NT):
                o = transpose(tail[:, t * B:(t + 1) * B], mask_f[:, t * P:(t + 1) * P])
            o.then_inc(mask_tps, 1)
            pe.wait_ge(w_tsb, 6)

            def f_xnt(n):
                pe.wait_ge(ln1_done, n + 1)
                if not isinstance(n, int) or n > 0:
                    pe.wait_ge(v2_sb, n)
                transpose_tiles(front[0], xn).then_inc(xnt_ps, 1)

            def f_ctxt(n, p, u):
                pe.wait_ge(ctx_loaded[p], 16 * u + 16)
                if not isinstance(n, int) or n > 0:
                    pe.wait_ge(qlo_sb, n)
                transpose_tiles(front[1], ctx_in[:, p]).then_inc(ctxt_ps, 1)

            def f_q1(n):
                pe.wait_ge(xnt_sb, n + 1)
                project_t(front[0], wqk_sb, xn_t).then_inc(q1_ps, 1)

            def f_k(n):
                pe.wait_ge(ctxt_sb, n + 1)
                project_t(front[1], w_t[:, WK], ctx_t).then_inc(k_ps, 1)

            def f_scores(n):
                pe.wait_ge(q1_sb, n + 1)
                for q0, k1, to in ((0, P, 0), (P, S, P)):
                    for c in range(NC):
                        o = nc.tensor.matmul(front[0][:, to:to + k1], q1_t[:, c, q0:q0 + P], xn_t[:, c, 0:k1],
                                             start=(c == 0), stop=(c == NC - 1))
                o.then_inc(sc_ps, 1)

            def f_v1(n):
                pe.wait_ge(klo_sb, n + 1)
                project(front[1], xn_t, w_t[:, WV1]).then_inc(v1_ps, 1)

            def f_probs_t(n):
                pe.wait_ge(p1_sb, n + 1)
                for blk in range(3):
                    o = transpose(front[0][:, blk * P:(blk + 1) * P], p1[:, blk * P:(blk + 1) * P])
                o.then_inc(p1t_ps, 1)

            def f_attn(n):
                pe.wait_ge(p1t_sb, n + 1)
                pe.wait_ge(v1_sb, n + 1)
                nc.tensor.matmul(front[1][:, 0:D], p1_t[:, 0], v1[:, 0], start=True, stop=True)
                nc.tensor.matmul(front[1][:, D:2 * D], p1_t[:, 1], v1[:, 0], start=True, stop=False)
                nc.tensor.matmul(front[1][:, D:2 * D], p1_t[:, 2], v1[:, 1], start=False, stop=True
                                 ).then_inc(at_ps, 1)

            def f_xn2t(n):
                pe.wait_ge(ln2_done, n + 1)
                transpose_tiles(front[0], xn2).then_inc(xn2t_ps, 1)

            def f_q(n):
                pe.wait_ge(xn2t_sb, n + 1)
                project_t(front[1], w_t[:, WQ], xn2_t).then_inc(q_ps, 1)

            def f_v2(n):
                project(front[0], ctx_t, w_t[:, WV2]).then_inc(v2_ps, 1)

            def h_scores(s, p, u, n0, n1):
                for n in range(n0, n1):
                    qt, j = n // HJ, n % HJ
                    later = not isinstance(s, int)
                    if n == 0:
                        pe.wait_ge(stacked[p], 16 * STACK_DMAS * (u + 1))
                    if n >= 2:
                        pe.wait_ge(smax, 16 * s + n - 1)
                    elif n == 0 and (later or s > 0):
                        pe.wait_ge(nmt_sb, s)
                    elif n == 1 and (later or s > 1):
                        pe.wait_ge(on_sb, 2 * s - 2)
                    for r in range(2):
                        o = nc.tensor.matmul(s_ring[n % 2][:, r * S:(r + 1) * S],
                                             q_stack[:, p, j, qt * P:(qt + 1) * P], k_stack[:, p, r, j],
                                             start=True, stop=True)
                    o.then_inc(s_ps, 1)

            def h_max(s):
                pe.wait_ge(smax, 16 * s + 16)
                for qt in range(NT):
                    o = transpose(s_ring[0][0:H, qt * P:(qt + 1) * P], nmax[:, qt].rearrange("p r j -> p (r j)"))
                o.then_inc(nmt_ps, 1)

            def h_scores_t(b, p, g, r):
                jp, kt = g // 2, g % 2
                if g >= 1:
                    pe.wait_ge(exp_sb, 16 * b + 2 * g + r - 1)
                for jj in range(2):
                    o = nc.tensor.matmul(t_ring[r][:, jj * S:(jj + 1) * S],
                                         k_stack[:, p, r, 2 * jp + jj, kt * P:(kt + 1) * P],
                                         q_stack[:, p, 2 * jp + jj], start=True, stop=True)
                o.then_inc(st_ps, 1)

            def h_values(b, p, g):
                jp, kt = g // 2, g % 2
                pe.wait_ge(exp_sb, 16 * b + 2 * g + 2)
                if g == 0:
                    pe.wait_ge(v2_sb, b + 1)
                if kt == 0 and (not isinstance(b, int) or b > 0 or jp >= 1):
                    pe.wait_ge(o_sb, 4 * b + jp)
                for r in range(2):
                    for jj in range(2):
                        q = 32 * (2 * r + jj)
                        o = nc.tensor.matmul(pv[q:q + 32, 0:S],
                                             v_aug[:, p, kt, HJ * r + 2 * jp + jj],
                                             probs_t[:, g % 2, r, jj], start=(kt == 0), stop=(kt == 1))
                o.then_inc(pv_ps, 1)

            def t_queries(c, p):
                pe.wait_ge(o_sb, 4 * c + 4)
                if not isinstance(c, int) or c > 0:
                    pe.wait_ge(rank_sb, c)
                for qt, bank_ in enumerate((tail, s_ring[1])):
                    for jp in range(HJ // 2):
                        o = transpose(bank_[:, jp * P:(jp + 1) * P], o_t[:, p, jp, qt * P:(qt + 1) * P])
                    o.then_inc(oq_ps, 1)

            def t_ont(c):
                pe.wait_ge(on_sb, 2 * c + 2)
                transpose_tiles(tail, o_n).then_inc(ont_ps, 1)

            def t_fc(c):
                pe.wait_ge(ont_sb, c + 1)
                project(tail, o_nt, w_t[:, WFC]).then_inc(fc_ps, 1)

            def t_xn3t(c, p):
                pe.wait_ge(ln3_done, c + 1)
                transpose_tiles(tail, xn3[:, p]).then_inc(xn3t_ps, 1)

            def t_gate(c):
                pe.wait_ge(xn3t_sb, c + 1)
                for t in range(NT):
                    for k in range(NC):
                        o = nc.tensor.matmul(tail[:, t * E:(t + 1) * E], xn3_t[:, k, t * P:(t + 1) * P], wg_sb[:, k],
                                             start=(k == 0), stop=(k == NC - 1))
                o.then_inc(gate_ps, 1)

            def t_rank(c):
                pe.wait_ge(chosen_sb, c + 1)
                nc.tensor.matmul(tail[:, 0:NT * E], tri[:], chosen[:].rearrange("p t e -> p (t e)"),
                                 start=True, stop=False)
                nc.tensor.matmul(tail[:, E:2 * E], ones[:], chosen[:, 0], start=False, stop=True)
                nc.tensor.matmul(tail[:, NT * E:(NT + 1) * E], ones[:], chosen[:, 0], start=True, stop=False)
                nc.tensor.matmul(tail[:, NT * E:(NT + 1) * E], ones[:], chosen[:, 1], start=False, stop=True
                                 ).then_inc(rank_ps, 1)

            def iteration(b, p, h, c, t, s, f, n):
                q = 1 - p
                if f:
                    f_xnt(b + 2)
                    f_ctxt(b + 2, p, h + 1)
                    f_q1(b + 2)
                if c:
                    t_queries(b - 1, q)
                if f:
                    f_scores(b + 2)
                    f_k(b + 2)
                if s:
                    h_scores(b + 1, q, h + p, 0, 2)
                if t:
                    pe.wait_ge(max_stacked[p], 32 * h + 32)
                    h_scores_t(b, p, 0, 0)
                    h_scores_t(b, p, 0, 1)
                if f:
                    f_probs_t(b + 2)
                if s:
                    h_scores(b + 1, q, h + p, 2, 3)
                if c:
                    t_ont(b - 1)
                if s:
                    h_scores(b + 1, q, h + p, 3, 4)
                if t:
                    h_scores_t(b, p, 1, 0)
                    h_scores_t(b, p, 1, 1)
                if s:
                    h_scores(b + 1, q, h + p, 4, 5)
                if t:
                    h_values(b, p, 0)
                if s:
                    h_scores(b + 1, q, h + p, 5, 6)
                if t:
                    h_scores_t(b, p, 2, 0)
                if s:
                    h_scores(b + 1, q, h + p, 6, 7)
                if c:
                    t_fc(b - 1)
                if s:
                    h_scores(b + 1, q, h + p, 7, 8)
                if f:
                    f_v1(b + 2)
                if s:
                    h_scores(b + 1, q, h + p, 8, 9)
                if t:
                    h_scores_t(b, p, 2, 1)
                    h_values(b, p, 1)
                    h_scores_t(b, p, 3, 0)
                if s:
                    h_scores(b + 1, q, h + p, 9, 10)
                if f:
                    f_attn(b + 2)
                if t:
                    h_scores_t(b, p, 3, 1)
                    h_scores_t(b, p, 4, 0)
                    h_values(b, p, 2)
                if s:
                    h_scores(b + 1, q, h + p, 10, 11)
                if t:
                    h_scores_t(b, p, 4, 1)
                    h_values(b, p, 3)
                    h_scores_t(b, p, 5, 0)
                if c:
                    t_xn3t(b - 1, q)
                if t:
                    h_scores_t(b, p, 5, 1)
                if s:
                    h_scores(b + 1, q, h + p, 11, 12)
                if t:
                    h_values(b, p, 4)
                    h_scores_t(b, p, 6, 0)
                    h_scores_t(b, p, 6, 1)
                if s:
                    h_scores(b + 1, q, h + p, 12, 13)
                if t:
                    h_values(b, p, 5)
                    h_scores_t(b, p, 7, 0)
                if s:
                    h_scores(b + 1, q, h + p, 13, 14)
                if t:
                    h_scores_t(b, p, 7, 1)
                if f:
                    f_xn2t(b + 2)
                if t:
                    h_values(b, p, 6)
                if c:
                    t_gate(b - 1)
                if s:
                    h_scores(b + 1, q, h + p, 14, 15)
                if f:
                    f_q(b + 2)
                if s:
                    h_scores(b + 1, q, h + p, 15, 16)
                if t:
                    h_values(b, p, 7)
                if f:
                    f_v2(b + 2)
                if s:
                    h_max(b + 1)
                if c:
                    t_rank(b - 1)

            attention_loop(pe, iteration)

            def rows_transposed(s, p, h):
                pe.wait_ge(rows_in[p], 16 * h + 16)
                transpose_tiles(tail, rows[:, p]).then_inc(rt_ps, 1)

            HI, LO = 0, 1

            def gate_up(s, p, f):
                if not isinstance(s, int) or s > 0 or f >= 4:
                    pe.wait_ge(act_sb, FC * s + f - 3)
                for half in range(2):
                    products = [(c, w, r) for c in range(NC) for w, r in ((HI, rows_hi), (HI, rows_lo), (LO, rows_hi))]
                    for i, (c, w, r) in enumerate(products):
                        at = c * 2 * F + half * F + f * P
                        o = nc.tensor.matmul(gu_ring[f % 4][:, half * SLOT:(half + 1) * SLOT],
                                             wgu_sb[:, p, w, at:at + P], r[:, p, c],
                                             start=(i == 0), stop=(i == len(products) - 1))
                o.then_inc(gu_ps, 1)

            def down(s, p, f):
                pe.wait_ge(alo_sb, FC * s + f + 1)
                if f == 0 and (not isinstance(s, int) or s > 0):
                    pe.wait_ge(y0_sb, s)
                    pe.wait_ge(y1_sb, s)
                products = ((act_hi, HI), (act_lo, HI), (act_hi, LO))
                for t in range(NT):
                    for i, (a, w) in enumerate(products):
                        o = nc.tensor.matmul(front[t][:, 0:D], a[:, f % 4, t * P:(t + 1) * P],
                                             wd_sb[:, p, w, f * D:(f + 1) * D],
                                             start=(f == 0 and i == 0), stop=(f == FC - 1 and i == len(products) - 1))
                    if t == 0 and f == FC - 1:
                        o.then_inc(act_used, 1)
                o.then_inc(down_ps if f == FC - 1 else act_used, 1)

            def slot(s, p, h, ahead):
                pe.wait_ge(rlo_sb, s + 1)
                pe.wait_ge(w_in[p], 32 * h + 32)
                for f in range(FC):
                    gate_up(s, p, f)
                    if ahead and f == 4:
                        rows_transposed(s + 1, 1 - p, h + p)
                    if f >= 2:
                        down(s, p, f - 2)
                down(s, p, FC - 2)
                down(s, p, FC - 1)

            pe.wait_ge(rank_sb, B)
            rows_transposed(0, 0, 0)
            slot(0, 0, 0, True)
            with pe.Fori(0, (NSLOT - 3) // 2) as i:
                slot(2 * i + 1, 1, i, True)
                slot(2 * i + 2, 0, i + 1, True)
            slot(NSLOT - 2, 1, (NSLOT - 3) // 2, True)
            slot(NSLOT - 1, 0, (NSLOT - 1) // 2, False)


def kernel(x, ctx_1024, mask_BxS2_bf0, L0_attn_W_qk, L0_attn_W_v, L0_attn_alibi_slope, L0_xattn_wq, L0_xattn_wk,
           L0_xattn_wv, L0_xattn_wfc, L0_ffn_w_gate, L0_ffn_w_gate_up, L0_ffn_w_down):
    import concourse.bacc as bacc
    from concourse.bass_utils import run_bass_kernel_spmd

    given = {"x": x, "ctx": ctx_1024, "mask": mask_BxS2_bf0,
             "w_qk": L0_attn_W_qk, "w_v": L0_attn_W_v, "slope": L0_attn_alibi_slope, "wq": L0_xattn_wq,
             "wk": L0_xattn_wk, "wv": L0_xattn_wv, "wfc": L0_xattn_wfc, "w_gate": L0_ffn_w_gate,
             "w_gu": L0_ffn_w_gate_up, "w_down": L0_ffn_w_down}
    given = {k: np.ascontiguousarray(v) for k, v in given.items()}
    nc = bacc.Bacc("TRN2", target_bir_lowering=False, num_devices=1)
    aps = {k: nc.dram_tensor(f"in_{k}", v.shape, mybir.dt.from_np(v.dtype), kind="ExternalInput").ap()
           for k, v in given.items()}
    out = nc.dram_tensor("out", (B, S, D), F32, kind="ExternalOutput").ap()
    decoder_layer(nc, **aps, out=out)
    r = run_bass_kernel_spmd(nc, [{f"in_{k}": v for k, v in given.items()}], core_ids=[0])
    return r.results[0]["out"]
```

```python
from contextlib import ExitStack

import numpy as np
import concourse.bass as bass
from concourse import mybir

F32 = mybir.dt.float32
F16 = mybir.dt.float16
U32 = mybir.dt.uint32
I32 = mybir.dt.int32
U8 = mybir.dt.uint8
ALU = mybir.AluOpType
ACT = mybir.ActivationFunctionType
AX = mybir.AxisListType

B, S, D = 16, 256, 256
P = 128
NT = S // P
NC = D // P
H, HD = 16, 16
HJ = H // 2
E, F, TOPK = 8, 1024, 2
EPS_LN, EPS_GATE = 1e-5, 1e-9
SCALE = float(D) ** -0.5
HSCALE = float(HD) ** -0.5
NEG = -1.0e30
MASK_BIAS = -3.0e38
MASK_Q, MASK_K = 32768.0, -32768.0
MAX_Q, MAX_K = 1.0 / 64, 64.0

SLOT = 256
NSLOT = B * S * TOPK // SLOT + E - 1
REGION = B * S + SLOT
DUMMY = E * REGION
ENTRIES = DUMMY + SLOT
ROW, PLACE, GATE = range(3)
GB = 2
NG = B // GB
POOL_GROUPS = (2, 5)
FC = F // P
WSCALE, RSCALE, ASCALE = 128.0, 32.0, 32.0
PSCALE, XSCALE = 128.0, 32.0
UNSCALE = 1 / (PSCALE * XSCALE)
CHUNK = 1024
CHUNKS = 3
GU_CHUNKS = 2 * F * NC // CHUNK


def decoder_layer(nc, x, ctx, mask, w_qk, w_v, slope, wq, wk, wv, wfc, w_gate, w_gu, w_down, out):
    with ExitStack() as stack:
        def sb(name, shape, dt=F32):
            return stack.enter_context(nc.sbuf_tensor(name, shape, dt))

        attention = ExitStack()

        def ab(name, shape, dt=F32):
            return attention.enter_context(nc.sbuf_tensor(name, shape, dt))

        def bank(name):
            return stack.enter_context(nc.psum_tensor(name, [P, 512], F32))

        def sem(name):
            return stack.enter_context(nc.semaphore(name))

        def sems(name, n=2):
            return [sem(f"{name}{i}") for i in range(n)]

        entries = nc.dram_tensor("entries", [ENTRIES, 3], F32, kind="Internal").ap()
        normed = nc.dram_tensor("normed", [B * S, D], F32, kind="Internal").ap()
        results = nc.dram_tensor("results", [TOPK * B * S + SLOT, D], F32, kind="Internal").ap()
        gu_split = nc.dram_tensor("gu_split", [E, P, 2, NC * 2 * F], F16, kind="Internal").ap()
        down_split = nc.dram_tensor("down_split", [E, P, 2, FC * D], F16, kind="Internal").ap()
        mask_rows = nc.dram_tensor("mask_rows", [B, S], F16, kind="Internal").ap()

        ident = sb("ident", [P, P])
        tri = sb("tri", [P, P], F16)
        ones = sb("ones", [P, P], F16)
        half_neg = sb("half_neg", [P, NT])
        iota_e = sb("iota_e", [P, E])
        ids = sb("ids", [P, 2, B, NT, TOPK])
        slope_sb = sb("slope_sb", [P, 1])
        mask_u8 = sb("mask_u8", [B, S], U8)
        mask_f = sb("mask_f", [B, S])
        mask_h = sb("mask_h", [B, S], F16)
        mask_bias = sb("mask_bias", [P, NT, B])
        wg_sb = sb("wg_sb", [P, NC, E])
        WQK, WK, WV1, WQ, WV2, WFC = range(6)
        HI, LO = 0, 1

        x_res = sb("x_res", [P, B * NT, D])
        stats = sb("stats", [P, NT, 6])
        moments = sb("moments", [P, 2, NT, 2])
        var_eps = sb("var_eps", [P, 2, NT])
        rstd = sb("rstd", [P, 2, NT])
        nmax1 = sb("nmax1", [P, NT])
        sum1 = sb("sum1", [P, NT])
        rsum1 = sb("rsum1", [P, NT])

        nmax = sb("nmax", [P, NT, 2, HJ])
        nmax_t = sb("nmax_t", [H, S], F16)

        rden = sb("rden", [P, NT, HJ // 2, 4])
        stats3 = sb("stats3", [P, NT, 6])
        moments3 = sb("moments3", [P, NT, 2])
        var_eps3 = sb("var_eps3", [P, NT])
        rstd3 = sb("rstd3", [P, NT])
        lmax = sb("lmax", [P, NT])
        logits = sb("logits", [P, NT, E])
        gexp = sb("gexp", [P, NT, E])
        gsum = sb("gsum", [P, NT])
        grec = sb("grec", [P, NT])
        gprob = sb("gprob", [P, NT, E])
        top_v = sb("top_v", [P, NT, 8])
        top_i = sb("top_i", [P, NT, 8], U32)
        top_f = sb("top_f", [P, NT, TOPK])
        gden = sb("gden", [P, NT])
        gden1 = sb("gden1", [P, NT])
        gdenr = sb("gdenr", [P, NT])
        onehot = sb("onehot", [P, NT, TOPK, E])
        chosen = sb("chosen", [P, NT, E], F16)
        rank = sb("rank", [P, NT, E])
        onehot_pos = sb("onehot_pos", [P, NT, TOPK, E])
        pos_f = sb("pos_f", [P, NT * TOPK])
        pos_i = sb("pos_i", [P, 2, NT * TOPK], U32)
        entry = sb("entry", [P, 2, NT * TOPK, 3])
        next_row = sb("next_row", [P, E])

        region0 = sb("region0", [P, E])
        count = sb("count", [P, E])
        count_i = sb("count_i", [P, E], I32)
        slots_i = sb("slots_i", [P, E], I32)
        slots_f = sb("slots_f", [P, E])
        one_e = sb("one_e", [P, E])
        slot_end = sb("slot_end", [P, E])
        jump = sb("jump", [1, E])
        slot_id = sb("slot_id", [1, NSLOT])
        past = sb("past", [1, NSLOT, E])
        past_jump = sb("past_jump", [1, NSLOT, E])
        slot_e = sb("slot_e", [1, NSLOT])
        slot_r = sb("slot_r", [1, NSLOT])
        slot_r1 = sb("slot_r1", [1, NSLOT])
        slot_tab = sb("slot_tab", [1, 3, NSLOT], I32)
        used_slots = sb("used_slots", [1, 1], I32)
        slot_entry = sb("slot_entry", [P, NSLOT * NT, 3])
        row_i = sb("row_i", [P, 2, NT], U32)
        place_i = sb("place_i", [P, 2, NT], U32)
        slot_gate = sb("slot_gate", [P, 2, NT])

        w_piece = ab("w_piece", [P, 2, CHUNKS, CHUNK])
        w_scaled = ab("w_scaled", [P, CHUNKS, CHUNK])
        w_halves = ab("w_halves", [P, CHUNKS, 2, CHUNK], F16)
        w_raw = w_scaled[:].rearrange("p i c -> p (i c)")[:, 0:6 * NC * D].rearrange("p (i c n) -> p i c n", i=6, c=NC)
        Q_ROWS, MASK_ROW, MAX_ROW = 2 * HD, 6 * HD, 6 * HD + 1
        q_stack = ab("q_stack", [P, 2, HJ, S], F16)
        k_stack = ab("k_stack", [P, 2, 2, HJ, S], F16)
        v_aug = ab("v_aug", [P, 2, NT, H, 32])
        probs_t = ab("probs_t", [P, 2, 2, 2, S])
        fill_i = ab("fill_i", [P, ENTRIES // P], I32)
        fill = ab("fill", [P, ENTRIES // P, 3])
        alibi = ab("alibi", [P, P + S])
        row_const = ab("row_const", [H, 3, S], F16)
        w_split = ab("w_split", [P, 6, 2, NC, D], F16)
        xn_h = ab("xn_h", [P, 2, NC, S], F16)
        ctx_h = ab("ctx_h", [P, 2, NC, S], F16)
        xn2_h = ab("xn2_h", [P, 2, NC, S], F16)
        o_nh = ab("o_nh", [P, 2, NC, S], F16)
        x_in = ab("x_in", [P, 2, NT, D])
        ctx_in = ab("ctx_in", [P, 2, NT, D])
        xn = ab("xn", [P, NT, D])
        xn_t = ab("xn_t", [P, NC, S])
        q1_t = ab("q1_t", [P, NC, S])
        v1 = ab("v1", [P, NT, D])
        s1 = ab("s1", [P, P + S])
        p1 = ab("p1", [P, P + S])
        p1_t = ab("p1_t", [P, 3, P])
        xn2 = ab("xn2", [P, NT, D])
        xn2_t = ab("xn2_t", [P, NC, S])
        ctx_t = ab("ctx_t", [P, NC, S])
        q_hi = ab("q_hi", [P, NC, S], F16)
        q_lo = ab("q_lo", [P, NC, S], F16)
        k_hi = ab("k_hi", [P, NC, S], F16)
        k_lo = ab("k_lo", [P, NC, S], F16)
        o_t = ab("o_t", [P, 2, HJ // 2, S])
        o_n = ab("o_n", [P, NT, D])
        o_nt = ab("o_nt", [P, NC, S])
        xn3 = ab("xn3", [P, 2, NT, D])
        xn3_t = ab("xn3_t", [P, NC, S])

        attention.close()
        wgu_sb = sb("wgu_sb", [P, 2, 2, NC * 2 * F], F16)
        wd_sb = sb("wd_sb", [P, 2, 2, FC * D], F16)
        silu_g = sb("silu_g", [P, 2, SLOT])
        act_t = sb("act_t", [P, 2, SLOT])
        act_hi = sb("act_hi", [P, 4, SLOT], F16)
        act_lo = sb("act_lo", [P, 4, SLOT], F16)
        rows = sb("rows", [P, 2, NT, D])
        rows_hi = sb("rows_hi", [P, 2, NC, SLOT], F16)
        rows_lo = sb("rows_lo", [P, 2, NC, SLOT], F16)
        y_sb = sb("y_sb", [P, 2, NT, D])

        pair_in = sb("pair_in", [P, NG, TOPK, GB * NT, D])

        s_ring = [bank(f"s_ring{i}") for i in range(2)]
        t_ring = [bank(f"t_ring{i}") for i in range(2)]
        pv = bank("pv")
        front = [bank(f"front{i}") for i in range(2)]
        tail = bank("tail")
        gu_ring = s_ring + t_ring
        weight_banks = t_ring + s_ring + [pv]
        consts_loaded = sem("consts_loaded")
        raw_loaded = sems("raw_loaded", 6)
        pool_const = sem("pool_const")
        vec_const = sem("vec_const")
        w_tps = sem("w_tps")
        w_hi = sem("w_hi")
        w_lo = sem("w_lo")
        mask_tps = sem("mask_tps")
        rows_set = sem("rows_set")
        x_loaded, ctx_loaded = sems("x_loaded"), sems("ctx_loaded")
        ln1_step, ln1_var, ln1_rstd, ln1_done = map(sem, "ln1_step ln1_var ln1_rstd ln1_done".split())
        ln2_step, ln2_var, ln2_rstd, ln2_done = map(sem, "ln2_step ln2_var ln2_rstd ln2_done".split())
        xnt_ps, xnt_sb, xnt_lo, q1_ps, q1_sb, v1_ps, v1_sb = map(
            sem, "xnt_ps xnt_sb xnt_lo q1_ps q1_sb v1_ps v1_sb".split())
        sc_ps, s1_step, nmax1_sb, p1_sb, rsum1_sb = map(sem, "sc_ps s1_step nmax1_sb p1_sb rsum1_sb".split())
        p1t_ps, p1t_sb, at_ps, x1_sb = map(sem, "p1t_ps p1t_sb at_ps x1_sb".split())
        xn2t_ps, xn2t_sb, xn2t_lo, ctxt_ps, ctxt_sb, ctxt_lo = map(
            sem, "xn2t_ps xn2t_sb xn2t_lo ctxt_ps ctxt_sb ctxt_lo".split())
        q_ps, qhi_sb, qlo_sb, k_ps, khi_sb, klo_sb = map(sem, "q_ps qhi_sb qlo_sb k_ps khi_sb klo_sb".split())
        v2_ps, v2_sb = sem("v2_ps"), sem("v2_sb")
        stacked = sems("stacked")
        STACK_DMAS = 11
        s_ps, smax, nmt_ps, nmt_sb = map(sem, "s_ps smax nmt_ps nmt_sb".split())
        max_stacked = sems("max_stacked")
        st_ps, exp_sb, pv_ps, o_sb = map(sem, "st_ps exp_sb pv_ps o_sb".split())
        oq_ps, on_step, on_sb, ont_ps, ont_sb, ont_lo = map(sem, "oq_ps on_step on_sb ont_ps ont_sb ont_lo".split())
        fc_ps, x2_sb, ln3_step, ln3_var, ln3_rstd, ln3_done = map(
            sem, "fc_ps x2_sb ln3_step ln3_var ln3_rstd ln3_done".split())
        xn3t_ps, xn3t_sb, gate_ps, gate_step, logits_sb, gexp_sb = map(
            sem, "xn3t_ps xn3t_sb gate_ps gate_step logits_sb gexp_sb".split())
        chosen_sb, rank_ps, rank_sb, pos_sb = map(sem, "chosen_sb rank_ps rank_sb pos_sb".split())
        scattered, entry_free, normed_out = sems("scattered"), sem("entry_free"), sems("normed_out")
        piece_in = sems("piece_in")
        piece_hi, piece_split, piece_out = map(sem, "piece_hi piece_split piece_out".split())
        slot_step, table_sb, fill_step = map(sem, "slot_step table_sb fill_step".split())
        entry_in, row_sb, place_sb, y_free = sems("entry_in"), sem("row_sb"), sem("place_sb"), sem("y_free")
        rows_in, w_in, y_out = sems("rows_in"), sems("w_in"), sems("y_out")
        rt_ps, rhi_sb, rlo_sb, gu_ps, silu_sb, act_sb = map(
            sem, "rt_ps rhi_sb rlo_sb gu_ps silu_sb act_sb".split())
        ahi_sb, alo_sb, down_ps, y0_sb, y1_sb, act_used = map(sem, "ahi_sb alo_sb down_ps y0_sb y1_sb act_used".split())
        vec_step, vec_sums, pool_step, pool_sums, out_done = map(
            sem, "vec_step vec_sums pool_step pool_sums out_done".split())
        pair_got = sems("pair_got", NG)

        act_passed, vec_passed, pool_passed = map(sem, "act_passed vec_passed pool_passed".split())

        block = stack.enter_context(nc.Block())

        CONST_LOADS = 3
        ROW_SETS = 2 * 3 + 1
        LN_STEPS = 2
        GATE_STEPS = 17

        def attention_loop(eng, iteration):
            iteration(-2, 0, -1, False, False, False, True, True)
            iteration(-1, 1, -1, False, False, True, True, True)
            iteration(0, 0, 0, False, True, True, True, True)
            with eng.Fori(0, 6) as i:
                iteration(2 * i + 1, 1, i, True, True, True, True, True)
                iteration(2 * i + 2, 0, i + 1, True, True, True, True, True)
            iteration(13, 1, 6, True, True, True, True, False)
            iteration(14, 0, 7, True, True, True, False, False)
            iteration(15, 1, 7, True, True, False, False, False)
            iteration(16, 0, 8, True, False, False, False, False)

        def weight_parts(i, half):
            if i == WQK:
                return [(w_split[:, i, half], w_raw[:, i])]
            bank_ = weight_banks[i - 1]
            if i not in (WQ, WK):
                return [(w_split[:, i, half], bank_[:].rearrange("p (c n) -> p c n", c=NC))]
            parts = []
            for k in range(NC):
                for r in range(2):
                    to = w_split[:, i, half, k].rearrange("p (c r d j) -> p c r d j", c=2, r=2, d=HD)[:, :, r]
                    frm = bank_[:, k * D + r * P:k * D + (r + 1) * P]
                    parts.append((to, frm.rearrange("p (j c d) -> p c d j", c=2, d=HD)))
            return parts

        def combine(ops, eng, groups, step, sums):
            for n, g in enumerate(groups):
                eng.wait_ge(pair_got[g], 16 * TOPK)
                ops.tensor_tensor(pair_in[:, g, 0], pair_in[:, g, 0], x_res[:, g * GB * NT:(g + 1) * GB * NT], ALU.add
                                  ).then_inc(step, 1)
                eng.wait_ge(step, n + 1)
                ops.tensor_tensor(pair_in[:, g, 0], pair_in[:, g, 0], pair_in[:, g, 1], ALU.add).then_inc(sums, 1)

        @block.sync
        def _(sp):
            def load(b, p):
                sp.dma_start(x_in[:, p], x[b].rearrange("(t p) d -> p t d", p=P)).then_inc(x_loaded[p], 16)
                sp.dma_start(ctx_in[:, p], ctx[b].rearrange("(t p) d -> p t d", p=P)).then_inc(ctx_loaded[p], 16)

            load(0, 0)
            for i, w in enumerate((w_qk, wk, w_v, wq, wv, wfc)):
                sp.dma_start(w_raw[:, i], w.rearrange("(c p) n -> p c n", p=P)).then_inc(raw_loaded[i], 16)
            sp.dma_start(mask_u8[:], mask).then_inc(consts_loaded, 16)
            sp.dma_start(slope_sb[:], slope.rearrange("(a n) -> a n", a=1).to_broadcast([P, 1])
                         ).then_inc(consts_loaded, 16)
            sp.dma_start(wg_sb[:], w_gate.rearrange("(c p) n -> p c n", p=P)).then_inc(consts_loaded, 16)
            load(1, 1)

            def store_normed(c, p):
                sp.wait_ge(ln3_done, c + 1)
                sp.dma_start(normed[bass.ds(c * S, S)].rearrange("(t p) d -> p t d", p=P), xn3[:, p]
                             ).then_inc(normed_out[p], 16)

            def load_pieces(b, k, p):
                if not isinstance(b, int) or b >= 2:
                    sp.wait_ge(piece_hi, CHUNKS * (b - 1))
                for i in range(CHUNKS):
                    q = p * CHUNKS + i
                    if q < GU_CHUNKS:
                        src = w_gu[bass.ds(k, 1), q // 2 * P:(q // 2 + 1) * P, q % 2 * CHUNK:(q % 2 + 1) * CHUNK
                                   ].rearrange("e p n -> p (e n)")
                        sp.dma_start(w_piece[:, p, i], src).then_inc(piece_in[p], 16)
                    else:
                        r = (q - GU_CHUNKS) * 4
                        src = w_down[bass.ds(k, 1), r * P:(r + 4) * P].rearrange("e (c p) n -> p (e c) n", p=P)
                        sp.dma_start(w_piece[:, p, i].rearrange("p (c n) -> p c n", c=4), src).then_inc(piece_in[p], 16)

            def store_pieces(b, k, p):
                sp.wait_ge(piece_split, CHUNKS * b + CHUNKS)
                for i in range(CHUNKS):
                    q = p * CHUNKS + i
                    if q < GU_CHUNKS:
                        to = gu_split[bass.ds(k, 1), :, :, q * CHUNK:(q + 1) * CHUNK]
                    else:
                        to = down_split[bass.ds(k, 1), :, :, (q - GU_CHUNKS) * CHUNK:(q - GU_CHUNKS + 1) * CHUNK]
                    sp.dma_start(to.rearrange("e p a n -> p (e a) n"), w_halves[:, i]).then_inc(piece_out, 16)

            sp.wait_ge(vec_const, 1)
            sp.wait_ge(pool_const, 14)
            for p in range(2):
                sp.dma_start(q_stack[MASK_ROW:MASK_ROW + 1, p], row_const[0:HJ, 0]).then_inc(rows_set, 16)
                for r in range(2):
                    sp.dma_start(k_stack[MAX_ROW + r:MAX_ROW + r + 1, p, r], row_const[0:HJ, 1]).then_inc(rows_set, 16)
            sp.wait_ge(vec_const, 2)
            sp.dma_start(mask_rows, mask_h[:]).then_inc(rows_set, 16)
            for p in range(2):
                sp.sem_inc(normed_out[p], 16)
            sp.wait_ge(rows_set, 16 * ROW_SETS)

            def stack_rows(n, p):
                if not isinstance(n, int) or n >= 2:
                    sp.wait_ge(st_ps, 16 * n - 16)
                sp.dma_start(q_stack[MAX_ROW:MAX_ROW + 2, p], row_const[:, 2]).then_inc(stacked[p], 16)
                sp.dma_start(k_stack[MASK_ROW:MASK_ROW + 1, p], mask_rows[bass.ds(n, 1)].to_broadcast([H, S])
                             ).then_inc(stacked[p], 16)

            def k_rows(half, at, p):
                for r in range(2):
                    o = at + HD * r
                    sp.dma_start(k_stack[o:o + HD, p, r], half[64 * r:64 * r + 64].rearrange("p c q -> p (c q)")
                                 ).then_inc(stacked[p], 16)

            def q_rows(half, at, p):
                sp.dma_start(q_stack[at:at + Q_ROWS, p], half[:].rearrange("p c q -> p (c q)")).then_inc(stacked[p], 16)

            def stack_k(n, p):
                sp.wait_ge(khi_sb, n + 1)
                k_rows(k_hi, 0, p)
                k_rows(k_hi, Q_ROWS, p)
                sp.wait_ge(klo_sb, n + 1)
                k_rows(k_lo, 2 * Q_ROWS, p)

            def stack_q_hi(n, p):
                sp.wait_ge(qhi_sb, n + 1)
                q_rows(q_hi, 0, p)
                q_rows(q_hi, 2 * Q_ROWS, p)

            def stack_q_lo(n, p):
                sp.wait_ge(qlo_sb, n + 1)
                q_rows(q_lo, Q_ROWS, p)

            def stack_max(s, p):
                sp.wait_ge(nmt_sb, s + 1)
                sp.dma_start(q_stack[MAX_ROW:MAX_ROW + 2, p], nmax_t[:]).then_inc(max_stacked[p], 16)

            def load_next(n, p):
                if not isinstance(n, int) or n >= 2:
                    sp.wait_ge(x1_sb, n - 1)
                    sp.wait_ge(ctxt_sb, n - 1)
                    load(n, p)

            def load_gate_up(e, p, cond=None):
                sp.dma_start(wgu_sb[:, p], gu_split[bass.ds(e, 1)].rearrange("e p a n -> p (e a) n"), cond=cond
                             ).then_inc(w_in[p], 16)

            def load_down(e, p, cond=None):
                sp.dma_start(wd_sb[:, p], down_split[bass.ds(e, 1)].rearrange("e p a n -> p (e a) n"), cond=cond
                             ).then_inc(w_in[p], 16)

            def first_weights():
                sp.wait_ge(piece_out, 16 * CHUNKS * B)
                load_gate_up(0, 0)
                load_down(0, 0)

            def iteration(b, p, h, c, t, s, f, n):
                if c and not t:
                    first_weights()
                if n:
                    load_next(b + 3, 1 - p)
                if f:
                    load_pieces(b + 2, h + 1, p)
                if c:
                    store_normed(b - 1, 1 - p)
                if f:
                    stack_rows(b + 2, p)
                    stack_k(b + 2, p)
                if s:
                    stack_max(b + 1, 1 - p)
                if f:
                    stack_q_hi(b + 2, p)
                    stack_q_lo(b + 2, p)
                if s:
                    store_pieces(b + 1, h + p, 1 - p)

            attention_loop(sp, iteration)

            def entries_at(s, p, row):
                sp.dma_start(slot_entry[:, bass.ds(s * NT, NT)],
                             entries[bass.ds(row, SLOT)].rearrange("(t p) w -> p t w", p=P)
                             ).then_inc(entry_in[p], 16)

            def first_entry(s):
                return sp.value_load(slot_tab[0:1, 0, bass.ds(s, 1)], min_val=0, max_val=DUMMY)

            def expert(s):
                return sp.value_load(slot_tab[0:1, 1, bass.ds(s, 1)], min_val=0, max_val=E - 1)

            def other(s):
                return sp.value_load(slot_tab[0:1, 2, bass.ds(s, 1)], min_val=0, max_val=1)

            sp.wait_ge(entry_free, B + 2)
            entries_at(0, 0, 0)
            sp.wait_ge(table_sb, 1)
            entries_at(1, 1, first_entry(1))
            e = expert(1)
            sp.wait_ge(rows_in[0], 32)
            load_gate_up(e, 1)
            load_down(e, 1)
            sp.wait_ge(row_sb, 2)
            entries_at(2, 0, first_entry(2))
            entries_at(3, 1, first_entry(3))

            def slot(s, p, ahead):
                e, new = expert(s + 2), other(s + 2)
                if ahead:
                    row = first_entry(s + 4)
                sp.wait_ge(gu_ps, FC * s + FC)
                load_gate_up(e, p, new)
                sp.wait_ge(down_ps, s + 1)
                load_down(e, p, new)
                if ahead:
                    entries_at(s + 4, p, row)

            with sp.Fori(0, (NSLOT - 5) // 2) as i:
                slot(2 * i, 0, True)
                slot(2 * i + 1, 1, True)
            slot(NSLOT - 5, 0, True)
            slot(NSLOT - 4, 1, False)
            slot(NSLOT - 3, 0, False)

            used = sp.value_load(used_slots[0:1, 0:1], min_val=E, max_val=NSLOT)
            sp.wait_ge(y_free, used + 2)
            for g in range(NG):
                for k in range(TOPK):
                    first = k * B * S + g * GB * S
                    sp.dma_start(pair_in[:, g, k], results[first:first + GB * S].rearrange("(t p) d -> p t d", p=P)
                                 ).then_inc(pair_got[g], 16)
            for g in range(NG):
                by_pool = sum(i <= g for i in POOL_GROUPS)
                if g in POOL_GROUPS:
                    sp.wait_ge(pool_sums, by_pool)
                else:
                    sp.wait_ge(vec_sums, g + 1 - by_pool)
                sp.dma_start(out[g * GB:(g + 1) * GB].rearrange("b (t p) d -> p (b t) d", p=P), pair_in[:, g, 0]
                             ).then_inc(out_done, 16)
            sp.wait_ge(out_done, 16 * NG)

        @block.gpsimd
        def _(pool):
            pool.sem_inc(entry_free, 1)
            pool.sem_inc(y_free, 2)
            def f_norm1(n, p):
                pool.wait_ge(ln1_var, n + 1)
                nc.gpsimd.tensor_tensor(rstd[:, 0], var_eps[:, 0], half_neg[:], ALU.pow).then_inc(ln1_rstd, 1)
                pool.wait_ge(ln1_rstd, n + 1)
                if not isinstance(n, int) or n > 0:
                    pool.wait_ge(xnt_ps, n)
                pool.sem_inc(pool_passed, 1)
                for t in range(NT):
                    o = nc.gpsimd.tensor_scalar(xn[:, t], x_in[:, p, t], moments[:, 0, t, 0:1], rstd[:, 0, t:t + 1],
                                                ALU.subtract, ALU.mult)
                o.then_inc(ln1_done, 1)

            def rsqrt_norm2(n):
                pool.wait_ge(ln2_var, n + 1)
                nc.gpsimd.tensor_tensor(rstd[:, 1], var_eps[:, 1], half_neg[:], ALU.pow).then_inc(ln2_rstd, 1)

            nc.gpsimd.memset(ident[:], 0.0).then_inc(pool_const, 1)
            nc.gpsimd.memset(tri[:], 1.0).then_inc(pool_const, 1)
            nc.gpsimd.memset(half_neg[:], -0.5).then_inc(pool_const, 1)
            nc.gpsimd.iota(iota_e[:], pattern=[[1, E]], base=0, channel_multiplier=0,
                           allow_small_or_imprecise_dtypes=True).then_inc(pool_const, 1)
            nc.gpsimd.iota(region0[:], pattern=[[REGION, E]], base=0, channel_multiplier=0,
                           allow_small_or_imprecise_dtypes=True).then_inc(pool_const, 1)
            nc.gpsimd.iota(ids[:, ROW], pattern=[[S, B], [P, NT], [0, TOPK]], base=0, channel_multiplier=1,
                           allow_small_or_imprecise_dtypes=True).then_inc(pool_const, 1)
            nc.gpsimd.iota(ids[:, PLACE], pattern=[[S, B], [P, NT], [B * S, TOPK]], base=0, channel_multiplier=1,
                           allow_small_or_imprecise_dtypes=True).then_inc(pool_const, 1)
            nc.gpsimd.iota(fill_i[:], pattern=[[1, ENTRIES // P]], base=0, channel_multiplier=ENTRIES // P
                           ).then_inc(pool_const, 1)
            nc.gpsimd.iota(slot_id[:], pattern=[[1, NSLOT]], base=0, channel_multiplier=0,
                           allow_small_or_imprecise_dtypes=True).then_inc(pool_const, 1)
            nc.gpsimd.iota(alibi[:, 0:P], pattern=[[1, P]], base=0, channel_multiplier=-1,
                           allow_small_or_imprecise_dtypes=True).then_inc(pool_const, 1)
            nc.gpsimd.iota(alibi[:, P:P + S], pattern=[[1, S]], base=-P, channel_multiplier=-1,
                           allow_small_or_imprecise_dtypes=True).then_inc(pool_const, 1)
            pool.wait_ge(pool_const, 11)
            nc.gpsimd.affine_select(out=ident[:], in_=ident[:], compare_op=ALU.not_equal, fill=1.0, base=0,
                                    pattern=[[-1, P]], channel_multiplier=1).then_inc(pool_const, 1)
            nc.gpsimd.affine_select(out=tri[:], in_=tri[:], compare_op=ALU.is_gt, fill=0.0, base=0,
                                    pattern=[[1, P]], channel_multiplier=-1).then_inc(pool_const, 1)
            nc.gpsimd.memset(k_stack[:], 0.0).then_inc(pool_const, 1)
            f_norm1(0, 0)
            pool.wait_ge(vec_const, 3)
            nc.gpsimd.affine_select(out=alibi[:, 0:P], in_=alibi[:, 0:P], compare_op=ALU.is_ge, fill=NEG, base=0,
                                    pattern=[[-1, P]], channel_multiplier=1).then_inc(pool_const, 1)
            nc.gpsimd.affine_select(out=alibi[:, P:P + S], in_=alibi[:, P:P + S], compare_op=ALU.is_ge, fill=NEG,
                                    base=P, pattern=[[-1, S]], channel_multiplier=1).then_inc(pool_const, 1)

            def rsqrt_tail(c):
                pool.wait_ge(ln3_var, c + 1)
                nc.gpsimd.tensor_tensor(rstd3[:], var_eps3[:], half_neg[:], ALU.pow).then_inc(ln3_rstd, 1)

            def scatter(c, p, u):
                pool.wait_ge(scattered[1 - p], 64 * u + (FILL if p == 0 else 0))
                pool.sem_inc(entry_free, 1)
                pool.wait_ge(pos_sb, c + 1)
                pool.sem_inc(pool_passed, 1)
                for i in range(NT * TOPK):
                    nc.gpsimd.indirect_dma_start(
                        out=entries, out_offset=bass.IndirectOffsetOnAxis(ap=pos_i[:, p, i:i + 1], axis=0),
                        in_=entry[:, p, i], in_offset=None).then_inc(scattered[p], 16)

            def rest(src, halves, ready, lo, n):
                pool.wait_ge(ready, n + 1)
                nc.gpsimd.tensor_tensor(halves[:, LO], src[:], halves[:, HI], ALU.subtract).then_inc(lo, 1)

            def xn_rest(n):
                rest(xn_t, xn_h, xnt_sb, xnt_lo, n)

            def ctx_rest(n):
                rest(ctx_t, ctx_h, ctxt_sb, ctxt_lo, n)

            def xn2_rest(n):
                rest(xn2_t, xn2_h, xn2t_sb, xn2t_lo, n)

            def out_rest(c):
                rest(o_nt, o_nh, ont_sb, ont_lo, c)

            def split_lo(k, i):
                pool.wait_ge(piece_hi, CHUNKS * k + i + 1)
                nc.gpsimd.tensor_tensor(w_halves[:, i, 1], w_scaled[:, i], w_halves[:, i, 0], ALU.subtract
                                        ).then_inc(piece_split, 1)

            def iteration(b, p, h, c, t, s, f, n):
                if f:
                    xn_rest(b + 2)
                    ctx_rest(b + 2)
                if c:
                    out_rest(b - 1)
                if s:
                    split_lo(b + 1, 0)
                if c:
                    rsqrt_tail(b - 1)
                if n:
                    f_norm1(b + 3, 1 - p)
                if f:
                    rsqrt_norm2(b + 2)
                if s:
                    split_lo(b + 1, 1)
                if f:
                    xn2_rest(b + 2)
                if s:
                    split_lo(b + 1, 2)
                if c:
                    scatter(b - 1, 1 - p, h)

            FILL = 16
            pool.wait_ge(fill_step, 3)
            nc.gpsimd.dma_start(entries.rearrange("(p j) w -> p j w", p=P), fill[:]).then_inc(scattered[1], FILL)
            attention_loop(pool, iteration)

            pool.wait_ge(scattered[1], 64 * (B // 2) + FILL)
            pool.sem_inc(entry_free, 1)

            for p in range(2):
                pool.wait_ge(normed_out[p], 16 * (B // 2 + 1))

            def gather(s, p):
                pool.wait_ge(row_sb, s + 1)
                if not isinstance(s, int) or s >= 2:
                    pool.wait_ge(rt_ps, s - 1)
                pool.sem_inc(pool_passed, 1)
                for t in range(NT):
                    nc.gpsimd.indirect_dma_start(
                        out=rows[:, p, t], out_offset=None, in_=normed,
                        in_offset=bass.IndirectOffsetOnAxis(ap=row_i[:, p, t:t + 1], axis=0)).then_inc(rows_in[p], 16)

            def scatter_results(s, p, u):
                pool.wait_ge(y0_sb, s + 1)
                pool.wait_ge(y1_sb, s + 1)
                pool.sem_inc(pool_passed, 1)
                for t in range(NT):
                    nc.gpsimd.indirect_dma_start(
                        out=results, out_offset=bass.IndirectOffsetOnAxis(ap=place_i[:, p, t:t + 1], axis=0),
                        in_=y_sb[:, p, t], in_offset=None).then_inc(y_out[p], 16)
                pool.wait_ge(y_out[p], 32 * u)
                pool.sem_inc(y_free, 1)

            def slot(s, p, u, ahead):
                if ahead:
                    gather(s + 2, p)
                scatter_results(s, p, u)

            gather(0, 0)
            gather(1, 1)
            with pool.Fori(0, (NSLOT - 3) // 2) as i:
                slot(2 * i, 0, i + 1, True)
                slot(2 * i + 1, 1, i + 1, True)
            slot(NSLOT - 3, 0, (NSLOT - 1) // 2, True)
            slot(NSLOT - 2, 1, (NSLOT - 1) // 2, False)
            slot(NSLOT - 1, 0, (NSLOT + 1) // 2, False)
            combine(nc.gpsimd, pool, POOL_GROUPS, pool_step, pool_sums)

        @block.scalar
        def _(act):
            def copy(to, frm):
                return nc.scalar.activation(to, frm, ACT.Copy)

            def as_chunks(bank_):
                return bank_[:].rearrange("p (c n) -> p c n", c=NC)

            for i in range(6):
                if i == WQK:
                    act.wait_ge(raw_loaded[i], 16)
                else:
                    act.wait_ge(w_tps, i)
                for to, frm in weight_parts(i, HI):
                    o = nc.scalar.activation(to, frm, ACT.Copy, scale=PSCALE)
                o.then_inc(w_hi, 1)
            act.wait_ge(mask_tps, 1)
            nc.scalar.activation(mask_bias[:], tail[:, 0:NT * B].rearrange("p (t b) -> p t b", t=NT), ACT.Copy,
                                 scale=MASK_BIAS)

            def f_xnt(n):
                act.wait_ge(xnt_ps, n + 1)
                nc.scalar.activation(xn_t[:], as_chunks(front[0]), ACT.Copy, scale=XSCALE)
                nc.scalar.activation(xn_h[:, HI], as_chunks(front[0]), ACT.Copy, scale=XSCALE).then_inc(xnt_sb, 1)

            def f_q1(n):
                act.wait_ge(q1_ps, n + 1)
                nc.scalar.activation(q1_t[:], as_chunks(front[0]), ACT.Copy, scale=UNSCALE).then_inc(q1_sb, 1)

            def f_v1(n):
                act.wait_ge(v1_ps, n + 1)
                nc.scalar.activation(v1[:], as_chunks(front[1]), ACT.Copy, scale=UNSCALE).then_inc(v1_sb, 1)

            def f_probs(n):
                act.wait_ge(nmax1_sb, n + 1)
                nc.scalar.activation(p1[:, 0:P], s1[:, 0:P], ACT.Exp, bias=nmax1[:, 0:1], accum_out=sum1[:, 0:1])
                nc.scalar.activation(p1[:, P:P + S], s1[:, P:P + S], ACT.Exp, bias=nmax1[:, 1:2],
                                     accum_out=sum1[:, 1:2]).then_inc(p1_sb, 1)

            def f_probs_t(n):
                act.wait_ge(p1t_ps, n + 1)
                copy(p1_t[:], front[0][:, 0:3 * P].rearrange("p (b q) -> p b q", b=3)).then_inc(p1t_sb, 1)

            def f_xn2t(n):
                act.wait_ge(xn2t_ps, n + 1)
                nc.scalar.activation(xn2_t[:], as_chunks(front[0]), ACT.Copy, scale=XSCALE)
                nc.scalar.activation(xn2_h[:, HI], as_chunks(front[0]), ACT.Copy, scale=XSCALE).then_inc(xn2t_sb, 1)

            def f_ctxt(n):
                act.wait_ge(ctxt_ps, n + 1)
                nc.scalar.activation(ctx_t[:], as_chunks(front[1]), ACT.Copy, scale=XSCALE)
                nc.scalar.activation(ctx_h[:, HI], as_chunks(front[1]), ACT.Copy, scale=XSCALE).then_inc(ctxt_sb, 1)

            def f_q(n):
                act.wait_ge(q_ps, n + 1)
                nc.scalar.activation(q_hi[:], as_chunks(front[1]), ACT.Copy, scale=HSCALE * UNSCALE).then_inc(qhi_sb, 1)

            def f_k(n, q, u):
                act.wait_ge(k_ps, n + 1)
                if not isinstance(n, int) or n > 0:
                    act.wait_ge(stacked[q], 16 * STACK_DMAS * u)
                nc.scalar.activation(k_hi[:], as_chunks(front[1]), ACT.Copy, scale=UNSCALE).then_inc(khi_sb, 1)

            def f_v2(n, p):
                act.wait_ge(v2_ps, n + 1)
                if not isinstance(n, int) or n >= 2:
                    act.wait_ge(pv_ps, 8 * n - 8)
                nc.scalar.activation(v_aug[:, p, :, :, 0:HD], front[0][:].rearrange("p (t h d) -> p t h d", t=NT, h=H),
                                     ACT.Copy, scale=UNSCALE).then_inc(v2_sb, 1)

            def h_max(s):
                act.wait_ge(nmt_ps, s + 1)
                nc.scalar.activation(nmax_t[:], s_ring[0][0:H, 0:S], ACT.Copy, scale=MAX_Q).then_inc(nmt_sb, 1)

            def h_exp(b, g, r):
                act.wait_ge(st_ps, 16 * b + 2 * g + r + 1)
                if r == 0 and (not isinstance(b, int) or b > 0 or g >= 2):
                    act.wait_ge(pv_ps, 8 * b + g - 1)
                act.sem_inc(act_passed, 1)
                nc.scalar.activation(probs_t[:, g % 2, r], t_ring[r][:].rearrange("p (j q) -> p j q", j=2),
                                     ACT.Exp, bias=mask_bias[:, g % 2, bass.ds(b, 1)]).then_inc(exp_sb, 1)

            def h_out(b, p, jp):
                act.wait_ge(pv_ps, 8 * b + 2 * jp + 2)
                copy(o_t[:, p, jp], pv[:, 0:S]).then_inc(o_sb, 1)

            def t_ont(c):
                act.wait_ge(ont_ps, c + 1)
                nc.scalar.activation(o_nt[:], as_chunks(tail), ACT.Copy, scale=XSCALE)
                nc.scalar.activation(o_nh[:, HI], as_chunks(tail), ACT.Copy, scale=XSCALE).then_inc(ont_sb, 1)

            def t_xn3t(c):
                act.wait_ge(xn3t_ps, c + 1)
                copy(xn3_t[:], as_chunks(tail)).then_inc(xn3t_sb, 1)

            def t_gate(c):
                act.wait_ge(logits_sb, c + 1)
                nc.scalar.activation(gexp[:], logits[:], ACT.Exp).then_inc(gexp_sb, 1)

            def split_hi(k, i, p, u):
                act.wait_ge(piece_in[p], 16 * CHUNKS * u)
                if i == 0 and not (isinstance(k, int) and k == 0):
                    act.wait_ge(piece_split, CHUNKS * k)
                    act.wait_ge(piece_out, 16 * CHUNKS * k)
                nc.scalar.activation(w_halves[:, i, 0], w_piece[:, p, i], ACT.Copy, scale=WSCALE)
                nc.scalar.activation(w_scaled[:, i], w_piece[:, p, i], ACT.Copy, scale=WSCALE).then_inc(piece_hi, 1)

            def iteration(b, p, h, c, t, s, f, n):
                if f:
                    f_ctxt(b + 2)
                if t:
                    h_exp(b, 0, 0)
                    h_exp(b, 0, 1)
                if f:
                    f_xnt(b + 2)
                if t:
                    h_exp(b, 1, 0)
                    h_exp(b, 1, 1)
                    h_exp(b, 2, 0)
                    h_exp(b, 2, 1)
                if c:
                    t_ont(b - 1)
                if t:
                    h_out(b, p, 0)
                if f:
                    f_q1(b + 2)
                if t:
                    h_exp(b, 3, 0)
                if s:
                    split_hi(b + 1, 0, 1 - p, h + p + 1)
                if f:
                    f_k(b + 2, 1 - p, h + p + 1)
                if t:
                    h_exp(b, 3, 1)
                if f:
                    f_probs(b + 2)
                if t:
                    h_exp(b, 4, 0)
                if f:
                    f_probs_t(b + 2)
                if t:
                    h_exp(b, 4, 1)
                    h_out(b, p, 1)
                if f:
                    f_v1(b + 2)
                if t:
                    h_exp(b, 5, 0)
                if s:
                    split_hi(b + 1, 1, 1 - p, h + p + 1)
                if t:
                    h_exp(b, 5, 1)
                if c:
                    t_xn3t(b - 1)
                if t:
                    h_exp(b, 6, 0)
                    h_exp(b, 6, 1)
                if s:
                    split_hi(b + 1, 2, 1 - p, h + p + 1)
                if f:
                    f_xn2t(b + 2)
                if t:
                    h_out(b, p, 2)
                if c:
                    t_gate(b - 1)
                if t:
                    h_exp(b, 7, 0)
                    h_exp(b, 7, 1)
                if s:
                    h_max(b + 1)
                if f:
                    f_q(b + 2)
                if t:
                    h_out(b, p, 3)
                if f:
                    f_v2(b + 2, p)

            attention_loop(act, iteration)

            def rows_round(s, p):
                act.wait_ge(rt_ps, s + 1)
                nc.scalar.activation(rows_hi[:, p], as_chunks(tail), ACT.Copy, scale=RSCALE).then_inc(rhi_sb, 1)

            def act_round(s, f):
                act.wait_ge(act_sb, FC * s + f + 1)
                if not isinstance(s, int) or s > 0 or f >= 4:
                    act.wait_ge(act_used, FC * s + f - 3)
                copy(act_hi[:, f % 4], act_t[:, f % 2]).then_inc(ahi_sb, 1)

            def result(s, p):
                act.wait_ge(down_ps, s + 1)
                act.wait_ge(place_sb, s + 1)
                nc.scalar.activation(y_sb[:, p, 0], front[0][:, 0:D], ACT.Copy, scale=slot_gate[:, p, 0:1]
                                     ).then_inc(y0_sb, 1)

            def slot(s, p, ahead):
                first = isinstance(s, int) and s == 0
                for f in range(FC):
                    act.wait_ge(gu_ps, FC * s + f + 1)
                    if not first or f >= 2:
                        act.wait_ge(act_sb, FC * s + f - 1)
                    nc.scalar.activation(silu_g[:, f % 2], gu_ring[f % 4][:, 0:SLOT], ACT.Silu,
                                         scale=1 / (WSCALE * RSCALE)).then_inc(silu_sb, 1)
                    if f >= 1:
                        act_round(s, f - 1)
                    if f == 1 and not first:
                        result(s - 1, 1 - p)
                    if ahead and f == 5:
                        rows_round(s + 1, 1 - p)
                act_round(s, FC - 1)

            rows_round(0, 0)
            slot(0, 0, True)
            with act.Fori(0, (NSLOT - 3) // 2) as i:
                slot(2 * i + 1, 1, True)
                slot(2 * i + 2, 0, True)
            slot(NSLOT - 2, 1, True)
            slot(NSLOT - 1, 0, False)
            result(NSLOT - 1, 0)

        @block.vector
        def _(vec):
            def moments_of(src, k, st, mo, ve, step, var):
                vec.sem_inc(vec_passed, 1)
                for t in range(NT):
                    o = nc.vector.bn_stats(st[:, t], src[:, t])
                o.then_inc(step, 1)
                vec.wait_ge(step, LN_STEPS * k + 1)
                vec.sem_inc(vec_passed, 1)
                for t in range(NT):
                    o = nc.vector.bn_aggr(mo[:, t], st[:, t])
                o.then_inc(step, 1)
                vec.wait_ge(step, LN_STEPS * k + 2)
                nc.vector.tensor_scalar(ve, mo[:, :, 1], EPS_LN, None, ALU.add).then_inc(var, 1)

            def normalise(src, dst, k, mo, rs, rst, done):
                vec.wait_ge(rst, k + 1)
                for t in range(NT):
                    o = nc.vector.tensor_scalar(dst[:, t], src[:, t], mo[:, t, 0:1], rs[:, t:t + 1],
                                                ALU.subtract, ALU.mult)
                o.then_inc(done, 1)

            def residual(m):
                return x_res[:, bass.ds(m * NT, NT)]

            def f_moments1(n, p, u):
                vec.wait_ge(x_loaded[p], 16 * u + 16)
                if not isinstance(n, int) or n > 0:
                    vec.wait_ge(ln1_done, n)
                moments_of(x_in[:, p], n, stats, moments[:, 0], var_eps[:, 0], ln1_step, ln1_var)

            def f_scores(n):
                vec.wait_ge(sc_ps, n + 1)
                nc.vector.scalar_tensor_tensor(s1[:], front[0][:, 0:P + S], SCALE / XSCALE, alibi[:], ALU.mult, ALU.add
                                               ).then_inc(s1_step, 1)
                vec.wait_ge(s1_step, n + 1)
                nc.vector.tensor_reduce(nmax1[:, 0:1], s1[:, 0:P], AX.X, ALU.max, negate=True)
                nc.vector.tensor_reduce(nmax1[:, 1:2], s1[:, P:P + S], AX.X, ALU.max, negate=True
                                        ).then_inc(nmax1_sb, 1)

            def f_sums(n):
                vec.wait_ge(p1_sb, n + 1)
                nc.vector.reciprocal(rsum1[:], sum1[:]).then_inc(rsum1_sb, 1)

            def f_attn(n, p):
                vec.wait_ge(at_ps, n + 1)
                vec.wait_ge(rsum1_sb, n + 1)
                for t in range(NT):
                    o = nc.vector.scalar_tensor_tensor(
                        x_res[:, bass.ds(n * NT + t, 1)].rearrange("p a d -> p (a d)"),
                        front[1][:, t * D:(t + 1) * D], rsum1[:, t:t + 1], x_in[:, p, t], ALU.mult, ALU.add)
                o.then_inc(x1_sb, 1)
                vec.wait_ge(x1_sb, n + 1)
                moments_of(residual(n), n, stats, moments[:, 1], var_eps[:, 1], ln2_step, ln2_var)

            def f_norm2(n):
                normalise(residual(n), xn2, n, moments[:, 1], rstd[:, 1], ln2_rstd, ln2_done)

            def f_q(n):
                vec.wait_ge(qhi_sb, n + 1)
                nc.vector.scalar_tensor_tensor(q_lo[:], front[1][:].rearrange("p (c n) -> p c n", c=NC),
                                               HSCALE * UNSCALE, q_hi[:], ALU.mult, ALU.subtract).then_inc(qlo_sb, 1)

            def f_k(n):
                vec.wait_ge(khi_sb, n + 1)
                nc.vector.scalar_tensor_tensor(k_lo[:], front[1][:].rearrange("p (c n) -> p c n", c=NC), UNSCALE,
                                               k_hi[:], ALU.mult, ALU.subtract).then_inc(klo_sb, 1)

            def h_max(s, n0, n1):
                for n in range(n0, n1):
                    vec.wait_ge(s_ps, 16 * s + n + 1)
                    nc.vector.tensor_reduce(nmax[:, n // HJ, :, n % HJ],
                                            s_ring[n % 2][:].rearrange("p (r k) -> p r k", r=2),
                                            AX.X, ALU.max, negate=True).then_inc(smax, 1)

            def t_norm(c):
                outs = [bank_[:].rearrange("p (j c w) -> p j c w", j=HJ // 2, w=32) for bank_ in (tail, s_ring[1])]
                for qt in range(NT):
                    vec.wait_ge(oq_ps, 2 * c + qt + 1)
                    nc.vector.reciprocal(rden[:, qt], outs[qt][:, :, :, HD]).then_inc(on_step, 1)
                for qt in range(NT):
                    vec.wait_ge(on_step, 2 * c + qt + 1)
                    for r in range(2):
                        m = nc.vector.tensor_tensor(
                            o_n[:, qt, r * P:(r + 1) * P].rearrange("p (j c d) -> p j c d", c=2, d=HD),
                            outs[qt][:, :, 2 * r:2 * r + 2, 0:HD],
                            rden[:, qt, :, 2 * r:2 * r + 2].unsqueeze(3).to_broadcast([P, HJ // 2, 2, HD]), ALU.mult)
                    m.then_inc(on_sb, 1)

            def t_stream(c):
                vec.wait_ge(fc_ps, c + 1)
                nc.vector.scalar_tensor_tensor(residual(c), tail[:].rearrange("p (t d) -> p t d", t=NT), UNSCALE,
                                               residual(c), ALU.mult, ALU.add).then_inc(x2_sb, 1)
                vec.wait_ge(x2_sb, c + 1)
                moments_of(residual(c), c, stats3, moments3[:], var_eps3[:], ln3_step, ln3_var)

            def t_norm3(c, p, u):
                vec.wait_ge(normed_out[p], 16 * u + 16)
                normalise(residual(c), xn3[:, p], c, moments3, rstd3, ln3_rstd, ln3_done)

            def t_logits(c):
                at = GATE_STEPS * c
                vec.wait_ge(gate_ps, c + 1)
                lg = tail[:, 0:NT * E].rearrange("p (t e) -> p t e", t=NT)
                nc.vector.tensor_reduce(lmax[:], lg, AX.X, ALU.max).then_inc(gate_step, 1)
                vec.wait_ge(gate_step, at + 1)
                nc.vector.tensor_tensor(logits[:], lg, lmax[:].unsqueeze(2).to_broadcast([P, NT, E]), ALU.subtract
                                        ).then_inc(logits_sb, 1)

            def t_choose(c, p):
                at = GATE_STEPS * c
                vec.wait_ge(gexp_sb, c + 1)
                nc.vector.tensor_reduce(gsum[:], gexp[:], AX.X, ALU.add).then_inc(gate_step, 1)
                vec.wait_ge(gate_step, at + 2)
                nc.vector.reciprocal(grec[:], gsum[:]).then_inc(gate_step, 1)
                vec.wait_ge(gate_step, at + 3)
                nc.vector.tensor_tensor(gprob[:], gexp[:], grec[:].unsqueeze(2).to_broadcast([P, NT, E]), ALU.mult
                                        ).then_inc(gate_step, 1)
                vec.wait_ge(gate_step, at + 4)
                vec.sem_inc(vec_passed, 1)
                for t in range(NT):
                    nc.vector.max(top_v[:, t], gprob[:, t]).then_inc(gate_step, 1)
                vec.wait_ge(gate_step, at + 6)
                vec.sem_inc(vec_passed, 1)
                for t in range(NT):
                    nc.vector.max_index(top_i[:, t], top_v[:, t], gprob[:, t]).then_inc(gate_step, 1)
                nc.vector.tensor_tensor(gden[:], top_v[:, :, 0], top_v[:, :, 1], ALU.add).then_inc(gate_step, 1)
                vec.wait_ge(gate_step, at + 9)
                nc.vector.tensor_copy(top_f[:], top_i[:, :, 0:TOPK]).then_inc(gate_step, 1)
                nc.vector.tensor_scalar(gden1[:], gden[:], EPS_GATE, None, ALU.max).then_inc(gate_step, 1)
                vec.wait_ge(gate_step, at + 11)
                nc.vector.tensor_tensor(
                    onehot[:].rearrange("p t k e -> p (t k) e"),
                    iota_e[:].unsqueeze(1).to_broadcast([P, NT * TOPK, E]),
                    top_f[:].rearrange("p t k -> p (t k)").unsqueeze(2).to_broadcast([P, NT * TOPK, E]),
                    ALU.is_equal).then_inc(gate_step, 1)
                nc.vector.reciprocal(gdenr[:], gden1[:]).then_inc(gate_step, 1)
                vec.wait_ge(gate_step, at + 13)
                nc.vector.tensor_tensor(chosen[:], onehot[:, :, 0], onehot[:, :, 1], ALU.add).then_inc(chosen_sb, 1)
                vec.wait_ge(entry_free, c + 1)
                nc.vector.scalar_tensor_tensor(
                    entry[:, p, :, GATE].rearrange("p (t k) -> p t k", t=NT), top_v[:, :, 0:TOPK],
                    1 / (WSCALE * ASCALE), gdenr[:].unsqueeze(2).to_broadcast([P, NT, TOPK]), ALU.mult, ALU.mult)
                vec.sem_inc(vec_passed, 1)
                nc.vector.tensor_copy(entry[:, p, :, ROW:PLACE + 1],
                                      ids[:, :, bass.ds(c, 1)].rearrange("p w b t k -> p (b t k) w")
                                      ).then_inc(gate_step, 1)

            def t_place(c, p):
                at = GATE_STEPS * c
                vec.wait_ge(rank_ps, c + 1)
                nc.vector.tensor_tensor(rank[:], tail[:, 0:NT * E].rearrange("p (t e) -> p t e", t=NT),
                                        next_row[:].unsqueeze(1).to_broadcast([P, NT, E]), ALU.add
                                        ).then_inc(gate_step, 1)
                vec.wait_ge(gate_step, at + 15)
                for t in range(NT):
                    o = nc.vector.tensor_tensor(onehot_pos[:, t], onehot[:, t],
                                                rank[:, t].unsqueeze(1).to_broadcast([P, TOPK, E]), ALU.mult)
                o.then_inc(gate_step, 1)
                nc.vector.tensor_tensor(next_row[:], next_row[:], tail[:, NT * E:(NT + 1) * E], ALU.add
                                        ).then_inc(rank_sb, 1)
                vec.wait_ge(gate_step, at + 16)
                nc.vector.tensor_reduce(pos_f[:], onehot_pos[:].rearrange("p t k e -> p (t k) e"), AX.X, ALU.add
                                        ).then_inc(gate_step, 1)
                vec.wait_ge(gate_step, at + 17)
                nc.vector.tensor_copy(pos_i[:, p], pos_f[:]).then_inc(pos_sb, 1)

            def iteration(b, p, h, c, t, s, f, n):
                if c:
                    t_norm(b - 1)
                if s:
                    h_max(b + 1, 0, 6)
                if n:
                    f_moments1(b + 3, 1 - p, h + 1 + p)
                if f:
                    f_scores(b + 2)
                    f_k(b + 2)
                if c:
                    t_stream(b - 1)
                if s:
                    h_max(b + 1, 6, 8)
                if f:
                    f_sums(b + 2)
                if c:
                    t_norm3(b - 1, 1 - p, h + p - 1)
                if s:
                    h_max(b + 1, 8, 10)
                if f:
                    f_attn(b + 2, p)
                if s:
                    h_max(b + 1, 10, 12)
                if f:
                    f_norm2(b + 2)
                if s:
                    h_max(b + 1, 12, 13)
                if c:
                    t_logits(b - 1)
                if s:
                    h_max(b + 1, 13, 16)
                if c:
                    t_choose(b - 1, 1 - p)
                if f:
                    f_q(b + 2)
                if c:
                    t_place(b - 1, 1 - p)

            nc.vector.memset(row_const[:, 0], MASK_Q)
            nc.vector.memset(row_const[:, 1], MAX_K)
            nc.vector.memset(row_const[:, 2], 0.0)
            nc.vector.memset(ones[:], 1.0)
            nc.vector.memset(one_e[:], 1.0)
            nc.vector.memset(v_aug[:], 0.0).then_inc(slot_step, 1)
            vec.wait_ge(slot_step, 1)
            nc.vector.memset(v_aug[:, :, :, :, HD:HD + 1], 1.0)
            f_moments1(0, 0, 0)
            def weight_rest(i):
                vec.wait_ge(w_hi, i + 1)
                for (to, frm), (hi, _) in zip(weight_parts(i, LO), weight_parts(i, HI)):
                    o = nc.vector.scalar_tensor_tensor(to, frm, PSCALE, hi, ALU.mult, ALU.subtract)
                o.then_inc(w_lo, 1)

            nc.vector.memset(q_stack[:], 0.0).then_inc(vec_const, 1)
            weight_rest(WQK)
            weight_rest(WK)
            vec.wait_ge(consts_loaded, 16 * CONST_LOADS)
            nc.vector.tensor_copy(mask_f[:], mask_u8[:])
            nc.vector.tensor_scalar(mask_h[:], mask_u8[:], MASK_K, None, ALU.mult).then_inc(vec_const, 1)
            vec.wait_ge(pool_const, 13)
            nc.vector.tensor_scalar(alibi[:], alibi[:], slope_sb[:, 0:1], None, ALU.mult).then_inc(vec_const, 1)
            for i in (WV1, WQ, WV2, WFC):
                weight_rest(i)
            nc.vector.tensor_copy(next_row[:], region0[:])
            nc.vector.memset(fill[:], 0.0).then_inc(fill_step, 1)
            nc.vector.tensor_scalar(fill_i[:], fill_i[:], SLOT - 1, None, ALU.bitwise_and).then_inc(fill_step, 1)
            vec.wait_ge(fill_step, 2)
            nc.vector.tensor_scalar(fill[:, :, PLACE], fill_i[:], float(TOPK * B * S), None, ALU.add
                                    ).then_inc(fill_step, 1)
            vec.wait_ge(pool_const, 16)
            attention_loop(vec, iteration)

            step = [1]

            def then(ins):
                step[0] += 1
                ins.then_inc(slot_step, 1)
                vec.wait_ge(slot_step, step[0])

            vec.wait_ge(rank_sb, B)
            then(nc.vector.tensor_tensor(count[:], next_row[:], region0[:], ALU.subtract))
            then(nc.vector.tensor_scalar(count[:], count[:], float(SLOT - 1), None, ALU.add))
            then(nc.vector.tensor_copy(count_i[:], count[:]))
            then(nc.vector.tensor_scalar(slots_i[:], count_i[:], SLOT.bit_length() - 1, None,
                                         ALU.arith_shift_right))
            then(nc.vector.tensor_scalar(slots_f[:], slots_i[:], 1.0, None, ALU.max))
            then(nc.vector.tensor_tensor_scan(slot_end[:], one_e[:], slots_f[:], 0.0, ALU.mult, ALU.add))
            then(nc.vector.tensor_scalar(jump[:], slots_f[0:1], -float(SLOT), float(REGION), ALU.mult, ALU.add))
            then(nc.vector.tensor_tensor(past[:], slot_end[0:1].unsqueeze(1).to_broadcast([1, NSLOT, E]),
                                         slot_id[:].unsqueeze(2).to_broadcast([1, NSLOT, E]), ALU.is_le))
            then(nc.vector.tensor_tensor(past_jump[:], past[:], jump[:].unsqueeze(1).to_broadcast([1, NSLOT, E]),
                                         ALU.mult))
            then(nc.vector.tensor_reduce(slot_e[:], past[:], AX.X, ALU.add))
            then(nc.vector.tensor_reduce(slot_r[:], past_jump[:], AX.X, ALU.add))
            then(nc.vector.scalar_tensor_tensor(slot_r1[:], slot_id[:], float(SLOT), slot_r[:], ALU.mult, ALU.add))
            then(nc.vector.tensor_scalar(slot_tab[:, 0], slot_r1[:], float(DUMMY), None, ALU.min))
            nc.vector.tensor_scalar(slot_tab[:, 1], slot_e[:], float(E - 1), None, ALU.min)
            nc.vector.memset(slot_tab[:, 2, 0:2], 1)
            nc.vector.tensor_copy(used_slots[:], slot_end[0:1, E - 1:E])
            nc.vector.tensor_tensor(slot_tab[:, 2, 2:NSLOT], slot_e[:, 2:NSLOT], slot_e[:, 0:NSLOT - 2],
                                    ALU.not_equal).then_inc(table_sb, 1)
            def rows_rest(s, p):
                vec.wait_ge(rhi_sb, s + 1)
                nc.vector.scalar_tensor_tensor(rows_lo[:, p], tail[:].rearrange("p (c n) -> p c n", c=NC), RSCALE,
                                               rows_hi[:, p], ALU.mult, ALU.subtract).then_inc(rlo_sb, 1)

            def act_rest(s, f):
                vec.wait_ge(ahi_sb, FC * s + f + 1)
                nc.vector.tensor_tensor(act_lo[:, f % 4], act_t[:, f % 2], act_hi[:, f % 4], ALU.subtract
                                        ).then_inc(alo_sb, 1)

            def slot_rows(s, p, u):
                vec.wait_ge(entry_in[p], 16 * u)
                vec.sem_inc(vec_passed, 1)
                nc.vector.tensor_copy(row_i[:, p], slot_entry[:, bass.ds(s * NT, NT), ROW]).then_inc(row_sb, 1)

            def slot_places(s, p):
                vec.wait_ge(y_free, s + 1)
                vec.sem_inc(vec_passed, 1)
                nc.vector.tensor_copy(place_i[:, p], slot_entry[:, bass.ds(s * NT, NT), PLACE])
                nc.vector.tensor_copy(slot_gate[:, p], slot_entry[:, bass.ds(s * NT, NT), GATE]).then_inc(place_sb, 1)

            def result(s, p):
                vec.wait_ge(down_ps, s + 1)
                vec.wait_ge(place_sb, s + 1)
                nc.vector.tensor_scalar(y_sb[:, p, 1], front[1][:, 0:D], slot_gate[:, p, 1:2], None, ALU.mult
                                        ).then_inc(y1_sb, 1)

            def slot(s, p, u, ahead):
                first = isinstance(s, int) and s == 0
                if u is not None:
                    slot_rows(s + 2, p, u)
                for f in range(FC):
                    vec.wait_ge(silu_sb, FC * s + f + 1)
                    if not first or f >= 2:
                        vec.wait_ge(alo_sb, FC * s + f - 1)
                    nc.vector.scalar_tensor_tensor(act_t[:, f % 2], gu_ring[f % 4][:, SLOT:2 * SLOT],
                                                   ASCALE / (WSCALE * RSCALE), silu_g[:, f % 2], ALU.mult, ALU.mult
                                                   ).then_inc(act_sb, 1)
                    if f >= 1:
                        act_rest(s, f - 1)
                    if f == 1 and not first:
                        result(s - 1, 1 - p)
                    if ahead and f == 5:
                        rows_rest(s + 1, 1 - p)
                    if f == 6:
                        slot_places(s, p)
                act_rest(s, FC - 1)

            slot_rows(0, 0, 1)
            slot_rows(1, 1, 1)
            rows_rest(0, 0)
            slot(0, 0, 2, True)
            with vec.Fori(0, (NSLOT - 3) // 2) as i:
                slot(2 * i + 1, 1, i + 2, True)
                slot(2 * i + 2, 0, i + 3, True)
            slot(NSLOT - 2, 1, None, True)
            slot(NSLOT - 1, 0, None, False)
            result(NSLOT - 1, 0)

            combine(nc.vector, vec, [g for g in range(NG) if g not in POOL_GROUPS], vec_step, vec_sums)

        @block.tensor
        def _(pe):
            def transpose(to, frm):
                return nc.tensor.transpose(to, frm, ident[0:frm.shape[0], 0:frm.shape[0]])

            def transpose_tiles(bank_, src):
                for t in range(NT):
                    for c in range(NC):
                        o = transpose(bank_[:, c * S + t * P:c * S + (t + 1) * P], src[:, t, c * P:(c + 1) * P])
                return o

            def project_t(bank_, w, src, ob, products, start=False, stop=False):
                for i, (a, r) in enumerate(products):
                    for c in range(NC):
                        o = nc.tensor.matmul(bank_[:, ob * S:(ob + 1) * S], w_split[:, w, a, c, ob * P:(ob + 1) * P],
                                             src[:, r, c], start=(start and i == 0 and c == 0),
                                             stop=(stop and i == len(products) - 1 and c == NC - 1))
                return o

            def project(bank_, src, w, t, products, start=False, stop=False):
                for i, (a, r) in enumerate(products):
                    for c in range(NC):
                        o = nc.tensor.matmul(bank_[:, t * D:(t + 1) * D], src[:, r, c, t * P:(t + 1) * P],
                                             w_split[:, w, a, c], start=(start and i == 0 and c == 0),
                                             stop=(stop and i == len(products) - 1 and c == NC - 1))
                return o

            OF_HI, OF_LO = ((HI, HI), (LO, HI)), ((HI, LO),)

            pe.wait_ge(pool_const, 13)
            for i in range(1, 6):
                pe.wait_ge(raw_loaded[i], 16)
                transpose_tiles(weight_banks[i - 1], w_raw[:, i]).then_inc(w_tps, 1)
            pe.wait_ge(vec_const, 2)
            for t in range(NT):
                o = transpose(tail[:, t * B:(t + 1) * B], mask_f[:, t * P:(t + 1) * P])
            o.then_inc(mask_tps, 1)

            def weights(n, w):
                if isinstance(n, int) and n == 0:
                    pe.wait_ge(w_lo, w + 1)

            def f_xnt(n):
                pe.wait_ge(ln1_done, n + 1)
                if not isinstance(n, int) or n > 0:
                    pe.wait_ge(v2_sb, n)
                transpose_tiles(front[0], xn).then_inc(xnt_ps, 1)

            def f_ctxt(n, p, u):
                pe.wait_ge(ctx_loaded[p], 16 * u + 16)
                if not isinstance(n, int) or n > 0:
                    pe.wait_ge(qlo_sb, n)
                transpose_tiles(front[1], ctx_in[:, p]).then_inc(ctxt_ps, 1)

            def f_q1(n):
                weights(n, WQK)
                pe.wait_ge(xnt_sb, n + 1)
                project_t(front[0], WQK, xn_h, 0, OF_HI, start=True)

            def f_q1_rest(n):
                pe.wait_ge(xnt_lo, n + 1)
                project_t(front[0], WQK, xn_h, 0, OF_LO, stop=True)
                project_t(front[0], WQK, xn_h, 1, OF_HI + OF_LO, start=True, stop=True).then_inc(q1_ps, 1)

            def f_k(n):
                weights(n, WK)
                pe.wait_ge(ctxt_sb, n + 1)
                project_t(front[1], WK, ctx_h, 0, OF_HI, start=True)

            def f_k_rest(n):
                pe.wait_ge(ctxt_lo, n + 1)
                project_t(front[1], WK, ctx_h, 0, OF_LO, stop=True)
                project_t(front[1], WK, ctx_h, 1, OF_HI + OF_LO, start=True, stop=True).then_inc(k_ps, 1)

            def f_scores(n):
                pe.wait_ge(q1_sb, n + 1)
                for q0, k1, to in ((0, P, 0), (P, S, P)):
                    for c in range(NC):
                        o = nc.tensor.matmul(front[0][:, to:to + k1], q1_t[:, c, q0:q0 + P], xn_t[:, c, 0:k1],
                                             start=(c == 0), stop=(c == NC - 1))
                o.then_inc(sc_ps, 1)

            def f_v1(n):
                weights(n, WV1)
                pe.wait_ge(klo_sb, n + 1)
                for t in range(NT):
                    o = project(front[1], xn_h, WV1, t, OF_HI + OF_LO, start=True, stop=True)
                o.then_inc(v1_ps, 1)

            def f_probs_t(n):
                pe.wait_ge(p1_sb, n + 1)
                for blk in range(3):
                    o = transpose(front[0][:, blk * P:(blk + 1) * P], p1[:, blk * P:(blk + 1) * P])
                o.then_inc(p1t_ps, 1)

            def f_attn(n):
                pe.wait_ge(p1t_sb, n + 1)
                pe.wait_ge(v1_sb, n + 1)
                nc.tensor.matmul(front[1][:, 0:D], p1_t[:, 0], v1[:, 0], start=True, stop=True)
                nc.tensor.matmul(front[1][:, D:2 * D], p1_t[:, 1], v1[:, 0], start=True, stop=False)
                nc.tensor.matmul(front[1][:, D:2 * D], p1_t[:, 2], v1[:, 1], start=False, stop=True
                                 ).then_inc(at_ps, 1)

            def f_xn2t(n):
                pe.wait_ge(ln2_done, n + 1)
                transpose_tiles(front[0], xn2).then_inc(xn2t_ps, 1)

            def f_q(n):
                weights(n, WQ)
                pe.wait_ge(xn2t_sb, n + 1)
                project_t(front[1], WQ, xn2_h, 0, OF_HI, start=True)

            def f_q_rest(n):
                pe.wait_ge(xn2t_lo, n + 1)
                project_t(front[1], WQ, xn2_h, 0, OF_LO, stop=True)
                project_t(front[1], WQ, xn2_h, 1, OF_HI + OF_LO, start=True, stop=True).then_inc(q_ps, 1)

            def f_v2(n):
                weights(n, WV2)
                weights(n, WFC)
                for t in range(NT):
                    o = project(front[0], ctx_h, WV2, t, OF_HI + OF_LO, start=True, stop=True)
                o.then_inc(v2_ps, 1)

            def h_scores(s, p, u, n0, n1):
                for n in range(n0, n1):
                    qt, j = n // HJ, n % HJ
                    later = not isinstance(s, int)
                    if n == 0:
                        pe.wait_ge(stacked[p], 16 * STACK_DMAS * (u + 1))
                    if n >= 2:
                        pe.wait_ge(smax, 16 * s + n - 1)
                    elif n == 0 and (later or s > 0):
                        pe.wait_ge(nmt_sb, s)
                    elif n == 1 and (later or s > 1):
                        pe.wait_ge(on_sb, 2 * s - 2)
                    for r in range(2):
                        o = nc.tensor.matmul(s_ring[n % 2][:, r * S:(r + 1) * S],
                                             q_stack[:, p, j, qt * P:(qt + 1) * P], k_stack[:, p, r, j],
                                             start=True, stop=True)
                    o.then_inc(s_ps, 1)

            def h_max(s):
                pe.wait_ge(smax, 16 * s + 16)
                for qt in range(NT):
                    o = transpose(s_ring[0][0:H, qt * P:(qt + 1) * P], nmax[:, qt].rearrange("p r j -> p (r j)"))
                o.then_inc(nmt_ps, 1)

            def h_scores_t(b, p, g, r):
                jp, kt = g // 2, g % 2
                if g >= 1:
                    pe.wait_ge(exp_sb, 16 * b + 2 * g + r - 1)
                for jj in range(2):
                    o = nc.tensor.matmul(t_ring[r][:, jj * S:(jj + 1) * S],
                                         k_stack[:, p, r, 2 * jp + jj, kt * P:(kt + 1) * P],
                                         q_stack[:, p, 2 * jp + jj], start=True, stop=True)
                o.then_inc(st_ps, 1)

            def h_values(b, p, g):
                jp, kt = g // 2, g % 2
                pe.wait_ge(exp_sb, 16 * b + 2 * g + 2)
                if g == 0:
                    pe.wait_ge(v2_sb, b + 1)
                if kt == 0 and (not isinstance(b, int) or b > 0 or jp >= 1):
                    pe.wait_ge(o_sb, 4 * b + jp)
                for r in range(2):
                    for jj in range(2):
                        q = 32 * (2 * r + jj)
                        o = nc.tensor.matmul(pv[q:q + 32, 0:S],
                                             v_aug[:, p, kt, HJ * r + 2 * jp + jj],
                                             probs_t[:, g % 2, r, jj], start=(kt == 0), stop=(kt == 1))
                o.then_inc(pv_ps, 1)

            def t_queries(c, p):
                pe.wait_ge(o_sb, 4 * c + 4)
                if not isinstance(c, int) or c > 0:
                    pe.wait_ge(rank_sb, c)
                for qt, bank_ in enumerate((tail, s_ring[1])):
                    for jp in range(HJ // 2):
                        o = transpose(bank_[:, jp * P:(jp + 1) * P], o_t[:, p, jp, qt * P:(qt + 1) * P])
                    o.then_inc(oq_ps, 1)

            def t_ont(c):
                pe.wait_ge(on_sb, 2 * c + 2)
                transpose_tiles(tail, o_n).then_inc(ont_ps, 1)

            def t_fc(c):
                pe.wait_ge(ont_sb, c + 1)
                project(tail, o_nh, WFC, 0, OF_HI, start=True)

            def t_fc_rest(c):
                pe.wait_ge(ont_lo, c + 1)
                project(tail, o_nh, WFC, 0, OF_LO, stop=True)
                project(tail, o_nh, WFC, 1, OF_HI + OF_LO, start=True, stop=True).then_inc(fc_ps, 1)

            def t_xn3t(c, p):
                pe.wait_ge(ln3_done, c + 1)
                transpose_tiles(tail, xn3[:, p]).then_inc(xn3t_ps, 1)

            def t_gate(c):
                pe.wait_ge(xn3t_sb, c + 1)
                for t in range(NT):
                    for k in range(NC):
                        o = nc.tensor.matmul(tail[:, t * E:(t + 1) * E], xn3_t[:, k, t * P:(t + 1) * P], wg_sb[:, k],
                                             start=(k == 0), stop=(k == NC - 1))
                o.then_inc(gate_ps, 1)

            def t_rank(c):
                pe.wait_ge(chosen_sb, c + 1)
                nc.tensor.matmul(tail[:, 0:NT * E], tri[:], chosen[:].rearrange("p t e -> p (t e)"),
                                 start=True, stop=False)
                nc.tensor.matmul(tail[:, E:2 * E], ones[:], chosen[:, 0], start=False, stop=True)
                nc.tensor.matmul(tail[:, NT * E:(NT + 1) * E], ones[:], chosen[:, 0], start=True, stop=False)
                nc.tensor.matmul(tail[:, NT * E:(NT + 1) * E], ones[:], chosen[:, 1], start=False, stop=True
                                 ).then_inc(rank_ps, 1)

            def iteration(b, p, h, c, t, s, f, n):
                q = 1 - p
                if f:
                    f_ctxt(b + 2, p, h + 1)
                if c:
                    t_queries(b - 1, q)
                if t:
                    pe.wait_ge(max_stacked[p], 16 * h + 16)
                    h_scores_t(b, p, 0, 0)
                    h_scores_t(b, p, 0, 1)
                if f:
                    f_xnt(b + 2)
                    f_k(b + 2)
                if t:
                    h_scores_t(b, p, 1, 0)
                if c:
                    t_ont(b - 1)
                if s:
                    h_scores(b + 1, q, h + p, 0, 2)
                if t:
                    h_values(b, p, 0)
                    h_scores_t(b, p, 1, 1)
                if f:
                    f_q1(b + 2)
                if s:
                    h_scores(b + 1, q, h + p, 2, 3)
                if t:
                    h_scores_t(b, p, 2, 0)
                if s:
                    h_scores(b + 1, q, h + p, 3, 4)
                if t:
                    h_scores_t(b, p, 2, 1)
                    h_values(b, p, 1)
                if f:
                    f_q1_rest(b + 2)
                if t:
                    h_scores_t(b, p, 3, 0)
                if s:
                    h_scores(b + 1, q, h + p, 4, 6)
                if t:
                    h_scores_t(b, p, 3, 1)
                if f:
                    f_k_rest(b + 2)
                    f_scores(b + 2)
                if t:
                    h_values(b, p, 2)
                if c:
                    t_fc(b - 1)
                    t_fc_rest(b - 1)
                if s:
                    h_scores(b + 1, q, h + p, 6, 7)
                if t:
                    h_scores_t(b, p, 4, 0)
                    h_values(b, p, 3)
                    h_scores_t(b, p, 4, 1)
                if s:
                    h_scores(b + 1, q, h + p, 7, 8)
                if f:
                    f_probs_t(b + 2)
                    f_v1(b + 2)
                if t:
                    h_scores_t(b, p, 5, 0)
                if s:
                    h_scores(b + 1, q, h + p, 8, 10)
                if f:
                    f_attn(b + 2)
                if t:
                    h_scores_t(b, p, 5, 1)
                if c:
                    t_xn3t(b - 1, q)
                if s:
                    h_scores(b + 1, q, h + p, 10, 11)
                if t:
                    h_values(b, p, 4)
                    h_scores_t(b, p, 6, 0)
                    h_scores_t(b, p, 6, 1)
                if s:
                    h_scores(b + 1, q, h + p, 11, 12)
                if c:
                    t_gate(b - 1)
                if t:
                    h_scores_t(b, p, 7, 0)
                    h_scores_t(b, p, 7, 1)
                if s:
                    h_scores(b + 1, q, h + p, 12, 14)
                if f:
                    f_xn2t(b + 2)
                if s:
                    h_scores(b + 1, q, h + p, 14, 15)
                if t:
                    h_values(b, p, 5)
                if s:
                    h_scores(b + 1, q, h + p, 15, 16)
                if f:
                    f_q(b + 2)
                if t:
                    h_values(b, p, 6)
                if s:
                    h_max(b + 1)
                if f:
                    f_q_rest(b + 2)
                    f_v2(b + 2)
                if c:
                    t_rank(b - 1)
                if t:
                    h_values(b, p, 7)

            attention_loop(pe, iteration)

            def rows_transposed(s, p, h):
                pe.wait_ge(rows_in[p], 32 * h + 32)
                transpose_tiles(tail, rows[:, p]).then_inc(rt_ps, 1)

            def gate_up(s, p, f):
                if not isinstance(s, int) or s > 0 or f >= 4:
                    pe.wait_ge(act_sb, FC * s + f - 3)
                for half in range(2):
                    products = [(c, w, r) for c in range(NC) for w, r in ((HI, rows_hi), (HI, rows_lo), (LO, rows_hi))]
                    for i, (c, w, r) in enumerate(products):
                        at = c * 2 * F + half * F + f * P
                        o = nc.tensor.matmul(gu_ring[f % 4][:, half * SLOT:(half + 1) * SLOT],
                                             wgu_sb[:, p, w, at:at + P], r[:, p, c],
                                             start=(i == 0), stop=(i == len(products) - 1))
                o.then_inc(gu_ps, 1)

            def down(s, p, f):
                pe.wait_ge(alo_sb, FC * s + f + 1)
                if f == 0 and (not isinstance(s, int) or s > 0):
                    pe.wait_ge(y0_sb, s)
                    pe.wait_ge(y1_sb, s)
                products = ((act_hi, HI), (act_lo, HI), (act_hi, LO))
                for t in range(NT):
                    for i, (a, w) in enumerate(products):
                        o = nc.tensor.matmul(front[t][:, 0:D], a[:, f % 4, t * P:(t + 1) * P],
                                             wd_sb[:, p, w, f * D:(f + 1) * D],
                                             start=(f == 0 and i == 0), stop=(f == FC - 1 and i == len(products) - 1))
                    if t == 0 and f == FC - 1:
                        o.then_inc(act_used, 1)
                o.then_inc(down_ps if f == FC - 1 else act_used, 1)

            def slot(s, p, h, ahead):
                pe.wait_ge(rlo_sb, s + 1)
                pe.wait_ge(w_in[p], 32 * h + 32)
                for f in range(FC):
                    gate_up(s, p, f)
                    if ahead and f == 4:
                        rows_transposed(s + 1, 1 - p, h + p)
                    if f >= 2:
                        down(s, p, f - 2)
                    elif not isinstance(s, int) or s > 0:
                        down(s - 1, 1 - p, FC - 2 + f)

            pe.wait_ge(rank_sb, B)
            rows_transposed(0, 0, 0)
            slot(0, 0, 0, True)
            with pe.Fori(0, (NSLOT - 3) // 2) as i:
                slot(2 * i + 1, 1, i, True)
                slot(2 * i + 2, 0, i + 1, True)
            slot(NSLOT - 2, 1, (NSLOT - 3) // 2, True)
            slot(NSLOT - 1, 0, (NSLOT - 1) // 2, False)
            down(NSLOT - 1, 0, FC - 2)
            down(NSLOT - 1, 0, FC - 1)


def kernel(x, ctx_1024, mask_BxS2_bf0, L0_attn_W_qk, L0_attn_W_v, L0_attn_alibi_slope, L0_xattn_wq, L0_xattn_wk,
           L0_xattn_wv, L0_xattn_wfc, L0_ffn_w_gate, L0_ffn_w_gate_up, L0_ffn_w_down):
    import concourse.bacc as bacc
    from concourse.bass_utils import run_bass_kernel_spmd

    given = {"x": x, "ctx": ctx_1024, "mask": mask_BxS2_bf0,
             "w_qk": L0_attn_W_qk, "w_v": L0_attn_W_v, "slope": L0_attn_alibi_slope, "wq": L0_xattn_wq,
             "wk": L0_xattn_wk, "wv": L0_xattn_wv, "wfc": L0_xattn_wfc, "w_gate": L0_ffn_w_gate,
             "w_gu": L0_ffn_w_gate_up, "w_down": L0_ffn_w_down}
    given = {k: np.ascontiguousarray(v) for k, v in given.items()}
    nc = bacc.Bacc("TRN2", target_bir_lowering=False, num_devices=1)
    aps = {k: nc.dram_tensor(f"in_{k}", v.shape, mybir.dt.from_np(v.dtype), kind="ExternalInput").ap()
           for k, v in given.items()}
    out = nc.dram_tensor("out", (B, S, D), F32, kind="ExternalOutput").ap()
    decoder_layer(nc, **aps, out=out)
    r = run_bass_kernel_spmd(nc, [{f"in_{k}": v for k, v in given.items()}], core_ids=[0])
    return r.results[0]["out"]
```
